# Optimizing a Trainium2 kernel written in Bass

```python
import numpy as np
import jax
import jax.numpy as jnp

def _softmax(x, axis=-1):
    return jax.nn.softmax(x, axis=axis)

def _gelu(x):
    return jax.nn.gelu(x, approximate=True)

def _silu(x):
    return jax.nn.silu(x)

def _sigmoid(x):
    return jax.nn.sigmoid(x)

def _layernorm(x, axis=-1, eps=1e-05):
    m = jnp.mean(x, axis=axis, keepdims=True)
    v = jnp.var(x, axis=axis, keepdims=True)
    return (x - m) / jnp.sqrt(v + eps)

def _scatter_add(tgt, idx, src, axis=0):
    return tgt.at[idx].add(src)

def _segment_sum(src, seg, n):
    return jax.ops.segment_sum(src, seg, n)
kernel_name = 'mk_gnn_preln_d4_gnn_r8_937a58'

def setup_inputs(seed: int=0):
    np.random.seed(seed)
    _w = jnp.asarray

    def _rec_inputs():
        import jax
        import jax.numpy as jnp
        _gk = jax.random.key(seed)
        x = -8.776e-05 + 1 * jax.random.normal(jax.random.fold_in(_gk, 1), (6250, 128), jnp.float32)
        src = jax.random.randint(jax.random.fold_in(_gk, 2), (100000,), 0, 6250, jnp.int32)
        dst = jnp.minimum((6250 * jax.random.uniform(jax.random.fold_in(_gk, 3), (100000,)) ** 2.0).astype(jnp.int32), 49999)
        _o = jnp.argsort(dst, stable=True)
        src = src[_o]
        dst = dst[_o]
        edge_attr_3 = 0.000730401 + 0.999882 * jax.random.normal(jax.random.fold_in(_gk, 12), (100000, 3), jnp.float32)
        edge_attr_50 = 0.000202107 + 1.00009 * jax.random.normal(jax.random.fold_in(_gk, 13), (100000, 50), jnp.float32)
        edge_attr_64 = -9.77346e-05 + 0.999888 * jax.random.normal(jax.random.fold_in(_gk, 14), (100000, 64), jnp.float32)
        edge_weight = jax.random.uniform(jax.random.fold_in(_gk, 16), (100000,), jnp.float32, 0.0, 0.999998)
        return (x, src, dst, edge_attr_3, edge_attr_50, edge_attr_64, edge_weight)
    x, src, dst, edge_attr_3, edge_attr_50, edge_attr_64, edge_weight = _rec_inputs()

    def _L0_gnn_setup():
        import jax, jax.numpy as jnp
        import numpy as np
        N = 5000
        E = 80000
        IN = 128
        H = 4
        C = 32
        key = jax.random.key(seed)
        ks = jax.random.split(key, 5)
        x = jax.random.normal(ks[0], (N, IN), dtype=jnp.float32)
        edge_index = jax.random.randint(ks[1], (2, E), 0, N, dtype=jnp.int64)
        W_lin = jax.random.normal(ks[2], (IN, H * C), dtype=jnp.float32) * 0.05
        b_lin = jnp.zeros((H * C,), dtype=jnp.float32)
        W_att = jax.random.normal(ks[3], (2 * H * C, H), dtype=jnp.float32) * 0.05
        b_att = jnp.zeros((H,), dtype=jnp.float32)
        return {'x': x, 'edge_index': edge_index, 'W_lin': W_lin, 'b_lin': b_lin, 'W_att': W_att, 'b_att': b_att}
    _L0_gnn_all = _L0_gnn_setup()
    _L0_gnn_in = {k: v for k, v in _L0_gnn_all.items() if k in ('W_lin', 'b_lin', 'W_att', 'b_att')}
    del _L0_gnn_all

    def _L1_gnn_setup():
        import jax, jax.numpy as jnp
        import numpy as np
        N = 6250
        E = 100000
        F = 128
        K = 64
        NRI = 3
        NRA = 2

        def ssp(x):
            return jax.nn.softplus(x) - jnp.asarray(np.log(2.0), x.dtype)

        def _residual(m, W1, b1, W2, b2):
            y = ssp(m)
            h = ssp(y @ W1.T + b1)
            return m + h @ W2.T + b2
        key = jax.random.key(seed)
        ks = jax.random.split(key, 24)
        s = 0.05
        inp = {'features': jax.random.normal(ks[0], (N, F), jnp.float32), 'descriptors': jax.random.normal(ks[1], (E, K), jnp.float32), 'idx_i': jnp.sort(jax.random.randint(ks[2], (E,), 0, N)), 'idx_j': jax.random.randint(ks[3], (E,), 0, N), 'Wdesc': jax.random.normal(ks[4], (F, K), jnp.float32) * s, 'Wi': jax.random.normal(ks[5], (F, F), jnp.float32) * s, 'bi': jnp.zeros((F,), jnp.float32), 'Wj': jax.random.normal(ks[6], (F, F), jnp.float32) * s, 'bj': jnp.zeros((F,), jnp.float32), 'Wri1': jax.random.normal(ks[7], (NRI, F, F), jnp.float32) * s, 'bri1': jnp.zeros((NRI, F), jnp.float32), 'Wri2': jax.random.normal(ks[8], (NRI, F, F), jnp.float32) * s, 'bri2': jnp.zeros((NRI, F), jnp.float32), 'Wd': jax.random.normal(ks[9], (F, F), jnp.float32) * s, 'bd': jnp.zeros((F,), jnp.float32), 'u': jnp.ones((F,), jnp.float32), 'Wra1': jax.random.normal(ks[10], (NRA, F, F), jnp.float32) * s, 'bra1': jnp.zeros((NRA, F), jnp.float32), 'Wra2': jax.random.normal(ks[11], (NRA, F, F), jnp.float32) * s, 'bra2': jnp.zeros((NRA, F), jnp.float32)}
        return inp
    _L1_gnn_all = _L1_gnn_setup()
    _L1_gnn_in = {k: v for k, v in _L1_gnn_all.items() if k in ('Wdesc', 'Wi', 'bi', 'Wj', 'bj', 'Wri1', 'bri1', 'Wri2', 'bri2', 'Wd', 'bd', 'u', 'Wra1', 'bra1', 'Wra2', 'bra2')}
    del _L1_gnn_all

    def _L2_gnn_setup():
        import jax, jax.numpy as jnp
        import numpy as np
        N, E, H = (6250, 100000, 128)
        LN_EPS = 1e-05

        def layer_norm(x, gamma, beta):
            mu = jnp.mean(x, axis=-1, keepdims=True)
            var = jnp.mean((x - mu) ** 2, axis=-1, keepdims=True)
            return (x - mu) * jax.lax.rsqrt(var + LN_EPS) * gamma + beta
        key = jax.random.key(seed)
        ks = jax.random.split(key, 8)
        sc = 1.0 / np.sqrt(2 * H)
        return {'x': jax.random.normal(ks[0], (N, H), dtype=jnp.float32), 'edge_index': jax.random.randint(ks[1], (2, E), 0, N, dtype=jnp.int64), 'edge_weights': jax.random.uniform(ks[2], (E,), dtype=jnp.float32), 'msg_w': jax.random.normal(ks[3], (2 * H, H), dtype=jnp.float32) * sc, 'msg_b': jnp.zeros((H,), jnp.float32), 'msg_g': jnp.ones((H,), jnp.float32), 'msg_beta': jnp.zeros((H,), jnp.float32), 'upd_w': jax.random.normal(ks[4], (2 * H, H), dtype=jnp.float32) * sc, 'upd_b': jnp.zeros((H,), jnp.float32), 'upd_g': jnp.ones((H,), jnp.float32), 'upd_beta': jnp.zeros((H,), jnp.float32), 'gate_w': jax.random.normal(ks[5], (H, 1), dtype=jnp.float32) / np.sqrt(H), 'gate_b': jnp.zeros((1,), jnp.float32)}
    _L2_gnn_all = _L2_gnn_setup()
    _L2_gnn_in = {k: v for k, v in _L2_gnn_all.items() if k in ('msg_w', 'msg_b', 'msg_g', 'msg_beta', 'upd_w', 'upd_b', 'upd_g', 'upd_beta', 'gate_w', 'gate_b')}
    del _L2_gnn_all

    def _L3_gnn_setup():
        import jax, jax.numpy as jnp
        import numpy as np
        LOG2 = float(np.log(2.0))
        CUTOFF = 10.0
        N, E, H, F, G = (6250, 78125, 128, 128, 50)

        def ssp(x):
            return jax.nn.softplus(x) - LOG2
        key = jax.random.key(seed)
        ks = jax.random.split(key, 12)
        s = 0.05
        return {'x': jax.random.normal(ks[0], (N, H), jnp.float32), 'edge_index': jax.random.randint(ks[1], (2, E), 0, N, dtype=jnp.int32), 'edge_weight': jax.random.normal(ks[2], (E, 3), jnp.float32), 'edge_attr': jax.random.normal(ks[3], (E, G), jnp.float32), 'mlp_w1': jax.random.normal(ks[4], (F, G), jnp.float32) * s, 'mlp_b1': jax.random.normal(ks[5], (F,), jnp.float32) * s, 'mlp_w2': jax.random.normal(ks[6], (F, F), jnp.float32) * s, 'mlp_b2': jax.random.normal(ks[7], (F,), jnp.float32) * s, 'lin1_w': jax.random.normal(ks[8], (F, H), jnp.float32) * s, 'lin2_w': jax.random.normal(ks[9], (H, F), jnp.float32) * s, 'lin2_b': jax.random.normal(ks[10], (H,), jnp.float32) * s}
    _L3_gnn_all = _L3_gnn_setup()
    _L3_gnn_in = {k: v for k, v in _L3_gnn_all.items() if k in ('mlp_w1', 'mlp_b1', 'mlp_w2', 'mlp_b2', 'lin1_w', 'lin2_w', 'lin2_b')}
    del _L3_gnn_all
    return {'x': x, 'src': src, 'dst': dst, 'edge_attr_3': edge_attr_3, 'edge_attr_50': edge_attr_50, 'edge_attr_64': edge_attr_64, 'edge_weight': edge_weight, 'L0_gnn_W_lin': _L0_gnn_in['W_lin'], 'L0_gnn_b_lin': _L0_gnn_in['b_lin'], 'L0_gnn_W_att': _L0_gnn_in['W_att'], 'L0_gnn_b_att': _L0_gnn_in['b_att'], 'L1_gnn_Wdesc': _L1_gnn_in['Wdesc'], 'L1_gnn_Wi': _L1_gnn_in['Wi'], 'L1_gnn_bi': _L1_gnn_in['bi'], 'L1_gnn_Wj': _L1_gnn_in['Wj'], 'L1_gnn_bj': _L1_gnn_in['bj'], 'L1_gnn_Wri1': _L1_gnn_in['Wri1'], 'L1_gnn_bri1': _L1_gnn_in['bri1'], 'L1_gnn_Wri2': _L1_gnn_in['Wri2'], 'L1_gnn_bri2': _L1_gnn_in['bri2'], 'L1_gnn_Wd': _L1_gnn_in['Wd'], 'L1_gnn_bd': _L1_gnn_in['bd'], 'L1_gnn_u': _L1_gnn_in['u'], 'L1_gnn_Wra1': _L1_gnn_in['Wra1'], 'L1_gnn_bra1': _L1_gnn_in['bra1'], 'L1_gnn_Wra2': _L1_gnn_in['Wra2'], 'L1_gnn_bra2': _L1_gnn_in['bra2'], 'L2_gnn_msg_w': _L2_gnn_in['msg_w'], 'L2_gnn_msg_b': _L2_gnn_in['msg_b'], 'L2_gnn_msg_g': _L2_gnn_in['msg_g'], 'L2_gnn_msg_beta': _L2_gnn_in['msg_beta'], 'L2_gnn_upd_w': _L2_gnn_in['upd_w'], 'L2_gnn_upd_b': _L2_gnn_in['upd_b'], 'L2_gnn_upd_g': _L2_gnn_in['upd_g'], 'L2_gnn_upd_beta': _L2_gnn_in['upd_beta'], 'L2_gnn_gate_w': _L2_gnn_in['gate_w'], 'L2_gnn_gate_b': _L2_gnn_in['gate_b'], 'L3_gnn_mlp_w1': _L3_gnn_in['mlp_w1'], 'L3_gnn_mlp_b1': _L3_gnn_in['mlp_b1'], 'L3_gnn_mlp_w2': _L3_gnn_in['mlp_w2'], 'L3_gnn_mlp_b2': _L3_gnn_in['mlp_b2'], 'L3_gnn_lin1_w': _L3_gnn_in['lin1_w'], 'L3_gnn_lin2_w': _L3_gnn_in['lin2_w'], 'L3_gnn_lin2_b': _L3_gnn_in['lin2_b']}

def reference(x, src, dst, edge_attr_3, edge_attr_50, edge_attr_64, edge_weight, L0_gnn_W_lin, L0_gnn_b_lin, L0_gnn_W_att, L0_gnn_b_att, L1_gnn_Wdesc, L1_gnn_Wi, L1_gnn_bi, L1_gnn_Wj, L1_gnn_bj, L1_gnn_Wri1, L1_gnn_bri1, L1_gnn_Wri2, L1_gnn_bri2, L1_gnn_Wd, L1_gnn_bd, L1_gnn_u, L1_gnn_Wra1, L1_gnn_bra1, L1_gnn_Wra2, L1_gnn_bra2, L2_gnn_msg_w, L2_gnn_msg_b, L2_gnn_msg_g, L2_gnn_msg_beta, L2_gnn_upd_w, L2_gnn_upd_b, L2_gnn_upd_g, L2_gnn_upd_beta, L2_gnn_gate_w, L2_gnn_gate_b, L3_gnn_mlp_w1, L3_gnn_mlp_b1, L3_gnn_mlp_w2, L3_gnn_mlp_b2, L3_gnn_lin1_w, L3_gnn_lin2_w, L3_gnn_lin2_b):
    import jax
    import jax.numpy as jnp

    def _L0_gnn_ref(x, edge_index, W_lin, b_lin, W_att, b_att):
        import jax, jax.numpy as jnp
        import numpy as np
        N = 5000
        E = 80000
        IN = 128
        H = 4
        C = 32
        n = x.shape[0]
        row, col = (edge_index[0], edge_index[1])
        xl = x @ W_lin + b_lin
        hc = xl.shape[1]
        s_i = xl @ W_att[:hc]
        s_j = xl @ W_att[hc:]
        alpha = s_i[row] + s_j[col] + b_att
        alpha = jnp.where(alpha >= 0, alpha, 0.2 * alpha)
        amax = jax.ops.segment_max(alpha, row, num_segments=n)
        alpha = jnp.exp(alpha - amax[row])
        asum = jax.ops.segment_sum(alpha, row, num_segments=n)
        alpha = alpha / (asum[row] + 1e-16)
        xh = xl.reshape(n, H, C)
        msg = alpha[:, :, None] * xh[row]
        out = jax.ops.segment_sum(msg, col, num_segments=n)
        deg = jax.ops.segment_sum(jnp.ones((row.shape[0],), xl.dtype), col, num_segments=n)
        out = jnp.where(deg[:, None, None] > 0, out, xh)
        return out.reshape(n, H * C)

    def _L1_gnn_ref(features, descriptors, Wdesc, Wi, bi, Wj, bj, Wri1, bri1, Wri2, bri2, Wd, bd, u, Wra1, bra1, Wra2, bra2, idx_i, idx_j):
        import jax, jax.numpy as jnp
        import numpy as np
        N = 6250
        E = 100000
        F = 128
        K = 64
        NRI = 3
        NRA = 2

        def ssp(x):
            return jax.nn.softplus(x) - jnp.asarray(np.log(2.0), x.dtype)

        def _residual(m, W1, b1, W2, b2):
            y = ssp(m)
            h = ssp(y @ W1.T + b1)
            return m + h @ W2.T + b2
        x = features
        xa = ssp(x)
        g = descriptors @ Wdesc.T
        xi = ssp(xa @ Wi.T + bi)
        xj_all = ssp(xa @ Wj.T + bj)
        pxj = g * xj_all[idx_j]
        xj = jax.ops.segment_sum(pxj, idx_i, num_segments=x.shape[0])
        message = xi + xj
        for k in range(NRI):
            message = _residual(message, Wri1[k], bri1[k], Wri2[k], bri2[k])
        message = ssp(message)
        x = u * x + message @ Wd.T + bd
        for k in range(NRA):
            x = _residual(x, Wra1[k], bra1[k], Wra2[k], bra2[k])
        return x

    def _L2_gnn_ref(x, edge_index, edge_weights, msg_w, msg_b, msg_g, msg_beta, upd_w, upd_b, upd_g, upd_beta, gate_w, gate_b):
        import jax, jax.numpy as jnp
        import numpy as np
        N, E, H = (6250, 100000, 128)
        LN_EPS = 1e-05

        def layer_norm(x, gamma, beta):
            mu = jnp.mean(x, axis=-1, keepdims=True)
            var = jnp.mean((x - mu) ** 2, axis=-1, keepdims=True)
            return (x - mu) * jax.lax.rsqrt(var + LN_EPS) * gamma + beta
        num_nodes = x.shape[0]
        src, dst = (edge_index[0], edge_index[1])
        em = jnp.concatenate([x[src], x[dst]], axis=-1)
        em = jax.nn.relu(layer_norm(em @ msg_w + msg_b, msg_g, msg_beta))
        em = em * edge_weights[:, None]
        msgs = jax.ops.segment_sum(em, dst, num_segments=num_nodes)
        counts = jax.ops.segment_sum(jnp.ones((src.shape[0], 1), x.dtype), dst, num_segments=num_nodes)
        valid = (counts > 0).astype(x.dtype)
        messages = msgs / (counts + 1e-08) * valid
        gate = jax.nn.sigmoid(x @ gate_w + gate_b)
        combined = jnp.concatenate([x, messages], axis=-1)
        h_new = jax.nn.relu(layer_norm(combined @ upd_w + upd_b, upd_g, upd_beta))
        return gate * h_new + (1.0 - gate) * x

    def _L3_gnn_ref(x, edge_index, edge_weight, edge_attr, mlp_w1, mlp_b1, mlp_w2, mlp_b2, lin1_w, lin2_w, lin2_b):
        import jax, jax.numpy as jnp
        import numpy as np
        LOG2 = float(np.log(2.0))
        CUTOFF = 10.0
        N, E, H, F, G = (6250, 78125, 128, 128, 50)

        def ssp(x):
            return jax.nn.softplus(x) - LOG2
        d = jnp.linalg.norm(edge_weight, axis=1)
        C = 0.5 * (jnp.cos(d * jnp.pi / CUTOFF) + 1.0) * (d <= CUTOFF)
        W = ssp(edge_attr @ mlp_w1.T + mlp_b1) @ mlp_w2.T + mlp_b2
        W = W * C[:, None]
        i, j = (edge_index[0], edge_index[1])
        messages = W * (x[j] @ lin1_w.T)
        agg = jax.ops.segment_sum(messages, i, num_segments=x.shape[0])
        h = ssp(agg @ lin2_w.T + lin2_b)
        return x + h
    edge_index = jnp.stack([src, dst])
    h = jnp.maximum(_layernorm(x, axis=-1), 0.0)
    x = x + _L0_gnn_ref(h, edge_index, L0_gnn_W_lin, L0_gnn_b_lin, L0_gnn_W_att, L0_gnn_b_att)
    h = jnp.maximum(_layernorm(x, axis=-1), 0.0)
    x = x + _L1_gnn_ref(h, edge_attr_64, L1_gnn_Wdesc, L1_gnn_Wi, L1_gnn_bi, L1_gnn_Wj, L1_gnn_bj, L1_gnn_Wri1, L1_gnn_bri1, L1_gnn_Wri2, L1_gnn_bri2, L1_gnn_Wd, L1_gnn_bd, L1_gnn_u, L1_gnn_Wra1, L1_gnn_bra1, L1_gnn_Wra2, L1_gnn_bra2, src, dst)
    h = jnp.maximum(_layernorm(x, axis=-1), 0.0)
    x = x + _L2_gnn_ref(h, edge_index, edge_weight, L2_gnn_msg_w, L2_gnn_msg_b, L2_gnn_msg_g, L2_gnn_msg_beta, L2_gnn_upd_w, L2_gnn_upd_b, L2_gnn_upd_g, L2_gnn_upd_beta, L2_gnn_gate_w, L2_gnn_gate_b)
    h = jnp.maximum(_layernorm(x, axis=-1), 0.0)
    x = x + _L3_gnn_ref(h, edge_index, edge_attr_3, edge_attr_50, L3_gnn_mlp_w1, L3_gnn_mlp_b1, L3_gnn_mlp_w2, L3_gnn_mlp_b2, L3_gnn_lin1_w, L3_gnn_lin2_w, L3_gnn_lin2_b)
    return x

_drawn_inputs = setup_inputs


def setup_inputs(seed=0):
    import zlib

    import numpy as np

    out = dict(_drawn_inputs(seed))
    spreads = {'L0_gnn_b_lin': (0.0, 0.1),
     'L0_gnn_b_att': (0.0, 2.0),
     'L1_gnn_bi': (0.0, 0.8),
     'L1_gnn_bj': (0.0, 0.666),
     'L1_gnn_bri1': (0.0, 0.8),
     'L1_gnn_bri2': (0.0, 0.313),
     'L1_gnn_bd': (0.0, 2.0),
     'L1_gnn_u': (1.0, 0.6),
     'L1_gnn_bra1': (0.0, 2.0),
     'L1_gnn_bra2': (0.0, 2.0),
     'L2_gnn_msg_b': (0.0, 2.0),
     'L2_gnn_msg_g': (1.0, 0.6),
     'L2_gnn_msg_beta': (0.0, 2.0),
     'L2_gnn_upd_b': (0.0, 2.0),
     'L2_gnn_upd_g': (1.0, 0.6),
     'L2_gnn_upd_beta': (0.0, 2.0)}
    factors = {'edge_attr_3': 64.0,
     'edge_attr_50': 27.776,
     'edge_weight': 200.0,
     'L1_gnn_Wi': 2.783,
     'L1_gnn_Wri1': 8.0,
     'L1_gnn_Wri2': 6.069,
     'L3_gnn_mlp_w1': 27.992,
     'L3_gnn_mlp_b1': 200.0,
     'L3_gnn_mlp_w2': 26.608,
     'L3_gnn_lin2_b': 200.0,
     'L2_gnn_msg_w': 64.0,
     'L2_gnn_upd_w': 64.0,
     'L2_gnn_gate_w': 45.716,
     'L3_gnn_mlp_b2': 64.0,
     'L3_gnn_lin1_w': 7.21,
     'L3_gnn_lin2_w': 8.0}
    for name, (base, spread) in spreads.items():
        noise = np.random.default_rng([zlib.crc32(name.encode()), seed]).standard_normal(out[name].shape)
        drawn = base * np.exp(spread * noise) if base else spread * noise
        out[name] = jnp.asarray(drawn.astype(out[name].dtype))
    for name, factor in factors.items():
        out[name] = (out[name] * factor).astype(out[name].dtype)
    return out
```

```python
from contextlib import ExitStack

import concourse.bass as bass
from concourse import mybir

ALU = mybir.AluOpType
ACT = mybir.ActivationFunctionType
F32 = mybir.dt.float32
BF16 = mybir.dt.bfloat16
I32 = mybir.dt.int32
AX = mybir.AxisListType.X

P = 128
N = 6250
E = 100000
NB = -(-N // P)
NP = NB * P
GT = 8
T = 784
EP = T * P
PAD_KEY = NP - 1
SLOTS = T + NB - 1
G = 4
STEPS = SLOTS // G
H = 128
HEADS = 4
A50, A64, A3 = 50, 64, 3
C64 = A50
CM = A50 + A64
NREC = CM + A3 + 1
W_DST, W_SRC, W_POS = NREC, NREC + 1, NREC + 2
META = 8
BIG = 131072.0
NEG = -1.0e30
EPS = 1e-5
SEC = 448
NSEC = NP // SEC
T1W = H + 3 * HEADS
MATS = ["W_lin", "Wi", "Wj", "Wri1_0", "Wri1_1", "Wri1_2", "Wri2_0", "Wri2_1", "Wri2_2", "Wd", "Wra1_0", "Wra1_1",
        "Wra2_0", "Wra2_1", "msg_top", "msg_bottom", "upd_top", "upd_bottom", "lin1", "lin2", "mlp_w2", "mlp_w1",
        "Wdesc", "W_att"]
VECS = ["bi", "bri1_0", "bri1_1", "bri1_2", "bri2_0", "bri2_1", "bri2_2", "bd", "u", "bra1_0", "bra1_1", "bra2_0",
        "bra2_1", "mlp_b1", "lin2_b"]
ROWS = ["b_lin", "bj", "msg_b", "msg_g", "msg_beta", "upd_b", "upd_g", "upd_beta", "gate_w", "mlp_b2", "b_att", "gate_b"]
BANK = 512
assert SLOTS % (2 * G) == 0 and T % GT == 0 and NP % SEC == 0 and EP < BIG


class Step:

    def __init__(self, i, half, par):
        self.i, self.half, self.par = i, half, par


class Chain:

    def __init__(self, eng, sem):
        self.eng, self.sem = eng, sem
        self.done, self.loop, self.per = 0, None, 0

    def __call__(self, ins):
        ins.then_inc(self.sem, 1)
        self.done += 1
        return ins

    def wait(self, back=0):
        n = self.done - back
        if n <= 0:
            return
        self.eng.wait_ge(self.sem, n if self.loop is None else self.loop * self.per + n)


def run_steps(eng, chain, stages, n):
    lag = max(s for _, s in stages)
    first = max(lag + 2, 2)
    if (n - first) % 2:
        first += 1

    def one(r):
        for f, s in stages:
            if 0 <= r - s < n:
                f(Step(r - s, (r - s) // 2, (r - s) % 2))

    if n < first + 4:
        for r in range(n + lag):
            one(r)
        return
    for r in range(first):
        before = chain.done
        one(r)
    chain.per = 2 * (chain.done - before)
    pairs = (n - first) // 2
    with eng.Fori(0, pairs) as k:
        chain.loop = k
        start = chain.done
        for u in range(2):
            for f, s in stages:
                c = first + u - s
                f(Step(2 * k + c, k + c // 2, c % 2))
        assert chain.done - start == chain.per
    chain.loop = None
    chain.done = start + chain.per * pairs
    for r in range(n, n + lag):
        one(r)


def wait_step(eng, sem, st, back=0):
    v = st.i + (1 - back)
    if isinstance(v, int) and v <= 0:
        return
    eng.wait_ge(sem, v)


def wait_tiles(eng, sem, st, back=0):
    v = st.i * GT + (GT * (1 - back) + 1)
    if isinstance(v, int) and v <= 1:
        return
    eng.wait_ge(sem, v)


def take_waits(eng, tally):
    eng.sem_inc(tally, 1)


def wait_load(eng, sems, st, n):
    eng.wait_ge(sems[st.par], st.half * (16 * n) + 16 * n)


def wait_free(eng, sems, st, n):
    if isinstance(st.half, int) and st.half == 0:
        return
    eng.wait_ge(sems[st.par], st.half * (16 * n))


class Buffers:
    pass


def dram(kn, name, shape, dt=F32):
    return kn.nc.dram_tensor(name, shape, dt, kind="Internal").ap()

def phase(kn, name, build, psums=(), sbufs=(), sems=(), pairs=()):
    nc = kn.nc
    with ExitStack() as ctx:
        res, used = {}, []
        for n, shape, dt in psums:
            res[n] = ctx.enter_context(nc.psum_tensor(f"{name}_{n}", shape, dt))
        for n, shape, dt in sbufs:
            res[n] = ctx.enter_context(nc.sbuf_tensor(f"{name}_{n}", shape, dt))
        for n in sems:
            res[n] = nc.alloc_semaphore(f"{name}_{n}")
            used.append(res[n])
        for n in pairs:
            res[n] = [nc.alloc_semaphore(f"{name}_{n}{j}") for j in range(2)]
            used += res[n]
        bodies = build(res)
        own = {n: nc.alloc_semaphore(f"{name}_{n}_own") for n in bodies}
        used += list(own.values())
        with nc.Block() as block:
            for eng_name, body in bodies.items():
                def run(eng, body=body, sem=own[eng_name]):
                    body(eng, Chain(eng, sem))

                {"sync": block.sync, "tensor": block.tensor, "vector": block.vector,
                 "scalar": block.scalar, "gpsimd": block.gpsimd}[eng_name](run)
        nc.clear_and_free_semaphores(used)
        nc.all_engine_barrier()

def setup(kn, ctx):
    nc = kn.nc

    def sb(name, shape, dt=F32):
        return ctx.enter_context(nc.sbuf_tensor(name, shape, dt))

    kn.X = sb("x_nodes", [P, NB, H])
    kn.ident = sb("ident", [P, P])
    kn.identb = sb("identb", [P, P], BF16)
    kn.ones = sb("ones", [P, P])
    kn.before = sb("before", [P, P])
    kn.beforeb = sb("beforeb", [P, P], BF16)
    kn.iota = sb("iota", [P, P])
    kn.iotab = sb("iotab", [P, P], BF16)
    kn.pcol = sb("pcol", [P, 1])
    kn.zero1 = sb("zero1", [P, 1])
    kn.half1 = sb("half1", [P, 1])
    kn.eps1 = sb("eps1", [P, 1])
    kn.hp1 = sb("half_pi", [P, 1])
    kn.start = sb("start", [P, 2, NB])
    kn.count = sb("count", [P, 2, NB])
    kn.slot_reg = sb("slot_reg", [P, SLOTS], I32)
    kn.local = sb("local", [P, 2, SLOTS])

def node_buffers(kn, ctx):
    def sb(name, shape, dt=F32):
        return ctx.enter_context(kn.nc.sbuf_tensor(name, shape, dt))

    kn.place = sb("k_place", [P, SLOTS], I32)
    kn.src_of = sb("k_src_of", [P, SLOTS], I32)
    kn.wt = sb("k_wt", [P, SLOTS])
    kn.cut = sb("k_cut", [P, SLOTS])
    kn.W = sb("k_weights", [P, len(MATS), H])
    kn.V = sb("k_vectors", [P, len(VECS)])
    kn.R = sb("k_rows", [P, len(ROWS), H])
    kn.Hn = sb("h_nodes", [P, NB, H])
    kn.AC = sb("acc", [P, NB, H])
    kn.TB = sb("table", [P, NB, H])
    kn.MT = sb("spare", [P, NB, H])

def flat(kn, t):
    return t[:, :, :].rearrange("p b h -> p (b h)")

def constants(kn):
    ins = kn.ins

    def build(r):
        def gpsimd(e, ch):
            ch(e.iota(r["ii"][:, :], [[1, P]], base=0, channel_multiplier=0))
            ch(e.iota(r["ip"][:, :], [[0, 1]], base=0, channel_multiplier=1))
            ch.wait()
            ch(e.tensor_copy(kn.iota[:, :], r["ii"][:, :]))
            e.tensor_copy(kn.pcol[:, :], r["ip"][:, :]).then_inc(r["ready"], 1)

        def vector(e, ch):
            ch(e.memset(kn.ones[:, :], 1.0))
            ch(e.memset(kn.zero1[:, :], 0.0))
            ch(e.memset(kn.half1[:, :], 0.5))
            ch(e.memset(kn.eps1[:, :], EPS))
            ch(e.memset(kn.hp1[:, :], 1.5707963267948966))
            e.wait_ge(r["ready"], 1)
            ch(e.tensor_copy(kn.iotab[:, :], kn.iota[:, :]))
            ch(e.tensor_scalar(kn.ident[:, :], kn.iota[:, :], kn.pcol[:, 0:1], None, ALU.is_equal))
            ch(e.tensor_scalar(kn.before[:, :], kn.iota[:, :], kn.pcol[:, 0:1], None, ALU.is_gt))
            ch.wait()
            ch(e.tensor_copy(kn.identb[:, :], kn.ident[:, :]))
            ch(e.tensor_copy(kn.beforeb[:, :], kn.before[:, :]))
            ch.wait()

        def sync(e, ch):
            full = (N // P) * P
            e.dma_start(kn.X[:, 0:N // P, :], ins["x"][0:full, :].rearrange("(b p) h -> p b h", p=P)).then_inc(r["ld"], 16)
            e.dma_start(kn.X[0:N - full, N // P, :], ins["x"][full:N, :]).then_inc(r["ld"], 16)
            e.wait_ge(r["ld"], 32)

        def scalar(e, ch):
            pass
        return dict(gpsimd=gpsimd, vector=vector, sync=sync)
    def build0(r):
        def vector(e, ch):
            ch(e.memset(kn.X[:, NB - 1, :], 0.0))
            ch.wait()
        return dict(vector=vector)
    phase(kn, "clear", build0)
    phase(kn, "const", build, sbufs=[("ii", [P, P], I32), ("ip", [P, 1], I32)], sems=["ready", "ld"])

def split_keys(kn):
    kn.lo_rows = dram(kn, "lo_rows", (2, EP), BF16)
    kn.khi = kn.keys_ctx.enter_context(kn.nc.sbuf_tensor("khi", [P, 2, T], F32))
    kn.klo = kn.keys_ctx.enter_context(kn.nc.sbuf_tensor("klo", [P, 2, T], F32))
    kn.kin = kn.keys_ctx.enter_context(kn.nc.sbuf_tensor("kin", [P, 2, T], I32))
    kn.klob = kn.keys_ctx.enter_context(kn.nc.sbuf_tensor("klob", [P, 2, T], BF16))
    kn.khib = kn.keys_ctx.enter_context(kn.nc.sbuf_tensor("khib", [P, 2, T], BF16))

    def build(r):
        def sync(e, ch):
            for q, n in enumerate(("dst", "src")):
                e.dma_start(kn.kin[:, q, :], kn.ins[n + "_tiles"]).then_inc(r["ld"], 16)
                e.dma_start(r["lin"][:, q, :], kn.ins[n + "_lin"].rearrange("(p c) -> p c", p=P)).then_inc(r["ld"], 16)
            e.wait_ge(r["lo"], 1)
            for q in range(2):
                e.dma_start(kn.lo_rows[q].rearrange("(p c) -> p c", p=P), r["linb"][:, q, :]).then_inc(r["st"], 16)
            e.wait_ge(r["st"], 32)

        def vector(e, ch):
            e.wait_ge(r["ld"], 64)
            ch(e.tensor_scalar(r["a"][:, :, :], kn.kin[:, :, :], 127, None, ALU.bitwise_and))
            ch(e.tensor_scalar(r["b"][:, :, :], kn.kin[:, :, :], 7, None, ALU.logical_shift_right))
            ch(e.tensor_scalar(r["c"][:, :, :], r["lin"][:, :, :], 127, None, ALU.bitwise_and))
            ch.wait()
            ch(e.tensor_copy(kn.klo[:, :, :], r["a"][:, :, :]))
            ch(e.tensor_copy(kn.khi[:, :, :], r["b"][:, :, :]))
            ch(e.tensor_copy(kn.klob[:, :, :], r["a"][:, :, :]))
            ch(e.tensor_copy(kn.khib[:, :, :], r["b"][:, :, :]))
            e.tensor_copy(r["linb"][:, :, :], r["c"][:, :, :]).then_inc(r["lo"], 1)
            ch.wait()
        return dict(sync=sync, vector=vector)
    phase(kn, "keys", build, sbufs=[("lin", [P, 2, T], I32), ("linb", [P, 2, T], BF16), ("a", [P, 2, T], I32),
                                     ("b", [P, 2, T], I32), ("c", [P, 2, T], I32)], sems=["ld", "lo", "st"])

def one_hots(kn, e, ch, r, st, q, what):
    w = P if what == "lo" else NB
    src = kn.klob if what == "lo" else kn.khib
    tiles = src[:, q, bass.ds(st.i * GT, GT)]
    return e.tensor_tensor(r["oh" + what][:, st.par, q, :, :], tiles.unsqueeze(2).to_broadcast([P, GT, w]),
                           kn.iotab[:, None, 0:w].to_broadcast([P, GT, w]), ALU.is_equal)

def histogram(kn):
    n = T // GT

    def build(r):
        def vector(e, ch):
            def hot(st):
                wait_step(e, r["pe"], st, 2)
                for q in range(2):
                    one_hots(kn, e, ch, r, st, q, "lo")
                    ins = one_hots(kn, e, ch, r, st, q, "hi")
                ins.then_inc(r["hot"], 1)
            run_steps(e, ch, [(hot, 0)], n)
            e.wait_ge(r["pe"], n)
            for q in range(2):
                ch(e.tensor_copy(kn.count[:, q, :], r["hist"][:, q, 0:NB]))
            ch.wait()

        def tensor(e, ch):
            def add(st, first=False):
                wait_step(e, r["hot"], st)
                for j in range(GT):
                    for q in range(2):
                        f = isinstance(st.i, int) and st.i == 0 and j == 0
                        ins = e.matmul(r["hist"][:, q, 0:NB], r["ohlo"][:, st.par, q, j, :],
                                       r["ohhi"][:, st.par, q, j, :], start=f, stop=False, skip_group_check=True)
                ins.then_inc(r["pe"], 1)
            run_steps(e, ch, [(add, 0)], n)
        return dict(vector=vector, tensor=tensor)
    phase(kn, "hist", build, psums=[("hist", [P, 2, 512], F32)],
               sbufs=[("ohlo", [P, 2, 2, GT, P], BF16), ("ohhi", [P, 2, 2, GT, NB], BF16)], sems=["hot", "pe"])

def offsets(kn):
    half = SLOTS // 2
    nt = -(-T // P)

    def build(r):
        def tensor(e, ch):
            e.matmul(r["small"][:, 0:2 * NB], kn.before[:, :], kn.count[:, :, :].rearrange("p q b -> p (q b)"),
                     start=True, stop=True)
            e.matmul(r["small"][:, 2 * NB:4 * NB], kn.ones[:, :],
                     kn.count[:, :, :].rearrange("p q b -> p (q b)"), start=True, stop=True,
                     skip_group_check=True).then_inc(r["sums"], 1)
            for q in range(2):
                e.wait_ge(r["less"], q + 1)
                for h in range(2):
                    for c in range(nt):
                        ins = e.matmul(r["tiles"][:, q, h, 0:half], kn.ones[:, :],
                                       r["lt"][:, q, c, h * half:(h + 1) * half], start=(c == 0), stop=(c == nt - 1))
                ins.then_inc(r["counted"], 1)

        def gpsimd(e, ch):
            e.iota(r["is"][:, :], [[1, SLOTS]], base=0, channel_multiplier=0).then_inc(r["iota"], 1)

        def vector(e, ch):
            e.wait_ge(r["iota"], 1)
            ch(e.tensor_copy(r["s"][:, :], r["is"][:, :]))
            for c in range(nt):
                ch(e.tensor_scalar(r["last"][:, c:c + 1], kn.pcol[:, 0:1], float(P), float(P * P * c + P - 1),
                                   ALU.mult, ALU.add))
            e.wait_ge(r["sums"], 1)
            ch(e.tensor_copy(r["tot"][:, :], r["small"][:, 2 * NB:4 * NB]))
            ch.wait()
            for q in range(2):
                ch(e.tensor_tensor_scan(r["upto"][:, q, :], kn.ones[:, 0:NB], r["tot"][:, q * NB:(q + 1) * NB], 0.0,
                                        ALU.mult, ALU.add))
            ch.wait()
            ch(e.tensor_tensor(r["excl"][:, :], r["upto"][:, :, :].rearrange("p q b -> p (q b)"), r["tot"][:, :],
                               ALU.subtract))
            ch.wait()
            ch(e.tensor_tensor(kn.start[:, :, :].rearrange("p q b -> p (q b)"), r["small"][:, 0:2 * NB],
                               r["excl"][:, :], ALU.add))
            for q in range(2):
                for c in range(nt):
                    ch(e.tensor_scalar(r["le"][:, q, c, :], r["upto"][:, q, 0:NB - 1], r["last"][:, c:c + 1], None,
                                       ALU.is_le))
            ch.wait()
            for q in range(2):
                ch(e.tensor_reduce(r["blk"][:, q, :], r["le"][:, q, :, :], AX, ALU.add))
            for c in range(nt):
                ch(e.tensor_scalar(r["t"][:, c:c + 1], kn.pcol[:, 0:1], float(P * c), None, ALU.add))
            ch.wait()
            for q in range(2):
                ch(e.tensor_tensor(r["val"][:, q, :], r["blk"][:, q, :], r["t"][:, :], ALU.add))
            ch.wait()
            for q in range(2):
                for c in range(nt):
                    ins = e.tensor_scalar(r["lt"][:, q, c, :], r["s"][:, :], r["val"][:, q, c:c + 1], None, ALU.is_gt)
                ins.then_inc(r["less"], 1)
            e.wait_ge(r["counted"], 2)
            for q in range(2):
                for h in range(2):
                    cols = slice(h * half, (h + 1) * half)
                    ch(e.tensor_copy(kn.slot_reg[64 * q:64 * q + 32, cols], r["tiles"][0:32, q, h, 0:half]))
                    ch(e.scalar_tensor_tensor(r["b"][:, q, cols], r["tiles"][:, q, h, 0:half], -1.0, r["s"][:, cols],
                                              ALU.mult, ALU.add))
            ch.wait()
            for q in range(2):
                ch(e.tensor_copy(kn.slot_reg[64 * q + 32:64 * q + 64, :], r["b"][0:32, q, :]))
                ch(e.tensor_scalar(kn.local[:, q, :], r["b"][:, q, :], float(P), None, ALU.mult))
            ch.wait()
        return dict(tensor=tensor, gpsimd=gpsimd, vector=vector)
    phase(kn, "offsets", build, psums=[("small", [P, 512], F32), ("tiles", [P, 2, 2, 512], F32)],
               sbufs=[("is", [P, SLOTS], I32), ("s", [P, SLOTS], F32), ("last", [P, nt], F32), ("tot", [P, 2 * NB], F32),
                      ("upto", [P, 2, NB], F32), ("excl", [P, 2 * NB], F32), ("le", [P, 2, nt, NB - 1], F32),
                      ("blk", [P, 2, nt], F32), ("t", [P, nt], F32), ("val", [P, 2, nt], F32),
                      ("lt", [P, 2, nt, SLOTS], F32), ("b", [P, 2, SLOTS], F32)],
               sems=["sums", "iota", "less", "counted"])

def sort(kn):
    n = T // GT
    rec_tiles = kn.ins["rec"].rearrange("(t p) c -> p t c", p=P)
    kn.sorted = dram(kn, "sorted_records", (EP, P))

    def build(r):
        def sync(e, ch):
            def load(st):
                wait_tiles(e, r["grown"], st, 2)
                wait_free(e, r["sent"], st, GT)
                for q in range(2):
                    e.dma_start(r["rows"][:, st.par, q, :],
                                kn.lo_rows[q:q + 1, bass.ds(st.i * (GT * P), GT * P)].to_broadcast([P, GT * P])
                                ).then_inc(r["ld"][st.par], 16)
                e.dma_start(r["rec"][:, st.par, :, 0:NREC], rec_tiles[:, bass.ds(st.i * GT, GT), :]
                            ).then_inc(r["ld"][st.par], 16)
            e.wait_ge(r["cleared"], 1)
            run_steps(e, ch, [(load, 0)], n)

        def vector(e, ch):
            e.memset(r["rec"][:, :, :, :], 0.0).then_inc(r["cleared"], 1)

            def hot(st):
                wait_tiles(e, r["grown"], st, 2)
                wait_load(e, r["ld"], st, 3)
                for q in range(2):
                    one_hots(kn, e, ch, r, st, q, "lo")
                    one_hots(kn, e, ch, r, st, q, "hi")
                e.tensor_scalar(r["ohT"][:, st.par, :, :], r["rows"][:, st.par, :, :], kn.pcol[:, 0:1], None,
                                ALU.is_equal).then_inc(r["hot"], 1)

            def mask(st):
                for u in range(4):
                    q, h = u // 2, u % 2
                    e.wait_ge(r["same_done"], st.i * 4 + (u + 1))
                    e.tensor_tensor(r["mask"][:, st.par, q, 4 * h:4 * h + 4, :], r["same"][:, u % 2, :, :],
                                    kn.before[:, None, :].to_broadcast([P, 4, P]), ALU.mult
                                    ).then_inc(r["masked"], 1)

            def place(st):
                wait_tiles(e, r["grown"], st)
                wait_free(e, r["sent"], st, GT)
                ch.wait()
                for q in range(2):
                    ch(e.tensor_tensor(r["pick"][:, q, :, :], r["rank"][:, st.par, q, :, 0:NB],
                                       r["ohhi"][:, st.par, q, :, :], ALU.mult))
                tiles = kn.kin[:, :, bass.ds(st.i * GT, GT)]
                ch(e.tensor_copy(r["rec"][:, st.par, :, W_DST:W_SRC + 1].rearrange("p t q -> p q t"), tiles))
                ch.wait()
                ch(e.tensor_reduce(r["pos"][:, :, :], r["pick"][:, :, :, :], AX, ALU.add))
                ch.wait()
                ch(e.tensor_copy(r["idx"][:, st.par, :], r["pos"][:, 0, :]))
                e.tensor_scalar(r["rec"][:, st.par, :, W_POS], r["pos"][:, 1, :], BIG, None, ALU.add
                                ).then_inc(r["placed"], 1)
            run_steps(e, ch, [(hot, 0), (mask, 0), (place, 1)], n)

        def scalar(e, ch):
            e.wait_ge(r["grown"], 1)
            e.activation(r["snap"][:, 0, :, :], r["running"][:, :, 0:NB], ACT.Copy).then_inc(r["snapped"], 1)

            def snap(st):
                for j in range(GT):
                    e.wait_ge(r["grown"], st.i * GT + (j + 2))
                    e.activation(r["snap"][:, (j + 1) % 2, :, :], r["running"][:, :, 0:NB], ACT.Copy
                                 ).then_inc(r["snapped"], 1)
            run_steps(e, ch, [(snap, 0)], n)

        def tensor(e, ch):
            for q in range(2):
                ins = e.matmul(r["running"][:, q, 0:NB], kn.ident[:, :], kn.start[:, q, :], start=True, stop=False,
                               skip_group_check=True)
            ins.then_inc(r["grown"], 1)

            def same(st):
                wait_step(e, r["hot"], st)
                for u in range(4):
                    q, h = u // 2, u % 2
                    v = st.i * 4 + (u - 1)
                    if not isinstance(v, int) or v > 0:
                        e.wait_ge(r["masked"], v)
                    for j in range(4):
                        t = r["ohT"][:, st.par, q, (4 * h + j) * P:(4 * h + j + 1) * P]
                        ins = e.matmul(r["same"][:, u % 2, j, :], t, t, start=True, stop=True)
                    ins.then_inc(r["same_done"], 1)

            def rank(st):
                wait_step(e, r["placed"], st, 2)
                e.wait_ge(r["masked"], st.i * 4 + 4)
                for j in range(GT):
                    e.wait_ge(r["snapped"], st.i * GT + (j + 1))
                    for q in range(2):
                        out = r["rank"][:, st.par, q, j, 0:NB]
                        e.matmul(out, r["ohT"][:, st.par, q, j * P:(j + 1) * P], r["snap"][:, j % 2, q, :],
                                 start=True, stop=False, skip_group_check=True)
                        e.matmul(out, r["mask"][:, st.par, q, j, :], r["ohhi"][:, st.par, q, j, :],
                                 start=False, stop=True, skip_group_check=True)
                        ins = e.matmul(r["running"][:, q, 0:NB], r["ohlo"][:, st.par, q, j, :],
                                       r["ohhi"][:, st.par, q, j, :], start=False, stop=False, skip_group_check=True)
                    ins.then_inc(r["grown"], 1)
            run_steps(e, ch, [(same, 0), (rank, 0)], n)

        def gpsimd(e, ch):
            def send(st):
                wait_step(e, r["placed"], st)
                take_waits(e, kn.tally)
                for j in range(GT):
                    e.indirect_dma_start(kn.sorted[:, :],
                                         bass.IndirectOffsetOnAxis(ap=r["idx"][:, st.par, j:j + 1], axis=0),
                                         r["rec"][:, st.par, j, :], None, bounds_check=EP - 1
                                         ).then_inc(r["sent"][st.par], 16)
            run_steps(e, ch, [(send, 0)], n)
            for j in range(2):
                e.wait_ge(r["sent"][j], 16 * GT * (n // 2))
        return dict(sync=sync, vector=vector, scalar=scalar, tensor=tensor, gpsimd=gpsimd)
    phase(kn, "sort", build, psums=[("same", [P, 2, 4, P], F32), ("rank", [P, 2, 2, GT, 64], F32),
                                     ("running", [P, 2, 512], F32)],
               sbufs=[("rows", [P, 2, 2, GT * P], BF16), ("rec", [P, 2, GT, P], F32), ("ohlo", [P, 2, 2, GT, P], BF16),
                      ("ohhi", [P, 2, 2, GT, NB], BF16), ("ohT", [P, 2, 2, GT * P], F32),
                      ("mask", [P, 2, 2, GT, P], BF16), ("pick", [P, 2, GT, NB], F32), ("pos", [P, 2, GT], F32),
                      ("idx", [P, 2, GT], I32), ("snap", [P, 2, 2, NB], F32)],
               sems=["cleared", "hot", "same_done", "masked", "grown", "snapped", "placed"],
               pairs=["ld", "sent"])

def slot_columns(kn):
    chunk = 98
    srt = kn.sorted.rearrange("(t p) c -> p t c", p=P)
    meta = flat(kn, kn.MT).rearrange("p (t c) -> p t c", c=META)

    def build(r):
        def sync(e, ch):
            for n, t in ((kn.W, kn.ins["mats"]), (kn.V, kn.ins["vecs"])):
                e.dma_start(n[tuple([slice(None)] * len(t.shape))], t).then_inc(r["wld"], 16)
            e.dma_start(kn.R[:, :, :].rearrange("p r h -> p (r h)"),
                        kn.ins["rows"].to_broadcast([P, len(ROWS) * H])).then_inc(r["wld"], 16)
            for c in range(T // chunk):
                e.dma_start(meta[:, c * chunk:(c + 1) * chunk, :], srt[:, c * chunk:(c + 1) * chunk, CM:CM + META]
                            ).then_inc(r["ld"], 16)
            e.wait_ge(r["ld"], 16 * (T // chunk))
            e.wait_ge(r["wld"], 48)

        def vector(e, ch):
            e.wait_ge(r["ld"], 16 * (T // chunk))

            def pick(st):
                for j in range(G):
                    t = e.value_load(kn.slot_reg[0:1, bass.ds(st.i * G + j, 1)], min_val=0, max_val=T - 1)
                    ins = e.tensor_copy(r["m"][:, bass.ds((st.i * G + j) * META, META)],
                                        meta[:, bass.ds(t, 1), :].rearrange("p a c -> p (a c)"))
                    ch(ins)
            run_steps(e, ch, [(pick, 0)], STEPS)
            ch.wait()
            m = r["m"][:, :].rearrange("p (s c) -> p s c", c=META)
            ch(e.tensor_tensor(kn.local[:, 0, :], m[:, :, 4], kn.local[:, 0, :], ALU.subtract))
            ch(e.tensor_copy(kn.src_of[:, :], m[:, :, 5]))
            ch(e.tensor_copy(kn.wt[:, :], m[:, :, 3]))
            ch(e.tensor_tensor(r["a"][:, 0, :], m[:, :, 0], m[:, :, 0], ALU.mult))
            ch(e.tensor_tensor(r["a"][:, 1, :], m[:, :, 1], m[:, :, 1], ALU.mult))
            ch(e.tensor_tensor(r["a"][:, 2, :], m[:, :, 2], m[:, :, 2], ALU.mult))
            ch.wait()
            ch(e.tensor_tensor(r["a"][:, 0, :], r["a"][:, 0, :], r["a"][:, 1, :], ALU.add))
            ch.wait()
            ch(e.tensor_scalar(r["a"][:, 1, :], kn.local[:, 0, :], float(P), None, ALU.is_lt))
            ch.wait()
            ch(e.scalar_tensor_tensor(r["a"][:, 1, :], kn.local[:, 0, :], 0.0, r["a"][:, 1, :], ALU.is_ge, ALU.mult))
            e.tensor_tensor(r["a"][:, 0, :], r["a"][:, 0, :], r["a"][:, 2, :], ALU.add).then_inc(r["sq"], 1)
            ch.wait()
            ch(e.scalar_tensor_tensor(kn.place[:, :], r["a"][:, 1, :], -BIG, m[:, :, 6], ALU.mult, ALU.add))
            e.wait_ge(r["root"], 1)
            ch(e.tensor_scalar(kn.cut[:, :], r["a"][:, 0, :], 10.0, None, ALU.is_le))
            e.tensor_scalar(r["a"][:, 2, :], r["a"][:, 0, :], 10.0, None, ALU.min).then_inc(r["capped"], 1)
            e.wait_ge(r["cosine"], 1)
            ch(e.tensor_scalar(r["a"][:, 0, :], r["a"][:, 2, :], 1.0, 0.5, ALU.add, ALU.mult))
            ch.wait()
            ch(e.tensor_tensor(kn.cut[:, :], kn.cut[:, :], r["a"][:, 0, :], ALU.mult))
            ch.wait()

        def scalar(e, ch):
            e.wait_ge(r["sq"], 1)
            e.activation(r["a"][:, 0, :], r["a"][:, 0, :], ACT.Sqrt).then_inc(r["root"], 1)
            e.wait_ge(r["capped"], 1)
            e.activation(r["a"][:, 2, :], r["a"][:, 2, :], ACT.Sin, bias=kn.hp1[:, 0:1],
                         scale=-3.141592653589793 / 10.0).then_inc(r["cosine"], 1)
        return dict(sync=sync, vector=vector, scalar=scalar)
    phase(kn, "slots", build, sbufs=[("m", [P, SLOTS * META], F32), ("a", [P, 3, SLOTS], F32)],
               sems=["ld", "wld", "sq", "root", "capped", "cosine"])

def mat(kn, name, rows=P):
    return kn.W[0:rows, MATS.index(name), :]

def vec(kn, name):
    i = VECS.index(name)
    return kn.V[:, i:i + 1]

def row(kn, name):
    return kn.R[:, ROWS.index(name), :]

def block(kn, t, b):
    return flat(kn, t)[:, bass.ds(b * P, P)]

def layernorm(kn, name, src=None, dst=None, func=ACT.Relu):
    src, dst = src or kn.X, dst or kn.Hn

    def build(r):
        def vector(e, ch):
            def stats(st):
                ch(e.bn_stats(r["six"][:, bass.ds(st.i * 6, 6)], block(kn, src, st.i)))
            run_steps(e, ch, [(stats, 0)], NB)
            ch.wait()
            for b in range(NB):
                ch(e.bn_aggr(r["mv"][:, 2 * b:2 * b + 2], r["six"][:, 6 * b:6 * b + 6]))
            ch.wait()
            mv = r["mv"][:, :].rearrange("p (b k) -> p b k", k=2)
            e.tensor_copy(r["var"][:, :], mv[:, :, 1]).then_inc(r["var_ok"], 1)
            e.wait_ge(r["std"], 1)
            ch(e.reciprocal(r["rstd"][:, :], r["var"][:, :]))
            ch.wait()
            e.scalar_tensor_tensor(r["shift"][:, :], mv[:, :, 0], -1.0, r["rstd"][:, :], ALU.mult, ALU.mult
                                   ).then_inc(r["scales"], 1)

        def scalar(e, ch):
            e.wait_ge(r["var_ok"], 1)
            e.activation(r["var"][:, :], r["var"][:, :], ACT.Sqrt, bias=kn.eps1[:, 0:1]).then_inc(r["std"], 1)
            e.wait_ge(r["scales"], 1)

            def norm(st):
                ch(e.activation(block(kn, dst, st.i), block(kn, src, st.i), func,
                                bias=r["shift"][:, bass.ds(st.i, 1)], scale=r["rstd"][:, bass.ds(st.i, 1)]))
            run_steps(e, ch, [(norm, 0)], NB)
            ch.wait()
        return dict(vector=vector, scalar=scalar)
    phase(kn, name, build, sbufs=[("six", [P, 6 * NB], F32), ("mv", [P, 2 * NB], F32), ("var", [P, NB], F32),
                                   ("rstd", [P, NB], F32), ("shift", [P, NB], F32)],
               sems=["var_ok", "std", "scales"])

def l0_nodes(kn):
    def build(r):
        def tensor(e, ch):
            def turn(st):
                wait_step(e, r["fetched"], st)
                wait_step(e, r["hT_ok"], st, 2)
                e.transpose(r["pA"][:, st.par, 0:P], r["hb"][:, st.par, :], kn.ident[:, :]).then_inc(r["turned"], 1)

            def lin(st):
                wait_step(e, r["hT_ok"], st)
                wait_step(e, r["xl_ok"], st, 2)
                e.matmul(r["pB"][:, st.par, 0:P], r["hT"][:, st.par, :], mat(kn, "W_lin"), start=True, stop=True
                         ).then_inc(r["lin_ok"], 1)

            def turn_xl(st):
                wait_step(e, r["xl_ok"], st)
                wait_step(e, r["xlT_ok"], st, 2)
                e.transpose(r["pC"][:, st.par, 0:P], r["xl"][:, st.par, :], kn.ident[:, :]).then_inc(r["xl_turned"], 1)

            def att(st):
                wait_step(e, r["xlT_ok"], st)
                wait_step(e, r["s_ok"], st, 2)
                e.matmul(r["pD"][:, st.par, 0:2 * HEADS], r["xlT"][:, st.par, :], mat(kn, "W_att")[:, 0:2 * HEADS],
                         start=True, stop=True).then_inc(r["att_ok"], 1)
            run_steps(e, ch, [(turn, 0), (lin, 0), (turn_xl, 1), (att, 1)], NB)

        def scalar(e, ch):
            def fetch(st):
                wait_step(e, r["turned"], st, 2)
                e.activation(r["hb"][:, st.par, :], block(kn, kn.Hn, st.i), ACT.Copy).then_inc(r["fetched"], 1)

            def copy_h(st):
                wait_step(e, r["turned"], st)
                wait_step(e, r["lin_ok"], st, 2)
                e.activation(r["hT"][:, st.par, :], r["pA"][:, st.par, 0:P], ACT.Copy).then_inc(r["hT_ok"], 1)

            def copy_xl(st):
                wait_step(e, r["xl_turned"], st)
                wait_step(e, r["att_ok"], st, 2)
                e.activation(r["xlT"][:, st.par, :], r["pC"][:, st.par, 0:P], ACT.Copy).then_inc(r["xlT_ok"], 1)
            run_steps(e, ch, [(fetch, 0), (copy_h, 0), (copy_xl, 1)], NB)

        def vector(e, ch):
            def xl(st):
                wait_step(e, r["lin_ok"], st)
                wait_step(e, r["xl_turned"], st, 2)
                ch(e.tensor_tensor(block(kn, kn.TB, st.i), r["pB"][:, st.par, 0:P], row(kn, "b_lin"), ALU.add))
                e.tensor_tensor(r["xl"][:, st.par, :], r["pB"][:, st.par, 0:P], row(kn, "b_lin"), ALU.add
                                ).then_inc(r["xl_ok"], 1)

            def s(st):
                wait_step(e, r["att_ok"], st)
                e.tensor_tensor(kn.sij[:, bass.ds(st.i * 2 * HEADS, 2 * HEADS)], r["pD"][:, st.par, 0:2 * HEADS],
                                row(kn, "b_att")[:, 0:2 * HEADS], ALU.add).then_inc(r["s_ok"], 1)
            run_steps(e, ch, [(xl, 0), (s, 1)], NB)
            e.wait_ge(r["s_ok"], NB)
            sij = kn.sij[:, :].rearrange("p (b k) -> p b k", k=2 * HEADS)
            ch(e.memset(r["first"][:, :, 4:5], 1.0))
            ch(e.memset(r["first"][:, :, 6:8], 0.0))
            ch(e.tensor_copy(r["first"][:, :, 0:4], sij[:, :, 0:4]))
            ch(e.tensor_scalar(r["first"][:, :, 5], kn.iota[:, 0:NB], float(P), kn.pcol[:, 0:1], ALU.mult, ALU.add))
            ch(e.memset(kn.MT[:, :, :], 0.0))
            ch(e.tensor_scalar(r["none"][:, :], kn.count[:, 1, :], 0.0, None, ALU.is_equal))
            ch.wait()
            e.scalar_tensor_tensor(r["at"][:, :], r["none"][:, :], BIG, kn.start[:, 1, :], ALU.mult, ALU.add
                                   ).then_inc(r["rows_ok"], 1)

        def sync(e, ch):
            e.wait_ge(r["rows_ok"], 1)
            e.dma_start(kn.firsts.rearrange("(p c) k -> p (c k)", p=P), flat(kn, kn.MT)).then_inc(r["zeroed"], 16)
            e.wait_ge(r["zeroed"], 16)

        def gpsimd(e, ch):
            e.wait_ge(r["zeroed"], 16)
            for b in range(NB):
                e.indirect_dma_start(kn.firsts[:, :], bass.IndirectOffsetOnAxis(ap=r["at"][:, b:b + 1], axis=0),
                                     r["first"][:, b, :], None, bounds_check=EP - 1, oob_is_err=False
                                     ).then_inc(r["sent"], 16)
            e.wait_ge(r["sent"], 16 * NB)
        return dict(tensor=tensor, scalar=scalar, vector=vector, sync=sync, gpsimd=gpsimd)
    kn.firsts = dram(kn, "firsts", (EP, 8))
    phase(kn, "l0n", build, psums=[(n, [P, 2, BANK], F32) for n in ("pA", "pB", "pC", "pD")],
               sbufs=[("hb", [P, 2, P], F32), ("xl", [P, 2, P], F32), ("hT", [P, 2, P], F32),
                      ("xlT", [P, 2, P], F32), ("first", [P, NB, 8], F32),
                      ("none", [P, NB], F32), ("at", [P, NB], I32)],
               sems=["fetched", "turned", "hT_ok", "lin_ok", "xl_ok", "xl_turned", "xlT_ok", "att_ok", "s_ok", "rows_ok",
                     "zeroed", "sent"])

def hot_stage(kn, e, r, q, free, back=2):
    def hot(st):
        wait_step(e, free, st, back)
        for j in range(G):
            ins = e.tensor_scalar(r["oh"][:, st.par, j, :], kn.iota[:, :],
                                  kn.local[:, q, bass.ds(st.i * G + j, 1)], None, ALU.is_equal)
        ins.then_inc(r["hot"], 1)
    return hot

def turn_hot_stage(kn, e, r, banks=2):
    def turn(st):
        wait_step(e, r["hot"], st)
        wait_step(e, r["ohT_ok"], st, banks)
        for j in range(G):
            ins = e.transpose(r["pT"][:, st.par % banks, j, :], r["oh"][:, st.par, j, :], kn.ident[:, :])
        ins.then_inc(r["turned"], 1)
    return turn

def copy_hot_stage(kn, e, r, used, banks=2):
    def copy(st):
        wait_step(e, r["turned"], st)
        wait_step(e, used, st, 2)
        e.activation(r["ohT"][:, st.par, :, :], r["pT"][:, st.par % banks, :, :], ACT.Copy
                     ).then_inc(r["ohT_ok"], 1)
    return copy

def slot_value(kn, e, st, j, which):
    return e.value_load(kn.slot_reg[which:which + 1, bass.ds(st.i * G + j, 1)], min_val=0,
                        max_val=(T if which % 64 == 0 else NB) - 1)

def add_stage(kn, e, ch, r, q):
    def add(st):
        wait_step(e, r["summed"], st)
        for j in range(G):
            b = slot_value(kn, e, st, j, 64 * q + 32)
            ch.wait()
            acc = block(kn, kn.AC, b)
            ins = e.tensor_tensor(acc, acc, r["pR"][:, st.par, j, :], ALU.add)
            if j < G - 1:
                ch(ins)
        ins.then_inc(r["added"], 1)
        e.wait_ge(r["added"], st.i + 1)
    return add

def l0_scores(kn):
    kn.sj_src = dram(kn, "sj_src", (EP, HEADS))
    kn.slot_sj = flat(kn, kn.MT)[:, 0:SLOTS * HEADS]

    def build(r):
        def vector(e, ch):
            hot = hot_stage(kn, e, r, 0, r["turned"])

            def idx(st):
                wait_free(e, r["sent"], st, G)
                e.tensor_copy(r["idx"][:, st.par, :], kn.place[:, bass.ds(st.i * G, G)]).then_inc(r["idx_ok"], 1)
            run_steps(e, ch, [(hot, 0), (idx, 0)], STEPS)

        def tensor(e, ch):
            turn = turn_hot_stage(kn, e, r)

            def pick(st):
                wait_step(e, r["ohT_ok"], st)
                wait_step(e, r["kept"], st, 2)
                for j in range(G):
                    b = slot_value(kn, e, st, j, 32)
                    ins = e.matmul(r["pS"][:, st.par, j * HEADS:(j + 1) * HEADS], r["ohT"][:, st.par, j, :],
                                   kn.sij[:, bass.ds(b * (2 * HEADS) + HEADS, HEADS)], start=True, stop=True)
                ins.then_inc(r["picked"], 1)
            run_steps(e, ch, [(turn, 0), (pick, 1)], STEPS)

        def scalar(e, ch):
            copy = copy_hot_stage(kn, e, r, r["picked"])

            def keep(st):
                wait_step(e, r["picked"], st)
                e.activation(kn.slot_sj[:, bass.ds(st.i * G * HEADS, G * HEADS)],
                             r["pS"][:, st.par, 0:G * HEADS], ACT.Copy).then_inc(r["kept"], 1)
                wait_free(e, r["sent"], st, G)
                e.activation(r["out"][:, st.par, :, :].rearrange("p j k -> p (j k)"), r["pS"][:, st.par, 0:G * HEADS], ACT.Copy).then_inc(r["out_ok"], 1)
            run_steps(e, ch, [(copy, 0), (keep, 1)], STEPS)

        def gpsimd(e, ch):
            def send(st):
                wait_step(e, r["out_ok"], st)
                wait_step(e, r["idx_ok"], st)
                take_waits(e, kn.tally)
                for j in range(G):
                    e.indirect_dma_start(kn.sj_src[:, :],
                                         bass.IndirectOffsetOnAxis(ap=r["idx"][:, st.par, j:j + 1], axis=0),
                                         r["out"][:, st.par, j, :], None, bounds_check=EP - 1, oob_is_err=False
                                         ).then_inc(r["sent"][st.par], 16)
            run_steps(e, ch, [(send, 0)], STEPS)
            for j in range(2):
                e.wait_ge(r["sent"][j], 16 * G * (STEPS // 2))
        return dict(vector=vector, tensor=tensor, scalar=scalar, gpsimd=gpsimd)
    phase(kn, "l0s", build, psums=[("pT", [P, 2, G, P], F32), ("pS", [P, 2, BANK], F32)],
               sbufs=[("oh", [P, 2, G, P], F32), ("ohT", [P, 2, G, P], F32), ("out", [P, 2, G, HEADS], F32),
                      ("idx", [P, 2, G], I32)],
               sems=["hot", "turned", "ohT_ok", "picked", "kept", "out_ok", "idx_ok"], pairs=["sent"])

def l0_segments(kn):
    kn.run_ml = dram(kn, "run_ml", (EP, 2 * HEADS))
    kn.src_sorted = dram(kn, "src_sorted", (EP,))
    fl = flat(kn, kn.AC)
    firsts = fl.rearrange("p (c k) -> p c k", k=8)
    d0 = fl[:, 0:HEADS * T].rearrange("p (k c) -> p k c", k=HEADS)
    d1 = fl[:, HEADS * T:2 * HEADS * T].rearrange("p (k c) -> p k c", k=HEADS)
    hl = flat(kn, kn.Hn)
    sj = hl[:, 0:HEADS * T].rearrange("p (c k) -> p c k", k=HEADS)
    si = hl[:, HEADS * T:2 * HEADS * T].rearrange("p (k c) -> p k c", k=HEADS)
    both = hl.rearrange("p (c k) -> p c k", k=2 * HEADS)

    def build(r):
        turns = [0]

        def sync(e, ch):
            e.dma_start(fl, kn.firsts.rearrange("(p c) k -> p (c k)", p=P)).then_inc(r["ld"], 16)
            e.dma_start(hl[:, 0:HEADS * T], kn.sj_src.rearrange("(p c) k -> p (c k)", p=P)).then_inc(r["ld"], 16)
            e.wait_ge(r["keys_ok"], 1)
            e.dma_start(kn.src_sorted.rearrange("(p c) -> p c", p=P), r["keyrow"][:, :]).then_inc(r["st"], 16)
            e.wait_ge(r["both_ok"], 1)
            e.dma_start(kn.run_ml.rearrange("(p c) k -> p (c k)", p=P), hl).then_inc(r["st"], 16)
            e.wait_ge(r["st"], 32)

        n_carry = 4

        def tensor(e, ch):
            for i in range(n_carry):
                e.wait_ge(r["ends_ok"], i + 1)
                e.transpose(r["pa"][0:HEADS, 0:P], r["ends"][:, 0:HEADS], kn.ident[:, :])
                e.transpose(r["pb"][0:HEADS, 0:P], r["ends"][:, HEADS:2 * HEADS], kn.ident[:, :]).then_inc(r["rows_ok"], 1)
                e.wait_ge(r["carried"], i + 1)
                e.transpose(r["pc"][:, 0:HEADS], r["crow"][0:HEADS, 0:P], kn.ident[0:HEADS, 0:HEADS]
                            ).then_inc(r["back"], 1)

        def vector(e, ch):
            def carry(op0, op1, init):
                i = turns[0]
                turns[0] += 1
                ch.wait()
                e.tensor_copy(r["ends"][:, 0:1], r["ends"][:, 0:1]).then_inc(r["ends_ok"], 1)
                e.wait_ge(r["rows_ok"], i + 1)
                ch(e.tensor_copy(r["arow"][0:HEADS, :], r["pa"][0:HEADS, 0:P]))
                ch(e.memset(r["crow"][0:HEADS, 0:1], init))
                ch.wait()
                e.tensor_tensor_scan(r["crow"][0:HEADS, 1:P + 1], r["arow"][0:HEADS, :], r["pb"][0:HEADS, 0:P], init,
                                     op0, op1).then_inc(r["carried"], 1)
                e.wait_ge(r["back"], i + 1)
                ch(e.tensor_copy(r["carry"][:, :], r["pc"][:, 0:HEADS]))
                ch.wait()

            e.wait_ge(r["ld"], 32)
            ch(e.tensor_scalar(r["cont"][:, :], firsts[:, :, 4], -1.0, 1.0, ALU.mult, ALU.add))
            ch(e.tensor_scalar(r["mask"][:, :], firsts[:, :, 4], NEG, None, ALU.mult))
            ch(e.tensor_reduce(r["any"][:, :], firsts[:, :, 4], AX, ALU.max))
            ch.wait()
            ch(e.tensor_scalar(r["through"][:, :], r["any"][:, :].to_broadcast([P, HEADS]), -1.0, 1.0, ALU.mult, ALU.add))
            ch.wait()
            for rep in range(2):
                for k in range(HEADS):
                    ch(e.tensor_tensor_scan(si[:, k, :], r["cont"][:, :], firsts[:, :, k],
                                            0.0 if rep == 0 else r["carry"][:, k:k + 1], ALU.mult, ALU.add))
                ch.wait()
                if rep == 0:
                    ch(e.tensor_copy(r["ends"][:, 0:HEADS], r["through"][:, :]))
                    ch(e.tensor_copy(r["ends"][:, HEADS:], si[:, :, T - 1]))
                    carry(ALU.mult, ALU.add, 0.0)
            ch(e.memset(r["zeros"][:, :], 0.0))
            ch.wait()
            for rep in range(2):
                ch(e.tensor_tensor_scan(r["keyrow"][:, :], r["zeros"][:, :], firsts[:, :, 5],
                                        0.0 if rep == 0 else r["carry"][:, 0:1], ALU.add, ALU.max))
                ch.wait()
                if rep == 0:
                    ch(e.memset(r["ends"][:, 0:HEADS], 0.0))
                    ch(e.tensor_copy(r["ends"][:, HEADS:], r["keyrow"][:, T - 1:T].to_broadcast([P, HEADS])))
                    carry(ALU.add, ALU.max, 0.0)
            e.tensor_copy(r["carry"][:, 0:1], r["carry"][:, 0:1]).then_inc(r["keys_ok"], 1)
            for k in range(HEADS):
                ch(e.tensor_tensor(r["al"][:, k, :], si[:, k, :], sj[:, :, k], ALU.add))
            ch.wait()
            ch(e.scalar_tensor_tensor(r["al"][:, :, :], r["al"][:, :, :], 0.2, r["al"][:, :, :], ALU.mult, ALU.max))
            ch.wait()
            for rep in range(2):
                for k in range(HEADS):
                    ch(e.tensor_tensor_scan(r["m"][:, k, 1:T + 1], r["mask"][:, :], r["al"][:, k, :],
                                            NEG if rep == 0 else r["carry"][:, k:k + 1], ALU.add, ALU.max))
                ch.wait()
                if rep == 0:
                    ch(e.tensor_scalar(r["ends"][:, 0:HEADS], r["any"][:, :].to_broadcast([P, HEADS]), NEG, None, ALU.mult))
                    ch(e.tensor_copy(r["ends"][:, HEADS:], r["m"][:, :, T]))
                    carry(ALU.add, ALU.max, NEG)
            ch(e.tensor_copy(r["m"][:, :, 0], r["carry"][:, :]))
            ch.wait()
            ch(e.tensor_tensor(d0, r["m"][:, :, 0:T], r["m"][:, :, 1:T + 1], ALU.subtract))
            ch(e.tensor_tensor(d1, r["al"][:, :, :], r["m"][:, :, 1:T + 1], ALU.subtract))
            ch(e.tensor_tensor(r["mm"][:, :], r["m"][:, :, 0], r["m"][:, :, T], ALU.subtract))
            ch.wait()
            ch(e.tensor_scalar(d0, d0, 0.0, None, ALU.min))
            e.tensor_scalar(r["mm"][:, :], r["mm"][:, :], 0.0, None, ALU.min).then_inc(r["diffs"], 1)
            e.wait_ge(r["exps"], 1)
            for k in range(HEADS):
                ch(e.tensor_tensor(d0[:, k, :], d0[:, k, :], r["cont"][:, :], ALU.mult))
            ch(e.tensor_tensor(r["ends"][:, 0:HEADS], r["mm"][:, :], r["through"][:, :], ALU.mult))
            ch.wait()
            for rep in range(2):
                for k in range(HEADS):
                    ch(e.tensor_tensor_scan(r["al"][:, k, :], d0[:, k, :], d1[:, k, :],
                                            0.0 if rep == 0 else r["carry"][:, k:k + 1], ALU.mult, ALU.add))
                ch.wait()
                if rep == 0:
                    ch(e.tensor_copy(r["ends"][:, HEADS:], r["al"][:, :, T - 1]))
                    carry(ALU.mult, ALU.add, 0.0)
            for k in range(HEADS):
                ch(e.tensor_copy(both[:, :, k], r["m"][:, k, 1:T + 1]))
                ins = e.tensor_copy(both[:, :, HEADS + k], r["al"][:, k, :])
                if k < HEADS - 1:
                    ch(ins)
            ins.then_inc(r["both_ok"], 1)

        def scalar(e, ch):
            e.wait_ge(r["diffs"], 1)
            ch(e.activation(d0, d0, ACT.Exp))
            ch(e.activation(d1, d1, ACT.Exp))
            e.activation(r["mm"][:, :], r["mm"][:, :], ACT.Exp).then_inc(r["exps"], 1)
        return dict(sync=sync, tensor=tensor, vector=vector, scalar=scalar)
    phase(kn, "l0g", build, psums=[(n, [P, BANK], F32) for n in ("pa", "pb", "pc")],
               sbufs=[("keyrow", [P, T], F32), ("cont", [P, T], F32), ("mask", [P, T], F32), ("zeros", [P, T], F32),
                      ("any", [P, 1], F32), ("through", [P, HEADS], F32), ("ends", [P, 2 * HEADS], F32),
                      ("arow", [HEADS, P], F32), ("crow", [HEADS, P + 1], F32), ("carry", [P, HEADS], F32),
                      ("mm", [P, HEADS], F32), ("al", [P, HEADS, T], F32), ("m", [P, HEADS, T + 1], F32)],
               sems=["ld", "st", "keys_ok", "both_ok", "ends_ok", "rows_ok", "carried", "back", "diffs", "exps"])

def l0_table(kn):
    kn.by_src = dram(kn, "l0_by_src", (NP, T1W))
    rows = T // 7

    def build(r):
        def sync(e, ch):
            e.dma_start(r["kr"][:, :, :], kn.src_sorted.rearrange("(k t p) -> t k p", p=P, k=7)).then_inc(r["kld"], 16)
            tab = kn.by_src.rearrange("(b p) c -> p b c", p=P)
            e.dma_start(tab[:, :, 0:H], kn.TB[:, :, :]).then_inc(r["st"], 16)
            e.wait_ge(r["small_ok"], 1)
            e.dma_start(tab[:, :, H:T1W], r["small"][:, :, :]).then_inc(r["st"], 16)
            e.wait_ge(r["st"], 32)

        def tensor(e, ch):
            e.wait_ge(r["kld"], 16)
            for k in range(7):
                ins = e.transpose(r["pk"][:, k // 4, (k % 4) * rows:(k % 4 + 1) * rows], r["kr"][:, k, :],
                                  kn.ident[0:rows, 0:rows])
            ins.then_inc(r["turned"], 1)

        def vector(e, ch):
            ch(e.tensor_tensor(r["f"][:, :], kn.start[:, 1, :], kn.count[:, 1, :], ALU.add))
            ch.wait()
            e.tensor_scalar(r["at"][:, :], r["f"][:, :], -1.0, 0.0, ALU.add, ALU.max).then_inc(r["at_ok"], 1)
            e.wait_ge(r["turned"], 1)
            ch(e.tensor_copy(r["key"][:, 0:4 * rows], r["pk"][:, 0, 0:4 * rows]))
            ch(e.tensor_copy(r["key"][:, 4 * rows:], r["pk"][:, 1, 0:3 * rows]))
            ch.wait()

            def pick(st):
                for j in range(G):
                    t = slot_value(kn, e, st, j, 64)
                    col = kn.local[:, 1, bass.ds(st.i * G + j, 1)]
                    ch(e.tensor_tensor(col, r["key"][:, bass.ds(t, 1)], col, ALU.subtract))
            run_steps(e, ch, [(pick, 0)], STEPS)
            e.wait_ge(r["got"], 16 * NB)
            sij = kn.sij[:, :].rearrange("p (b k) -> p b k", k=2 * HEADS)
            ch(e.tensor_copy(r["small"][:, :, 0:HEADS], sij[:, :, 0:HEADS]))
            ch(e.tensor_copy(r["small"][:, :, HEADS:2 * HEADS], r["ml"][:, :, 0:HEADS]))
            ch(e.tensor_scalar(r["l"][:, :, :], r["ml"][:, :, HEADS:], 1e-16, None, ALU.add))
            ch.wait()
            e.reciprocal(r["small"][:, :, 2 * HEADS:], r["l"][:, :, :]).then_inc(r["small_ok"], 1)
            ch(e.memset(kn.AC[:, :, :], 0.0))
            ch.wait()

        def gpsimd(e, ch):
            e.wait_ge(r["at_ok"], 1)
            for b in range(NB):
                e.indirect_dma_start(r["ml"][:, b, :], None, kn.run_ml[:, :],
                                     bass.IndirectOffsetOnAxis(ap=r["at"][:, b:b + 1], axis=0), bounds_check=EP - 1
                                     ).then_inc(r["got"], 16)
            e.wait_ge(r["got"], 16 * NB)
        return dict(sync=sync, tensor=tensor, vector=vector, gpsimd=gpsimd)
    phase(kn, "l0t", build, psums=[("pk", [P, 2, BANK], F32)],
               sbufs=[("kr", [rows, 7, P], F32), ("key", [P, T], F32), ("f", [P, NB], F32), ("at", [P, NB], I32),
                      ("ml", [P, NB, 2 * HEADS], F32), ("l", [P, NB, HEADS], F32), ("small", [P, NB, 3 * HEADS], F32)],
               sems=["kld", "st", "small_ok", "turned", "at_ok", "got"])

def gather_stage(kn, e, r, table, width, used):
    def gather(st):
        wait_step(e, r["idx_ok"], st)
        wait_step(e, used, st, 2)
        take_waits(e, kn.tally)
        for j in range(G):
            e.indirect_dma_start(r["rows"][:, st.par, j, 0:width], None, table[:, :],
                                 bass.IndirectOffsetOnAxis(ap=r["idx"][:, st.par, j:j + 1], axis=0),
                                 bounds_check=NP - 1).then_inc(r["got"][st.par], 16)
    return gather

def idx_stage(kn, e, r, columns, sems, n=G):
    def idx(st):
        wait_free(e, r[sems], st, n)
        e.tensor_copy(r["idx"][:, st.par, :], columns[:, bass.ds(st.i * G, G)]).then_inc(r["idx_ok"], 1)
    return idx

def l0_edges(kn):
    def build(r):
        def gpsimd(e, ch):
            run_steps(e, ch, [(gather_stage(kn, e, r, kn.by_src, T1W, r["msg_ok"]), 0)], STEPS)

        def vector(e, ch):
            idx = idx_stage(kn, e, r, kn.src_of, "got")
            hot = hot_stage(kn, e, r, 0, r["summed"])

            def alpha(st):
                wait_load(e, r["got"], st, G)
                a, rows = r["a"][:, st.par, :, :], r["rows"][:, st.par, :, :]
                sj = kn.slot_sj[:, bass.ds(st.i * G * HEADS, G * HEADS)].rearrange("p (j k) -> p j k", k=HEADS)
                ch.wait()
                ch(e.tensor_tensor(a, rows[:, :, H:H + HEADS], sj, ALU.add))
                ch.wait()
                ch(e.scalar_tensor_tensor(a, a, 0.2, a, ALU.mult, ALU.max))
                ch.wait()
                e.tensor_tensor(a, a, rows[:, :, H + HEADS:H + 2 * HEADS], ALU.subtract).then_inc(r["a_ok"], 1)

            def msg(st):
                wait_step(e, r["exp_ok"], st)
                wait_step(e, r["summed"], st, 2)
                a, rows = r["a"][:, st.par, :, :], r["rows"][:, st.par, :, :]
                ch(e.tensor_tensor(a, a, rows[:, :, H + 2 * HEADS:T1W], ALU.mult))
                ch.wait()
                e.tensor_tensor(r["msg"][:, st.par, :, :].rearrange("p j (k c) -> p j k c", k=HEADS),
                                rows[:, :, 0:H].rearrange("p j (k c) -> p j k c", k=HEADS),
                                a.unsqueeze(3).to_broadcast([P, G, HEADS, H // HEADS]), ALU.mult
                                ).then_inc(r["msg_ok"], 1)
            run_steps(e, ch, [(idx, 0), (hot, 0), (alpha, 1), (msg, 1), (add_stage(kn, e, ch, r, 0), 2)], STEPS)

        def scalar(e, ch):
            def exp(st):
                wait_step(e, r["a_ok"], st)
                e.activation(r["a"][:, st.par, :, :], r["a"][:, st.par, :, :], ACT.Exp).then_inc(r["exp_ok"], 1)
            run_steps(e, ch, [(exp, 0)], STEPS)

        def tensor(e, ch):
            def add(st):
                wait_step(e, r["hot"], st)
                wait_step(e, r["msg_ok"], st)
                wait_step(e, r["added"], st, 2)
                for j in range(G):
                    ins = e.matmul(r["pR"][:, st.par, j, :], r["oh"][:, st.par, j, :], r["msg"][:, st.par, j, :],
                                   start=True, stop=True)
                ins.then_inc(r["summed"], 1)
            run_steps(e, ch, [(add, 0)], STEPS)
        return dict(gpsimd=gpsimd, vector=vector, scalar=scalar, tensor=tensor)
    phase(kn, "l0e", build, psums=[("pR", [P, 2, G, P], F32)],
               sbufs=[("rows", [P, 2, G, T1W], F32), ("oh", [P, 2, G, P], F32), ("msg", [P, 2, G, H], F32),
                      ("a", [P, 2, G, HEADS], F32), ("idx", [P, 2, G], I32)],
               sems=["idx_ok", "hot", "a_ok", "exp_ok", "msg_ok", "summed", "added"], pairs=["got"])

def l0_close(kn):
    def build(r):
        def vector(e, ch):
            ch(e.tensor_scalar(r["none"][:, :], kn.count[:, 0, :], 0.0, None, ALU.is_equal))
            ch.wait()

            def add(st):
                x, xl, acc = (block(kn, t, st.i) for t in (kn.X, kn.TB, kn.AC))
                ch(e.scalar_tensor_tensor(acc, xl, r["none"][:, bass.ds(st.i, 1)], acc, ALU.mult, ALU.add))
                ch.wait()
                ch(e.tensor_tensor(x, x, acc, ALU.add))
            run_steps(e, ch, [(add, 0)], NB)
            ch.wait()
        return dict(vector=vector)
    phase(kn, "l0c", build, sbufs=[("none", [P, NB], F32)])

def log_part(kn, e, ch, out, src, bias=None):
    ch(e.activation(out, src, ACT.Abs, **({} if bias is None else {"bias": bias})))
    ch.wait()
    ch(e.activation(out, out, ACT.Exp, scale=-1.0))
    ch.wait()
    return e.activation(out, out, ACT.Ln, bias=kn.half1[:, 0:1], scale=0.5)

def fetch_stage(kn, e, r, src, name="fetched", buf="hb", used="turned"):
    def fetch(st):
        wait_step(e, r[used], st, 2)
        e.activation(r[buf][:, st.par, :], block(kn, src, st.i), ACT.Copy).then_inc(r[name], 1)
    return fetch

def l1_nodes(kn):
    def build(r):
        def tensor(e, ch):
            def turn(st):
                wait_step(e, r["fetched"], st)
                wait_step(e, r["xa_ok"], st, 2)
                e.transpose(r["pA"][:, st.par, 0:P], r["hb"][:, st.par, :], kn.ident[:, :]).then_inc(r["turned"], 1)

            def lin(st):
                wait_step(e, r["xa_ok"], st)
                wait_step(e, r["xi_ok"], st, 2)
                wait_step(e, r["y_ok"], st, 2)
                e.matmul(r["pB"][:, st.par, 0:P], mat(kn, "Wi"), r["xa"][:, st.par, :], start=True, stop=True)
                e.matmul(r["pC"][:, st.par, 0:P], r["xa"][:, st.par, :], mat(kn, "Wj"), start=True, stop=True
                         ).then_inc(r["lin_ok"], 1)
            run_steps(e, ch, [(turn, 0), (lin, 1)], NB)

        def scalar(e, ch):
            def part_a(st):
                wait_step(e, r["turned"], st)
                wait_step(e, r["xa_ok"], st, 2)
                log_part(kn, e, ch, r["la"][:, st.par, :], r["pA"][:, st.par, 0:P]).then_inc(r["la_ok"], 1)

            def part_b(st):
                wait_step(e, r["lin_ok"], st)
                wait_step(e, r["xi_ok"], st, 2)
                log_part(kn, e, ch, r["lb"][:, st.par, :], r["pB"][:, st.par, 0:P], vec(kn, "bi")).then_inc(r["lb_ok"], 1)

            def part_c(st):
                wait_step(e, r["y_ok"], st)
                wait_step(e, r["xj_ok"], st, 2)
                log_part(kn, e, ch, r["lc"][:, st.par, :], r["y"][:, st.par, :]).then_inc(r["lc_ok"], 1)
            run_steps(e, ch, [(fetch_stage(kn, e, r, kn.Hn), 0), (part_a, 0), (part_b, 1), (part_c, 1)], NB)

        def vector(e, ch):
            def xa(st):
                wait_step(e, r["la_ok"], st)
                wait_step(e, r["lin_ok"], st, 2)
                ch(e.tensor_copy(block(kn, kn.Hn, st.i), r["pA"][:, st.par, 0:P]))
                e.scalar_tensor_tensor(r["xa"][:, st.par, :], r["pA"][:, st.par, 0:P], 0.0, r["la"][:, st.par, :],
                                       ALU.max, ALU.add).then_inc(r["xa_ok"], 1)

            def y(st):
                wait_step(e, r["lin_ok"], st)
                wait_step(e, r["xj_ok"], st, 2)
                e.tensor_tensor(r["y"][:, st.par, :], r["pC"][:, st.par, 0:P], row(kn, "bj"), ALU.add
                                ).then_inc(r["y_ok"], 1)

            def xi(st):
                wait_step(e, r["lb_ok"], st)
                wait_step(e, r["xi_ok"], st, 2)
                ch(e.tensor_scalar(r["t"][:, st.par, :], r["pB"][:, st.par, 0:P], vec(kn, "bi"), 0.0, ALU.add, ALU.max))
                ch.wait()
                e.tensor_tensor(block(kn, kn.AC, st.i), r["t"][:, st.par, :], r["lb"][:, st.par, :], ALU.add
                                ).then_inc(r["xi_ok"], 1)

            def xj(st):
                wait_step(e, r["lc_ok"], st)
                e.scalar_tensor_tensor(block(kn, kn.TB, st.i), r["y"][:, st.par, :], 0.0, r["lc"][:, st.par, :],
                                       ALU.max, ALU.add).then_inc(r["xj_ok"], 1)
            run_steps(e, ch, [(xa, 0), (y, 1), (xi, 1), (xj, 1)], NB)
        return dict(tensor=tensor, scalar=scalar, vector=vector)
    phase(kn, "l1n", build, psums=[(n, [P, 2, BANK], F32) for n in ("pA", "pB", "pC")],
               sbufs=[(n, [P, 2, P], F32) for n in ("hb", "la", "lb", "lc", "xa", "y", "t")],
               sems=["fetched", "turned", "xa_ok", "xi_ok", "xj_ok", "y_ok", "lin_ok", "la_ok", "lb_ok", "lc_ok"])

def load_records(kn, e, r, column, width, used):
    def load(st):
        wait_step(e, used, st, 2)
        for j in range(G):
            t = slot_value(kn, e, st, j, 0)
            e.dma_start(r["rec"][:, st.par, j, 0:width], kn.sorted[bass.ds(t * P, P), column:column + width]
                        ).then_inc(r["ld"][st.par], 16)
    return load

def scatter_stage(kn, e, r):
    def send(st):
        wait_step(e, r["prod_ok"], st)
        wait_step(e, r["idx_ok"], st)
        take_waits(e, kn.tally)
        for j in range(G):
            e.indirect_dma_start(kn.products[:, :],
                                 bass.IndirectOffsetOnAxis(ap=r["idx"][:, st.par, j:j + 1], axis=0),
                                 r["prod"][:, st.par, j, :], None, bounds_check=EP - 1, oob_is_err=False
                                 ).then_inc(r["sent"][st.par], 16)
    return send

def scatter_all(kn, e, ch, r):
    run_steps(e, ch, [(scatter_stage(kn, e, r), 0)], STEPS)
    for j in range(2):
        e.wait_ge(r["sent"][j], 16 * G * (STEPS // 2))

def l1_edges(kn):
    def build(r):
        def sync(e, ch):
            run_steps(e, ch, [(load_records(kn, e, r, C64, A64, r["rec_turned"]), 0)], STEPS)

        def tensor(e, ch):
            turn_hot = turn_hot_stage(kn, e, r)

            def turn_rec(st):
                wait_load(e, r["ld"], st, G)
                wait_step(e, r["dT_ok"], st, 2)
                take_waits(e, kn.tally)
                for j in range(G):
                    ins = e.transpose(r["pD"][0:A64, st.par, j, :], r["rec"][:, st.par, j, :], kn.ident[:, :])
                ins.then_inc(r["rec_turned"], 1)

            def mults(st):
                wait_step(e, r["dT_ok"], st)
                wait_step(e, r["g_ok"], st, 2)
                for j in range(G):
                    ins = e.matmul(r["pG"][:, st.par, j, :], r["dT"][0:A64, st.par, j, :], mat(kn, "Wdesc", A64),
                                   start=True, stop=True)
                ins.then_inc(r["g_done"], 1)
                wait_step(e, r["ohT_ok"], st)
                wait_step(e, r["prod_ok"], st, 2)
                for j in range(G):
                    b = slot_value(kn, e, st, j, 32)
                    ins = e.matmul(r["pX"][:, st.par, j, :], r["ohT"][:, st.par, j, :], block(kn, kn.TB, b),
                                   start=True, stop=True)
                ins.then_inc(r["picked"], 1)
            run_steps(e, ch, [(turn_rec, 0), (turn_hot, 0), (mults, 1)], STEPS)

        def scalar(e, ch):
            def copy_rec(st):
                wait_step(e, r["rec_turned"], st)
                wait_step(e, r["g_done"], st, 2)
                e.activation(r["dT"][0:A64, st.par, :, :], r["pD"][0:A64, st.par, :, :], ACT.Copy).then_inc(r["dT_ok"], 1)

            def copy_g(st):
                wait_step(e, r["g_done"], st)
                wait_step(e, r["prod_ok"], st, 2)
                e.activation(r["g"][:, st.par, :, :], r["pG"][:, st.par, :, :], ACT.Copy).then_inc(r["g_ok"], 1)
            run_steps(e, ch, [(copy_rec, 0), (copy_hot_stage(kn, e, r, r["picked"]), 0), (copy_g, 1)], STEPS)

        def vector(e, ch):
            def prod(st):
                wait_step(e, r["g_ok"], st)
                wait_step(e, r["picked"], st)
                wait_free(e, r["sent"], st, G)
                e.tensor_tensor(r["prod"][:, st.par, :, :], r["g"][:, st.par, :, :], r["pX"][:, st.par, :, :], ALU.mult
                                ).then_inc(r["prod_ok"], 1)
            run_steps(e, ch, [(hot_stage(kn, e, r, 0, r["turned"]), 0), (idx_stage(kn, e, r, kn.place, "sent"), 0),
                              (prod, 1)], STEPS)

        def gpsimd(e, ch):
            scatter_all(kn, e, ch, r)
        return dict(sync=sync, tensor=tensor, scalar=scalar, vector=vector, gpsimd=gpsimd)
    phase(kn, "l1e", build, psums=[(n, [P, 2, G, P], F32) for n in ("pT", "pD", "pG", "pX")],
               sbufs=[("rec", [P, 2, G, A64], F32), ("oh", [P, 2, G, P], F32), ("ohT", [P, 2, G, P], F32),
                      ("dT", [A64, 2, G, P], F32), ("g", [P, 2, G, P], F32), ("prod", [P, 2, G, P], F32),
                      ("idx", [P, 2, G], I32)],
               sems=["hot", "turned", "ohT_ok", "rec_turned", "dT_ok", "g_done", "g_ok", "picked", "prod_ok", "idx_ok"],
               pairs=["ld", "sent"])

def sum_by_src(kn, name):
    def build(r):
        def sync(e, ch):
            def load(st):
                wait_step(e, r["summed"], st, 2)
                for j in range(G):
                    t = slot_value(kn, e, st, j, 64)
                    e.dma_start(r["rows"][:, st.par, j, :], kn.products[bass.ds(t * P, P), :]).then_inc(r["ld"][st.par], 16)
            run_steps(e, ch, [(load, 0)], STEPS)

        def vector(e, ch):
            run_steps(e, ch, [(hot_stage(kn, e, r, 1, r["summed"]), 0), (add_stage(kn, e, ch, r, 1), 1)], STEPS)

        def tensor(e, ch):
            def add(st):
                wait_step(e, r["hot"], st)
                wait_load(e, r["ld"], st, G)
                wait_step(e, r["added"], st, 2)
                for j in range(G):
                    ins = e.matmul(r["pR"][:, st.par, j, :], r["rows"][:, st.par, j, :], r["oh"][:, st.par, j, :],
                                   start=True, stop=True)
                ins.then_inc(r["summed"], 1)
            run_steps(e, ch, [(add, 0)], STEPS)
        return dict(sync=sync, vector=vector, tensor=tensor)
    phase(kn, name, build, psums=[("pR", [P, 2, G, P], F32)],
               sbufs=[("rows", [P, 2, G, P], F32), ("oh", [P, 2, G, P], F32)],
               sems=["hot", "summed", "added"], pairs=["ld"])

def sec(kn, t, st):
    return flat(kn, t)[:, bass.ds(st.i * SEC, SEC)]

def ssp_all(kn, name, dst, src):
    def build(r):
        def scalar(e, ch):
            def part(st):
                wait_step(e, r["done"], st, 2)
                log_part(kn, e, ch, r["l"][:, st.par, :], sec(kn, src, st)).then_inc(r["l_ok"], 1)
            run_steps(e, ch, [(part, 0)], NSEC)

        def vector(e, ch):
            def whole(st):
                wait_step(e, r["l_ok"], st)
                e.scalar_tensor_tensor(sec(kn, dst, st), sec(kn, src, st), 0.0, r["l"][:, st.par, :], ALU.max, ALU.add
                                       ).then_inc(r["done"], 1)
            run_steps(e, ch, [(whole, 0)], NSEC)
            e.wait_ge(r["done"], NSEC)
        return dict(scalar=scalar, vector=vector)
    phase(kn, name, build, sbufs=[("l", [P, 2, SEC], F32)], sems=["l_ok", "done"])

def linear_ssp(kn, name, dst, src, w, b):
    def build(r):
        def tensor(e, ch):
            def lin(st):
                wait_step(e, r["done"], st, 2)
                e.matmul(r["p"][:, st.par, 0:SEC], mat(kn, w), sec(kn, src, st), start=True, stop=True
                         ).then_inc(r["lin_ok"], 1)
            run_steps(e, ch, [(lin, 0)], NSEC)

        def scalar(e, ch):
            def part(st):
                wait_step(e, r["lin_ok"], st)
                wait_step(e, r["done"], st, 2)
                log_part(kn, e, ch, r["l"][:, st.par, :], r["p"][:, st.par, 0:SEC], vec(kn, b)).then_inc(r["l_ok"], 1)
            run_steps(e, ch, [(part, 0)], NSEC)

        def vector(e, ch):
            def whole(st):
                wait_step(e, r["l_ok"], st)
                wait_step(e, r["done"], st, 2)
                ch(e.tensor_scalar(r["t"][:, st.par, :], r["p"][:, st.par, 0:SEC], vec(kn, b), 0.0, ALU.add, ALU.max))
                ch.wait()
                e.tensor_tensor(sec(kn, dst, st), r["t"][:, st.par, :], r["l"][:, st.par, :], ALU.add
                                ).then_inc(r["done"], 1)
            run_steps(e, ch, [(whole, 0)], NSEC)
            e.wait_ge(r["done"], NSEC)
        return dict(tensor=tensor, scalar=scalar, vector=vector)
    phase(kn, name, build, psums=[("p", [P, 2, BANK], F32)], sbufs=[("l", [P, 2, SEC], F32), ("t", [P, 2, SEC], F32)],
               sems=["lin_ok", "l_ok", "done"])

def linear_add(kn, name, dst, src, w, b, scale=None):
    def build(r):
        def tensor(e, ch):
            def lin(st):
                wait_step(e, r["done"], st, 2)
                e.matmul(r["p"][:, st.par, 0:SEC], mat(kn, w), sec(kn, src, st), start=True, stop=True
                         ).then_inc(r["lin_ok"], 1)
            run_steps(e, ch, [(lin, 0)], NSEC)

        def vector(e, ch):
            def add(st):
                d = sec(kn, dst, st)
                if scale is not None:
                    ch(e.tensor_scalar(d, d, vec(kn, scale), None, ALU.mult))
                    ch.wait()
                wait_step(e, r["lin_ok"], st)
                e.scalar_tensor_tensor(d, r["p"][:, st.par, 0:SEC], vec(kn, b), d, ALU.add, ALU.add
                                       ).then_inc(r["done"], 1)
            run_steps(e, ch, [(add, 0)], NSEC)
            e.wait_ge(r["done"], NSEC)
        return dict(tensor=tensor, vector=vector)
    phase(kn, name, build, psums=[("p", [P, 2, BANK], F32)], sems=["lin_ok", "done"])

def residual(kn, name, m, w1, b1, w2, b2):
    ssp_all(kn, name + "y", kn.MT, m)
    linear_ssp(kn, name + "h", kn.TB, kn.MT, w1, b1)
    linear_add(kn, name + "m", m, kn.TB, w2, b2)

def l1_layers(kn):
    for k in range(3):
        residual(kn, f"ri{k}", kn.AC, f"Wri1_{k}", f"bri1_{k}", f"Wri2_{k}", f"bri2_{k}")
    ssp_all(kn, "msg", kn.MT, kn.AC)
    linear_add(kn, "dense", kn.Hn, kn.MT, "Wd", "bd", "u")
    for k in range(2):
        residual(kn, f"ra{k}", kn.Hn, f"Wra1_{k}", f"bra1_{k}", f"Wra2_{k}", f"bra2_{k}")

def add_turned(kn, name, src, also=None):
    def build(r):
        def scalar(e, ch):
            run_steps(e, ch, [(fetch_stage(kn, e, r, src), 0)], NB)

        def tensor(e, ch):
            def turn(st):
                wait_step(e, r["fetched"], st)
                wait_step(e, r["added"], st, 2)
                e.transpose(r["pA"][:, st.par, 0:P], r["hb"][:, st.par, :], kn.ident[:, :]).then_inc(r["turned"], 1)
            run_steps(e, ch, [(turn, 0)], NB)

        def vector(e, ch):
            def add(st):
                x = block(kn, kn.X, st.i)
                if also is not None:
                    ch(e.tensor_tensor(x, x, block(kn, also, st.i), ALU.add))
                    ch.wait()
                wait_step(e, r["turned"], st)
                e.tensor_tensor(x, x, r["pA"][:, st.par, 0:P], ALU.add).then_inc(r["added"], 1)
            run_steps(e, ch, [(add, 0)], NB)
            ch(e.memset(kn.AC[:, :, :], 0.0))
            ch.wait()
            e.wait_ge(r["added"], NB)
        return dict(scalar=scalar, tensor=tensor, vector=vector)
    phase(kn, name, build, psums=[("pA", [P, 2, BANK], F32)], sbufs=[("hb", [P, 2, P], F32)],
               sems=["fetched", "turned", "added"])

def tables(kn, name, w_table, w_rows=None, bias=None, rows=None):
    def build(r):
        def tensor(e, ch):
            def turn(st):
                wait_step(e, r["fetched"], st)
                wait_step(e, r["hT_ok"], st, 2)
                e.transpose(r["pA"][:, st.par, 0:P], r["hb"][:, st.par, :], kn.ident[:, :]).then_inc(r["turned"], 1)

            def lin(st):
                wait_step(e, r["hT_ok"], st)
                wait_step(e, r["tab_ok"], st, 2)
                if w_rows:
                    e.matmul(r["pC"][:, st.par, 0:P], r["hT"][:, st.par, :], mat(kn, w_rows), start=True, stop=True)
                e.matmul(r["pB"][:, st.par, 0:P], r["hT"][:, st.par, :], mat(kn, w_table), start=True, stop=True
                         ).then_inc(r["lin_ok"], 1)
            run_steps(e, ch, [(turn, 0), (lin, 1)], NB)

        def scalar(e, ch):
            def copy(st):
                wait_step(e, r["turned"], st)
                wait_step(e, r["lin_ok"], st, 2)
                e.activation(r["hT"][:, st.par, :], r["pA"][:, st.par, 0:P], ACT.Copy).then_inc(r["hT_ok"], 1)
            run_steps(e, ch, [(fetch_stage(kn, e, r, kn.Hn), 0), (copy, 0)], NB)

        def vector(e, ch):
            def out(st):
                wait_step(e, r["lin_ok"], st)
                if w_rows:
                    wait_free(e, r["st"], st, 1)
                    ch(e.tensor_tensor(r["a"][:, st.par, :], r["pC"][:, st.par, 0:P], row(kn, bias), ALU.add))
                e.tensor_copy(block(kn, kn.TB, st.i), r["pB"][:, st.par, 0:P]).then_inc(r["tab_ok"], 1)
            run_steps(e, ch, [(out, 0)], NB)
            e.wait_ge(r["tab_ok"], NB)

        def sync(e, ch):
            def store(st):
                wait_step(e, r["tab_ok"], st)
                e.dma_start(rows[bass.ds(st.i * P, P), :], r["a"][:, st.par, :]).then_inc(r["st"][st.par], 16)
            run_steps(e, ch, [(store, 0)], NB)
            e.wait_ge(r["st"][0], 16 * (NB - NB // 2))
            e.wait_ge(r["st"][1], 16 * (NB // 2))
        d = dict(tensor=tensor, scalar=scalar, vector=vector)
        if w_rows:
            d["sync"] = sync
        return d
    phase(kn, name, build, psums=[(n, [P, 2, BANK], F32) for n in ("pA", "pB", "pC")],
               sbufs=[(n, [P, 2, P], F32) for n in ("hb", "hT", "a")],
               sems=["fetched", "turned", "hT_ok", "lin_ok", "tab_ok"], pairs=["st"])

def l2_edges(kn):
    def build(r):
        def gpsimd(e, ch):
            run_steps(e, ch, [(gather_stage(kn, e, r, kn.l2_rows, H, r["v_ok"]), 0)], STEPS)

        def tensor(e, ch):
            def v(st):
                wait_load(e, r["got"], st, G)
                wait_step(e, r["normed"], st, 2)
                e.matmul(r["pV"][:, st.par, :, :].rearrange("p j c -> p (j c)"), kn.ident[:, :],
                         r["rows"][:, st.par, :, :].rearrange("p j c -> p (j c)"), start=True, stop=False,
                         skip_group_check=True)
                wait_step(e, r["ohT_ok"], st)
                for j in range(G):
                    b = slot_value(kn, e, st, j, 32)
                    ins = e.matmul(r["pV"][:, st.par, j, :], r["ohT"][:, st.par, j, :], block(kn, kn.TB, b),
                                   start=False, stop=(j == G - 1), skip_group_check=True)
                ins.then_inc(r["v_ok"], 1)

            def add(st):
                wait_step(e, r["z_ok"], st)
                wait_step(e, r["added"], st, 2)
                for j in range(G):
                    ins = e.matmul(r["pR"][:, st.par, j, :], r["oh"][:, st.par, j, :], r["z"][:, st.par, j, :],
                                   start=True, stop=True)
                ins.then_inc(r["summed"], 1)
            run_steps(e, ch, [(turn_hot_stage(kn, e, r), 0), (v, 0), (add, 1)], STEPS)

        def scalar(e, ch):
            def root(st):
                wait_step(e, r["stats"], st)
                e.activation(r["std"][:, st.par, :], r["mv"][:, st.par, :, 1], ACT.Sqrt, bias=kn.eps1[:, 0:1]
                             ).then_inc(r["std_ok"], 1)

            def norm(st):
                wait_step(e, r["scales"], st)
                wait_step(e, r["summed"], st, 2)
                for j in range(G):
                    ins = e.activation(r["z"][:, st.par, j, :], r["pV"][:, st.par, j, :], ACT.Identity,
                                       bias=r["shift"][:, st.par, j:j + 1], scale=r["rstd"][:, st.par, j:j + 1])
                ins.then_inc(r["normed"], 1)
            run_steps(e, ch, [(copy_hot_stage(kn, e, r, r["v_ok"]), 0), (root, 0), (norm, 0)], STEPS)

        def vector(e, ch):
            def stats(st):
                wait_step(e, r["v_ok"], st)
                wait_step(e, r["std_ok"], st, 2)
                ch.wait()
                for j in range(G):
                    ch(e.bn_stats(r["six"][:, st.par, j, :], r["pV"][:, st.par, j, :]))
                ch.wait()
                take_waits(e, kn.tally)
                for j in range(G):
                    ins = e.bn_aggr(r["mv"][:, st.par, j, :], r["six"][:, st.par, j, :])
                    if j < G - 1:
                        ch(ins)
                ins.then_inc(r["stats"], 1)

            def scales(st):
                wait_step(e, r["std_ok"], st)
                wait_step(e, r["normed"], st, 2)
                ch(e.reciprocal(r["rstd"][:, st.par, :], r["std"][:, st.par, :]))
                ch.wait()
                e.scalar_tensor_tensor(r["shift"][:, st.par, :], r["mv"][:, st.par, :, 0], -1.0, r["rstd"][:, st.par, :],
                                       ALU.mult, ALU.mult).then_inc(r["scales"], 1)

            def act(st):
                wait_step(e, r["normed"], st)
                z = r["z"][:, st.par, :, :]
                ch(e.tensor_tensor(z, z, row(kn, "msg_g").unsqueeze(1).to_broadcast([P, G, H]), ALU.mult))
                ch.wait()
                ch(e.tensor_tensor(z, z, row(kn, "msg_beta").unsqueeze(1).to_broadcast([P, G, H]), ALU.add))
                ch.wait()
                for j in range(G):
                    ins = e.tensor_scalar(r["z"][:, st.par, j, :], r["z"][:, st.par, j, :], 0.0,
                                          kn.wt[:, bass.ds(st.i * G + j, 1)], ALU.max, ALU.mult)
                ins.then_inc(r["z_ok"], 1)
            run_steps(e, ch, [(idx_stage(kn, e, r, kn.src_of, "got"), 0), (hot_stage(kn, e, r, 0, r["summed"]), 0),
                              (stats, 1), (scales, 1), (act, 1), (add_stage(kn, e, ch, r, 0), 2)], STEPS)
        return dict(gpsimd=gpsimd, tensor=tensor, scalar=scalar, vector=vector)
    phase(kn, "l2e", build, psums=[(n, [P, 2, G, P], F32) for n in ("pT", "pV", "pR")],
               sbufs=[("rows", [P, 2, G, H], F32), ("oh", [P, 2, G, P], F32), ("ohT", [P, 2, G, P], F32),
                      ("z", [P, 2, G, H], F32), ("six", [P, 2, G, 6], F32), ("mv", [P, 2, G, 2], F32),
                      ("std", [P, 2, G], F32), ("rstd", [P, 2, G], F32), ("shift", [P, 2, G], F32), ("idx", [P, 2, G], I32)],
               sems=["idx_ok", "hot", "turned", "ohT_ok", "v_ok", "stats", "std_ok", "scales", "normed", "z_ok",
                     "summed", "added"], pairs=["got"])

def l2_update(kn):
    def build(r):
        def vector(e, ch):
            ch(e.tensor_scalar(r["f"][:, :], kn.count[:, 0, :], 1e-8, None, ALU.add))
            ch(e.tensor_scalar(r["valid"][:, :], kn.count[:, 0, :], 0.0, None, ALU.is_gt))
            ch.wait()
            ch(e.reciprocal(r["f"][:, :], r["f"][:, :]))
            ch.wait()
            ch(e.tensor_tensor(r["f"][:, :], r["f"][:, :], r["valid"][:, :], ALU.mult))
            ch.wait()

            def mean(st):
                wait_step(e, r["turned"], st, 2)
                e.tensor_scalar(r["mb"][:, st.par, :], block(kn, kn.AC, st.i), r["f"][:, bass.ds(st.i, 1)], None,
                                ALU.mult).then_inc(r["mean_ok"], 1)

            def out(st):
                wait_step(e, r["lin_ok"], st)
                e.tensor_tensor(block(kn, kn.TB, st.i), r["pC"][:, st.par, 0:P], row(kn, "upd_b"), ALU.add
                                ).then_inc(r["out_ok"], 1)
            run_steps(e, ch, [(mean, 0), (out, 1)], NB)
            e.wait_ge(r["out_ok"], NB)

        def tensor(e, ch):
            def turn(st):
                wait_step(e, r["fetched"], st)
                wait_step(e, r["mean_ok"], st)
                wait_step(e, r["T_ok"], st, 2)
                e.transpose(r["pA"][:, st.par, 0:P], r["hb"][:, st.par, :], kn.ident[:, :])
                e.transpose(r["pA"][:, st.par, P:2 * P], r["mb"][:, st.par, :], kn.ident[:, :]).then_inc(r["turned"], 1)

            def lin(st):
                wait_step(e, r["T_ok"], st)
                wait_step(e, r["out_ok"], st, 2)
                e.matmul(r["pC"][:, st.par, 0:P], r["T"][:, st.par, 0:P], mat(kn, "upd_top"), start=True, stop=False)
                e.matmul(r["pC"][:, st.par, 0:P], r["T"][:, st.par, P:2 * P], mat(kn, "upd_bottom"), start=False,
                         stop=True).then_inc(r["lin_ok"], 1)
            run_steps(e, ch, [(turn, 0), (lin, 1)], NB)

        def scalar(e, ch):
            def copy(st):
                wait_step(e, r["turned"], st)
                wait_step(e, r["lin_ok"], st, 2)
                e.activation(r["T"][:, st.par, :], r["pA"][:, st.par, 0:2 * P], ACT.Copy).then_inc(r["T_ok"], 1)
            run_steps(e, ch, [(fetch_stage(kn, e, r, kn.Hn), 0), (copy, 0)], NB)
        return dict(vector=vector, tensor=tensor, scalar=scalar)
    phase(kn, "l2u", build, psums=[(n, [P, 2, BANK], F32) for n in ("pA", "pC")],
               sbufs=[("hb", [P, 2, P], F32), ("mb", [P, 2, P], F32), ("T", [P, 2, 2 * P], F32), ("f", [P, NB], F32),
                      ("valid", [P, NB], F32)],
               sems=["fetched", "mean_ok", "turned", "T_ok", "lin_ok", "out_ok"])

def l2_close(kn):
    X, Hn, MT, AC = (t[:, :, :] for t in (kn.X, kn.Hn, kn.MT, kn.AC))

    def over(name):
        return row(kn, name).unsqueeze(1).to_broadcast([P, NB, H])

    def build(r):
        def vector(e, ch):
            ch(e.tensor_tensor(AC, Hn, over("gate_w"), ALU.mult))
            ch(e.tensor_tensor(MT, MT, over("upd_g"), ALU.mult))
            ch(e.tensor_tensor(X, X, Hn, ALU.add))
            ch.wait()
            ch(e.tensor_reduce(r["z"][:, :], AC, AX, ALU.add))
            ch(e.tensor_tensor(MT, MT, over("upd_beta"), ALU.add))
            ch.wait()
            e.tensor_scalar(r["z"][:, :], r["z"][:, :], row(kn, "gate_b")[:, 0:1], None, ALU.add).then_inc(r["z_ok"], 1)
            ch(e.scalar_tensor_tensor(MT, MT, 0.0, Hn, ALU.max, ALU.subtract))
            e.wait_ge(r["exp_ok"], 1)
            ch(e.tensor_scalar(r["z"][:, :], r["z"][:, :], 1.0, None, ALU.add))
            ch.wait()
            ch(e.reciprocal(r["g"][:, :], r["z"][:, :]))
            ch.wait()
            ch(e.tensor_tensor(MT, MT, r["g"][:, :].unsqueeze(2).to_broadcast([P, NB, H]), ALU.mult))
            ch(e.memset(AC, 0.0))
            ch.wait()
            ch(e.tensor_tensor(X, X, MT, ALU.add))
            ch.wait()

        def scalar(e, ch):
            e.wait_ge(r["z_ok"], 1)
            e.activation(r["z"][:, :], r["z"][:, :], ACT.Exp, scale=-1.0).then_inc(r["exp_ok"], 1)
        return dict(vector=vector, scalar=scalar)
    phase(kn, "l2c", build, sbufs=[("z", [P, NB], F32), ("g", [P, NB], F32)], sems=["z_ok", "exp_ok"])

def l3_edges(kn):
    def build(r):
        def sync(e, ch):
            run_steps(e, ch, [(load_records(kn, e, r, 0, A50, r["rec_turned"]), 0)], STEPS)

        def tensor(e, ch):
            turn_hot = turn_hot_stage(kn, e, r, 1)

            def turn_rec(st):
                wait_load(e, r["ld"], st, G)
                wait_step(e, r["dT_ok"], st, 1)
                take_waits(e, kn.tally)
                for j in range(G):
                    ins = e.transpose(r["pD"][0:A50, j, :], r["rec"][:, st.par, j, :], kn.ident[:, :])
                ins.then_inc(r["rec_turned"], 1)

            def hidden(st):
                wait_step(e, r["dT_ok"], st)
                wait_step(e, r["s_ok"], st, 2)
                e.matmul(r["pH"][:, st.par, :], mat(kn, "mlp_w1", A50),
                         r["dT"][0:A50, st.par, :, :].rearrange("p j c -> p (j c)"), start=True, stop=True
                         ).then_inc(r["h_done"], 1)

            def mults(st):
                wait_step(e, r["ohT_ok"], st)
                wait_step(e, r["prod_ok"], st, 2)
                for j in range(G):
                    b = slot_value(kn, e, st, j, 32)
                    e.matmul(r["pX"][:, st.par, j, :], r["ohT"][:, st.par, j, :], block(kn, kn.TB, b),
                             start=True, stop=True)
                wait_step(e, r["s_ok"], st)
                wait_step(e, r["w_ok"], st, 2)
                for j in range(G):
                    ins = e.matmul(r["pW"][:, st.par, j, :], r["s"][:, st.par, j * P:(j + 1) * P], mat(kn, "mlp_w2"),
                                   start=True, stop=True)
                ins.then_inc(r["w_done"], 1)
            run_steps(e, ch, [(turn_rec, 0), (turn_hot, 0), (hidden, 0), (mults, 1)], STEPS)

        def scalar(e, ch):
            def copy_rec(st):
                wait_step(e, r["rec_turned"], st)
                wait_step(e, r["h_done"], st, 2)
                e.activation(r["dT"][0:A50, st.par, :, :], r["pD"][0:A50, :, :], ACT.Copy).then_inc(r["dT_ok"], 1)

            def part(st):
                wait_step(e, r["h_done"], st)
                wait_step(e, r["s_ok"], st, 2)
                log_part(kn, e, ch, r["l"][:, st.par, :], r["pH"][:, st.par, :], vec(kn, "mlp_b1")).then_inc(r["l_ok"], 1)
            run_steps(e, ch, [(copy_rec, 0), (copy_hot_stage(kn, e, r, r["w_done"], 1), 0), (part, 0)], STEPS)

        def vector(e, ch):
            def hid(st):
                wait_step(e, r["l_ok"], st)
                wait_step(e, r["w_done"], st, 2)
                ch(e.tensor_scalar(r["s"][:, st.par, :], r["pH"][:, st.par, :], vec(kn, "mlp_b1"), 0.0, ALU.add, ALU.max))
                ch.wait()
                e.tensor_tensor(r["s"][:, st.par, :], r["s"][:, st.par, :], r["l"][:, st.par, :], ALU.add
                                ).then_inc(r["s_ok"], 1)

            def prod(st):
                wait_step(e, r["w_done"], st)
                wait_free(e, r["sent"], st, G)
                e.tensor_tensor(r["prod"][:, st.par, :, :], r["pW"][:, st.par, :, :],
                                row(kn, "mlp_b2").unsqueeze(1).to_broadcast([P, G, H]), ALU.add).then_inc(r["w_ok"], 1)
                wait_step(e, r["w_ok"], st)
                for j in range(G):
                    out = r["prod"][:, st.par, j, :]
                    ins = e.scalar_tensor_tensor(out, r["pX"][:, st.par, j, :], kn.cut[:, bass.ds(st.i * G + j, 1)], out,
                                                 ALU.mult, ALU.mult)
                ins.then_inc(r["prod_ok"], 1)
            run_steps(e, ch, [(hot_stage(kn, e, r, 0, r["turned"]), 0), (idx_stage(kn, e, r, kn.place, "sent"), 0),
                              (hid, 0), (prod, 1)], STEPS)

        def gpsimd(e, ch):
            scatter_all(kn, e, ch, r)
        return dict(sync=sync, tensor=tensor, scalar=scalar, vector=vector, gpsimd=gpsimd)
    phase(kn, "l3e", build, psums=[("pT", [P, 1, G, P], F32), ("pD", [P, G, P], F32), ("pH", [P, 2, BANK], F32),
                                    ("pW", [P, 2, G, P], F32), ("pX", [P, 2, G, P], F32)],
               sbufs=[("rec", [P, 2, G, A50], F32), ("oh", [P, 2, G, P], F32), ("ohT", [P, 2, G, P], F32),
                      ("dT", [A50, 2, G, P], F32), ("l", [P, 2, G * P], F32), ("s", [P, 2, G * P], F32),
                      ("prod", [P, 2, G, P], F32), ("idx", [P, 2, G], I32)],
               sems=["hot", "turned", "ohT_ok", "rec_turned", "dT_ok", "h_done", "l_ok", "s_ok", "w_done", "w_ok",
                     "prod_ok", "idx_ok"], pairs=["ld", "sent"])

def store(kn):
    def build(r):
        def sync(e, ch):
            full = (N // P) * P
            e.dma_start(kn.out[0:full, :].rearrange("(b p) h -> p b h", p=P), kn.X[:, 0:N // P, :]).then_inc(r["st"], 16)
            e.dma_start(kn.out[full:N, :], kn.X[0:N - full, N // P, :]).then_inc(r["st"], 16)
            e.wait_ge(r["st"], 32)
        return dict(sync=sync)
    phase(kn, "store", build, sems=["st"])


def layout(inp):
    import numpy as np
    f = {k: np.asarray(v) for k, v in inp.items()}
    a = {}
    a["x"] = f["x"]
    rec = np.zeros((EP, NREC), np.float32)
    rec[:E, 0:A50] = f["edge_attr_50"]
    rec[:E, C64:C64 + A64] = f["edge_attr_64"]
    rec[:E, CM:CM + A3] = f["edge_attr_3"]
    rec[:E, CM + A3] = f["edge_weight"]
    a["rec"] = rec
    for n in ("src", "dst"):
        lin = np.full((EP,), PAD_KEY, np.int32)
        lin[:E] = f[n]
        a[n + "_lin"] = lin
        a[n + "_tiles"] = np.ascontiguousarray(lin.reshape(T, P).T)
    t = lambda n: f[n].T
    m = {"W_lin": f["L0_gnn_W_lin"], "Wi": t("L1_gnn_Wi"), "Wj": t("L1_gnn_Wj"), "Wd": t("L1_gnn_Wd"),
         "msg_top": f["L2_gnn_msg_w"][:H], "msg_bottom": f["L2_gnn_msg_w"][H:], "upd_top": f["L2_gnn_upd_w"][:H],
         "upd_bottom": f["L2_gnn_upd_w"][H:], "lin1": t("L3_gnn_lin1_w"), "lin2": t("L3_gnn_lin2_w"),
         "mlp_w2": t("L3_gnn_mlp_w2"), "mlp_w1": t("L3_gnn_mlp_w1"), "Wdesc": t("L1_gnn_Wdesc")}
    v = {"bi": f["L1_gnn_bi"], "bd": f["L1_gnn_bd"], "u": f["L1_gnn_u"], "mlp_b1": f["L3_gnn_mlp_b1"],
         "lin2_b": f["L3_gnn_lin2_b"]}
    for k, n in (("ri1", 3), ("ri2", 3), ("ra1", 2), ("ra2", 2)):
        for i in range(n):
            m[f"W{k}_{i}"] = f["L1_gnn_W" + k][i].T
            v[f"b{k}_{i}"] = f["L1_gnn_b" + k][i]
    att = f["L0_gnn_W_att"]
    m["W_att"] = np.concatenate([att[:H], att[H:]], axis=1)
    a["mats"] = np.zeros((P, len(MATS), H), np.float32)
    for i, n in enumerate(MATS):
        a["mats"][:m[n].shape[0], i, :m[n].shape[1]] = m[n]
    a["vecs"] = np.ascontiguousarray(np.stack([v[n] for n in VECS], axis=1))
    w = {"b_lin": f["L0_gnn_b_lin"], "bj": f["L1_gnn_bj"], "mlp_b2": f["L3_gnn_mlp_b2"], "b_att": f["L0_gnn_b_att"],
         "gate_w": f["L2_gnn_gate_w"][:, 0], "gate_b": f["L2_gnn_gate_b"]}
    for n in ("msg_b", "msg_g", "msg_beta", "upd_b", "upd_g", "upd_beta"):
        w[n] = f["L2_gnn_" + n]
    a["rows"] = np.zeros((1, len(ROWS) * H), np.float32)
    for i, n in enumerate(ROWS):
        a["rows"][0, i * H:i * H + w[n].size] = w[n]
    return a


def build_program(nc, ins, out, upto="all", dump=None):
    kn = Buffers()
    kn.nc, kn.ins, kn.out = nc, ins, out
    kn.tally = nc.alloc_semaphore("tally")
    with ExitStack() as ctx:
        setup(kn, ctx)
        constants(kn)
        with ExitStack() as keys_ctx:
            kn.keys_ctx = keys_ctx
            split_keys(kn)
            histogram(kn)
            if upto == "hist":
                dump(kn, "count", kn.count[:, :, :]); return

            offsets(kn)
            if upto == "off":
                dump(kn, "start", kn.start[:, :, :]); dump(kn, "slot", kn.slot_reg[:, :]); return
            sort(kn)
            if upto == "sort":
                dump(kn, "srt", kn.sorted); return
        node_buffers(kn, ctx)
        slot_columns(kn)
        with ExitStack() as l0:
            kn.sij = l0.enter_context(nc.sbuf_tensor("sij", [P, NB * 2 * HEADS], F32))
            layernorm(kn, "ln0")
            l0_nodes(kn)
            l0_scores(kn)
            if upto == "l0s":
                dump(kn, "h", kn.Hn[:, :, :]); dump(kn, "xl", kn.TB[:, :, :]); dump(kn, "sij", kn.sij[:, :]); dump(kn, "sj_src", kn.sj_src)
                dump(kn, "firsts", kn.firsts); dump(kn, "cut", kn.cut[:, :]); dump(kn, "place", kn.place[:, :]); return
            l0_segments(kn)
            l0_table(kn)
            if upto == "l0t":
                dump(kn, "by_src", kn.by_src); dump(kn, "keys", kn.src_sorted); return
            l0_edges(kn)
        l0_close(kn)
        if upto == "l0":
            dump(kn, "ac0", kn.AC[:, :, :]); dump(kn, "x1", kn.X[:, :, :]); return
        kn.products = dram(kn, "products", (EP, H))
        layernorm(kn, "ln1")
        l1_nodes(kn)
        if upto == "l1n":
            dump(kn, "xj", kn.TB[:, :, :]); dump(kn, "xi", kn.AC[:, :, :]); return
        l1_edges(kn)
        sum_by_src(kn, "l1r")
        if upto == "l1r":
            dump(kn, "ac1", kn.AC[:, :, :]); return
        l1_layers(kn)
        add_turned(kn, "l1c", kn.Hn)
        if upto == "l1":
            dump(kn, "x2", kn.X[:, :, :]); return
        layernorm(kn, "ln2")
        kn.l2_rows = dram(kn, "l2_rows", (NP, H))
        tables(kn, "l2t", "msg_bottom", "msg_top", "msg_b", kn.l2_rows)
        l2_edges(kn)
        if upto == "l2e":
            dump(kn, "ac2", kn.AC[:, :, :]); return
        l2_update(kn)
        layernorm(kn, "ln2b", kn.TB, kn.MT, ACT.Identity)
        l2_close(kn)
        if upto == "l2":
            dump(kn, "x3", kn.X[:, :, :]); return
        layernorm(kn, "ln3")
        tables(kn, "l3t", "lin1")
        l3_edges(kn)
        sum_by_src(kn, "l3r")
        if upto == "l3r":
            dump(kn, "ac3", kn.AC[:, :, :]); return
        linear_ssp(kn, "l3o", kn.MT, kn.AC, "lin2", "lin2_b")
        add_turned(kn, "l3c", kn.MT, kn.Hn)
        store(kn)


_ORDER = ["x", "rec", "src_lin", "dst_lin", "src_tiles", "dst_tiles", "mats", "vecs", "rows"]


def kernel(**inputs):
    import numpy as _np
    import concourse.bacc as _bacc
    from concourse import mybir as _mybir
    from concourse.bass_utils import run_bass_kernel_spmd as _run

    nc = _bacc.Bacc("TRN2", target_bir_lowering=False, num_devices=1)
    arrays = layout(inputs)
    args = {n: nc.dram_tensor(n, arrays[n].shape, _mybir.dt.from_np(arrays[n].dtype), kind="ExternalInput").ap()
            for n in _ORDER}
    out = nc.dram_tensor("out", (N, H), F32, kind="ExternalOutput").ap()
    build_program(nc, args, out)
    r = _run(nc, [arrays], core_ids=[0])
    return r.results[0]["out"]
```

```python
from contextlib import ExitStack

import concourse.bass as bass
from concourse import mybir

ALU = mybir.AluOpType
ACT = mybir.ActivationFunctionType
F32 = mybir.dt.float32
BF16 = mybir.dt.bfloat16
I32 = mybir.dt.int32
AX = mybir.AxisListType.X

P = 128
N = 6250
E = 100000
NB = -(-N // P)
NP = NB * P
GT = 8
T = 784
EP = T * P
PAD_KEY = NP - 1
SLOTS = T + NB - 1
G = 4
STEPS = SLOTS // G
H = 128
HEADS = 4
A50, A64, A3 = 50, 64, 3
C64 = A50
CM = A50 + A64
NREC = CM + A3 + 1
W_DST, W_SRC, W_POS = NREC, NREC + 1, NREC + 2
RING = 8
QUAD = 4
META = 8
BIG = 131072.0
NEG = -1.0e30
EPS = 1e-5
SEC = 448
NSEC = NP // SEC
T1W = H + 3 * HEADS
MATS = ["W_lin", "Wi", "Wj", "Wri1_0", "Wri1_1", "Wri1_2", "Wri2_0", "Wri2_1", "Wri2_2", "Wd", "Wra1_0", "Wra1_1",
        "Wra2_0", "Wra2_1", "msg_top", "msg_bottom", "upd_top", "upd_bottom", "lin1", "lin2", "mlp_w2", "mlp_w1",
        "Wdesc", "W_att"]
VECS = ["bi", "bri1_0", "bri1_1", "bri1_2", "bri2_0", "bri2_1", "bri2_2", "bd", "u", "bra1_0", "bra1_1", "bra2_0",
        "bra2_1", "mlp_b1", "lin2_b"]
ROWS = ["b_lin", "bj", "msg_b", "msg_g", "msg_beta", "upd_b", "upd_g", "upd_beta", "gate_w", "mlp_b2", "b_att", "gate_b"]
BANK = 512
assert SLOTS % (2 * G) == 0 and T % GT == 0 and NP % SEC == 0 and EP < BIG


class Step:

    def __init__(self, i, half, par, fourth, quad, ring):
        self.i, self.half, self.par, self.fourth, self.quad, self.ring = i, half, par, fourth, quad, ring


class Chain:

    def __init__(self, eng, sem):
        self.eng, self.sem = eng, sem
        self.done, self.loop, self.per = 0, None, 0

    def __call__(self, ins):
        ins.then_inc(self.sem, 1)
        self.done += 1
        return ins

    def wait(self, back=0):
        n = self.done - back
        if n <= 0:
            return
        self.eng.wait_ge(self.sem, n if self.loop is None else self.loop * self.per + n)


def run_steps(eng, chain, stages, n, unroll=2):
    lag = max(t[1] for t in stages)
    first = max(lag + 2, 2)
    while (n - first) % unroll:
        first += 1

    def one(r, k=None):
        for t in stages:
            c, size = r - t[1], (t[2] if len(t) > 2 else 1)
            if c % size or (k is None and not 0 <= c < n):
                continue
            steps = []
            for i in range(c, c + size):
                if k is None:
                    steps.append(Step(i, i // 2, i % 2, i // 4, i % 4, i % RING))
                else:
                    steps.append(Step(unroll * k + i, (unroll // 2) * k + i // 2, i % 2, (unroll // 4) * k + i // 4,
                                      i % 4, i % RING))
            t[0](steps if len(t) > 2 else steps[0])

    if n < first + 2 * unroll:
        for r in range(n + lag):
            one(r)
        return
    for r in range(first):
        one(r)
    rounds = (n - first) // unroll
    for u in range(unroll):
        before = chain.done
        one(first + u)
        chain.per = chain.per + chain.done - before if u else chain.done - before
    first += unroll
    with eng.Fori(0, rounds - 1) as k:
        chain.loop = k
        start = chain.done
        for u in range(unroll):
            one(first + u, k)
        assert chain.done - start == chain.per
    chain.loop = None
    chain.done = start + chain.per * (rounds - 1)
    for r in range(n, n + lag):
        one(r)


def wait_step(eng, sem, st, back=0):
    v = st.i + (1 - back)
    if isinstance(v, int) and v <= 0:
        return
    eng.wait_ge(sem, v)


def take_waits(eng, tally):
    eng.sem_inc(tally, 1)


def wait_load(eng, sems, st, n):
    eng.wait_ge(sems[st.par], st.half * (16 * n) + 16 * n)


def wait_free(eng, sems, st, n):
    if isinstance(st.half, int) and st.half == 0:
        return
    eng.wait_ge(sems[st.par], st.half * (16 * n))


class Buffers:
    pass


def dram(kn, name, shape, dt=F32):
    return kn.nc.dram_tensor(name, shape, dt, kind="Internal").ap()

def phase(kn, name, build, psums=(), sbufs=(), sems=(), pairs=()):
    nc = kn.nc
    with ExitStack() as ctx:
        res, used = {}, []
        for n, shape, dt in psums:
            res[n] = ctx.enter_context(nc.psum_tensor(f"{name}_{n}", shape, dt))
        for n, shape, dt in sbufs:
            res[n] = ctx.enter_context(nc.sbuf_tensor(f"{name}_{n}", shape, dt))
        for n in sems:
            res[n] = nc.alloc_semaphore(f"{name}_{n}")
            used.append(res[n])
        for n in pairs:
            res[n] = [nc.alloc_semaphore(f"{name}_{n}{j}") for j in range(2)]
            used += res[n]
        bodies = build(res)
        own = {n: nc.alloc_semaphore(f"{name}_{n}_own") for n in bodies}
        used += list(own.values())
        with nc.Block() as block:
            for eng_name, body in bodies.items():
                def run(eng, body=body, sem=own[eng_name]):
                    body(eng, Chain(eng, sem))

                {"sync": block.sync, "tensor": block.tensor, "vector": block.vector,
                 "scalar": block.scalar, "gpsimd": block.gpsimd}[eng_name](run)
        nc.clear_and_free_semaphores(used)
        nc.all_engine_barrier()

def setup(kn, ctx):
    nc = kn.nc

    def sb(name, shape, dt=F32):
        return ctx.enter_context(nc.sbuf_tensor(name, shape, dt))

    kn.X = sb("x_nodes", [P, NB, H])
    kn.ident = sb("ident", [P, P])
    kn.identb = sb("identb", [P, P], BF16)
    kn.ones = sb("ones", [P, P])
    kn.before = sb("before", [P, P])
    kn.beforeb = sb("beforeb", [P, P], BF16)
    kn.iota = sb("iota", [P, P])
    kn.iotab = sb("iotab", [P, P], BF16)
    kn.pcol = sb("pcol", [P, 1])
    kn.zero1 = sb("zero1", [P, 1])
    kn.half1 = sb("half1", [P, 1])
    kn.eps1 = sb("eps1", [P, 1])
    kn.hp1 = sb("half_pi", [P, 1])
    kn.start = sb("start", [P, 2, NB])
    kn.count = sb("count", [P, 2, NB])
    kn.slot_reg = sb("slot_reg", [P, SLOTS], I32)
    kn.local = sb("local", [P, 2, SLOTS])

def node_buffers(kn, ctx):
    def sb(name, shape, dt=F32):
        return ctx.enter_context(kn.nc.sbuf_tensor(name, shape, dt))

    kn.place = sb("k_place", [P, SLOTS], I32)
    kn.src_of = sb("k_src_of", [P, SLOTS], I32)
    kn.wt = sb("k_wt", [P, SLOTS])
    kn.cut = sb("k_cut", [P, SLOTS])
    kn.W = sb("k_weights", [P, len(MATS), H])
    kn.V = sb("k_vectors", [P, len(VECS)])
    kn.R = sb("k_rows", [P, len(ROWS), H])
    kn.Hn = sb("h_nodes", [P, NB, H])
    kn.AC = sb("acc", [P, NB, H])
    kn.TB = sb("table", [P, NB, H])
    kn.MT = sb("spare", [P, NB, H])

def flat(kn, t):
    return t[:, :, :].rearrange("p b h -> p (b h)")

def constants(kn):
    ins = kn.ins

    def build(r):
        def gpsimd(e, ch):
            ch(e.iota(r["ii"][:, :], [[1, P]], base=0, channel_multiplier=0))
            ch(e.iota(r["ip"][:, :], [[0, 1]], base=0, channel_multiplier=1))
            ch.wait()
            ch(e.tensor_copy(kn.iota[:, :], r["ii"][:, :]))
            e.tensor_copy(kn.pcol[:, :], r["ip"][:, :]).then_inc(r["ready"], 1)

        def vector(e, ch):
            ch(e.memset(kn.ones[:, :], 1.0))
            ch(e.memset(kn.zero1[:, :], 0.0))
            ch(e.memset(kn.half1[:, :], 0.5))
            ch(e.memset(kn.eps1[:, :], EPS))
            ch(e.memset(kn.hp1[:, :], 1.5707963267948966))
            e.wait_ge(r["ready"], 1)
            ch(e.tensor_copy(kn.iotab[:, :], kn.iota[:, :]))
            ch(e.tensor_scalar(kn.ident[:, :], kn.iota[:, :], kn.pcol[:, 0:1], None, ALU.is_equal))
            ch(e.tensor_scalar(kn.before[:, :], kn.iota[:, :], kn.pcol[:, 0:1], None, ALU.is_gt))
            ch.wait()
            ch(e.tensor_copy(kn.identb[:, :], kn.ident[:, :]))
            ch(e.tensor_copy(kn.beforeb[:, :], kn.before[:, :]))
            ch.wait()

        def sync(e, ch):
            full = (N // P) * P
            e.dma_start(kn.X[:, 0:N // P, :], ins["x"][0:full, :].rearrange("(b p) h -> p b h", p=P)).then_inc(r["ld"], 16)
            e.dma_start(kn.X[0:N - full, N // P, :], ins["x"][full:N, :]).then_inc(r["ld"], 16)
            e.wait_ge(r["ld"], 32)

        def scalar(e, ch):
            pass
        return dict(gpsimd=gpsimd, vector=vector, sync=sync)
    def build0(r):
        def vector(e, ch):
            ch(e.memset(kn.X[:, NB - 1, :], 0.0))
            ch.wait()
        return dict(vector=vector)
    phase(kn, "clear", build0)
    phase(kn, "const", build, sbufs=[("ii", [P, P], I32), ("ip", [P, 1], I32)], sems=["ready", "ld"])

def split_keys(kn):
    kn.lo_rows = dram(kn, "lo_rows", (2, EP), BF16)
    kn.khi = kn.keys_ctx.enter_context(kn.nc.sbuf_tensor("khi", [P, 2, T], F32))
    kn.klo = kn.keys_ctx.enter_context(kn.nc.sbuf_tensor("klo", [P, 2, T], F32))
    kn.kin = kn.keys_ctx.enter_context(kn.nc.sbuf_tensor("kin", [P, 2, T], I32))
    kn.klob = kn.keys_ctx.enter_context(kn.nc.sbuf_tensor("klob", [P, 2, T], BF16))
    kn.khib = kn.keys_ctx.enter_context(kn.nc.sbuf_tensor("khib", [P, 2, T], BF16))

    def build(r):
        def sync(e, ch):
            for q, n in enumerate(("dst", "src")):
                e.dma_start(kn.kin[:, q, :], kn.ins[n + "_tiles"]).then_inc(r["ld"], 16)
                e.dma_start(r["lin"][:, q, :], kn.ins[n + "_lin"].rearrange("(p c) -> p c", p=P)).then_inc(r["ld"], 16)
            e.wait_ge(r["lo"], 1)
            for q in range(2):
                e.dma_start(kn.lo_rows[q].rearrange("(p c) -> p c", p=P), r["linb"][:, q, :]).then_inc(r["st"], 16)
            e.wait_ge(r["st"], 32)

        def vector(e, ch):
            e.wait_ge(r["ld"], 64)
            ch(e.tensor_scalar(r["a"][:, :, :], kn.kin[:, :, :], 127, None, ALU.bitwise_and))
            ch(e.tensor_scalar(r["b"][:, :, :], kn.kin[:, :, :], 7, None, ALU.logical_shift_right))
            ch(e.tensor_scalar(r["c"][:, :, :], r["lin"][:, :, :], 127, None, ALU.bitwise_and))
            ch.wait()
            ch(e.tensor_copy(kn.klo[:, :, :], r["a"][:, :, :]))
            ch(e.tensor_copy(kn.khi[:, :, :], r["b"][:, :, :]))
            ch(e.tensor_copy(kn.klob[:, :, :], r["a"][:, :, :]))
            ch(e.tensor_copy(kn.khib[:, :, :], r["b"][:, :, :]))
            e.tensor_copy(r["linb"][:, :, :], r["c"][:, :, :]).then_inc(r["lo"], 1)
            ch.wait()
        return dict(sync=sync, vector=vector)
    phase(kn, "keys", build, sbufs=[("lin", [P, 2, T], I32), ("linb", [P, 2, T], BF16), ("a", [P, 2, T], I32),
                                     ("b", [P, 2, T], I32), ("c", [P, 2, T], I32)], sems=["ld", "lo", "st"])

def one_hots(kn, e, ch, r, st, q, what):
    w = P if what == "lo" else NB
    src = kn.klob if what == "lo" else kn.khib
    tiles = src[:, q, bass.ds(st.i * GT, GT)]
    return e.tensor_tensor(r["oh" + what][:, st.par, q, :, :], tiles.unsqueeze(2).to_broadcast([P, GT, w]),
                           kn.iotab[:, None, 0:w].to_broadcast([P, GT, w]), ALU.is_equal)

def histogram(kn):
    n = T // GT

    def build(r):
        def vector(e, ch):
            def hot(st):
                wait_step(e, r["pe"], st, 2)
                for q in range(2):
                    one_hots(kn, e, ch, r, st, q, "lo")
                    ins = one_hots(kn, e, ch, r, st, q, "hi")
                ins.then_inc(r["hot"], 1)
            run_steps(e, ch, [(hot, 0)], n)
            e.wait_ge(r["pe"], n)
            for q in range(2):
                ch(e.tensor_copy(kn.count[:, q, :], r["hist"][:, q, 0:NB]))
            ch.wait()

        def tensor(e, ch):
            def add(st, first=False):
                wait_step(e, r["hot"], st)
                for j in range(GT):
                    for q in range(2):
                        f = isinstance(st.i, int) and st.i == 0 and j == 0
                        ins = e.matmul(r["hist"][:, q, 0:NB], r["ohlo"][:, st.par, q, j, :],
                                       r["ohhi"][:, st.par, q, j, :], start=f, stop=False, skip_group_check=True)
                ins.then_inc(r["pe"], 1)
            run_steps(e, ch, [(add, 0)], n)
        return dict(vector=vector, tensor=tensor)
    phase(kn, "hist", build, psums=[("hist", [P, 2, 512], F32)],
               sbufs=[("ohlo", [P, 2, 2, GT, P], BF16), ("ohhi", [P, 2, 2, GT, NB], BF16)], sems=["hot", "pe"])

def offsets(kn):
    half = SLOTS // 2
    nt = -(-T // P)

    def build(r):
        def tensor(e, ch):
            e.matmul(r["small"][:, 0:2 * NB], kn.before[:, :], kn.count[:, :, :].rearrange("p q b -> p (q b)"),
                     start=True, stop=True)
            e.matmul(r["small"][:, 2 * NB:4 * NB], kn.ones[:, :],
                     kn.count[:, :, :].rearrange("p q b -> p (q b)"), start=True, stop=True,
                     skip_group_check=True).then_inc(r["sums"], 1)
            for q in range(2):
                e.wait_ge(r["less"], q + 1)
                for h in range(2):
                    for c in range(nt):
                        ins = e.matmul(r["tiles"][:, q, h, 0:half], kn.ones[:, :],
                                       r["lt"][:, q, c, h * half:(h + 1) * half], start=(c == 0), stop=(c == nt - 1))
                ins.then_inc(r["counted"], 1)

        def gpsimd(e, ch):
            e.iota(r["is"][:, :], [[1, SLOTS]], base=0, channel_multiplier=0).then_inc(r["iota"], 1)

        def vector(e, ch):
            e.wait_ge(r["iota"], 1)
            ch(e.tensor_copy(r["s"][:, :], r["is"][:, :]))
            for c in range(nt):
                ch(e.tensor_scalar(r["last"][:, c:c + 1], kn.pcol[:, 0:1], float(P), float(P * P * c + P - 1),
                                   ALU.mult, ALU.add))
            e.wait_ge(r["sums"], 1)
            ch(e.tensor_copy(r["tot"][:, :], r["small"][:, 2 * NB:4 * NB]))
            ch.wait()
            for q in range(2):
                ch(e.tensor_tensor_scan(r["upto"][:, q, :], kn.ones[:, 0:NB], r["tot"][:, q * NB:(q + 1) * NB], 0.0,
                                        ALU.mult, ALU.add))
            ch.wait()
            ch(e.tensor_tensor(r["excl"][:, :], r["upto"][:, :, :].rearrange("p q b -> p (q b)"), r["tot"][:, :],
                               ALU.subtract))
            ch.wait()
            ch(e.tensor_tensor(kn.start[:, :, :].rearrange("p q b -> p (q b)"), r["small"][:, 0:2 * NB],
                               r["excl"][:, :], ALU.add))
            for q in range(2):
                for c in range(nt):
                    ch(e.tensor_scalar(r["le"][:, q, c, :], r["upto"][:, q, 0:NB - 1], r["last"][:, c:c + 1], None,
                                       ALU.is_le))
            ch.wait()
            for q in range(2):
                ch(e.tensor_reduce(r["blk"][:, q, :], r["le"][:, q, :, :], AX, ALU.add))
            for c in range(nt):
                ch(e.tensor_scalar(r["t"][:, c:c + 1], kn.pcol[:, 0:1], float(P * c), None, ALU.add))
            ch.wait()
            for q in range(2):
                ch(e.tensor_tensor(r["val"][:, q, :], r["blk"][:, q, :], r["t"][:, :], ALU.add))
            ch.wait()
            for q in range(2):
                for c in range(nt):
                    ins = e.tensor_scalar(r["lt"][:, q, c, :], r["s"][:, :], r["val"][:, q, c:c + 1], None, ALU.is_gt)
                ins.then_inc(r["less"], 1)
            e.wait_ge(r["counted"], 2)
            for q in range(2):
                for h in range(2):
                    cols = slice(h * half, (h + 1) * half)
                    ch(e.tensor_copy(kn.slot_reg[64 * q:64 * q + 32, cols], r["tiles"][0:32, q, h, 0:half]))
                    ch(e.scalar_tensor_tensor(r["b"][:, q, cols], r["tiles"][:, q, h, 0:half], -1.0, r["s"][:, cols],
                                              ALU.mult, ALU.add))
            ch.wait()
            for q in range(2):
                ch(e.tensor_copy(kn.slot_reg[64 * q + 32:64 * q + 64, :], r["b"][0:32, q, :]))
                ch(e.tensor_scalar(kn.local[:, q, :], r["b"][:, q, :], float(P), None, ALU.mult))
            ch.wait()
        return dict(tensor=tensor, gpsimd=gpsimd, vector=vector)
    phase(kn, "offsets", build, psums=[("small", [P, 512], F32), ("tiles", [P, 2, 2, 512], F32)],
               sbufs=[("is", [P, SLOTS], I32), ("s", [P, SLOTS], F32), ("last", [P, nt], F32), ("tot", [P, 2 * NB], F32),
                      ("upto", [P, 2, NB], F32), ("excl", [P, 2 * NB], F32), ("le", [P, 2, nt, NB - 1], F32),
                      ("blk", [P, 2, nt], F32), ("t", [P, nt], F32), ("val", [P, 2, nt], F32),
                      ("lt", [P, 2, nt, SLOTS], F32), ("b", [P, 2, SLOTS], F32)],
               sems=["sums", "iota", "less", "counted"])

def sort(kn):
    n = T // GT
    rec_tiles = kn.ins["rec"].rearrange("(t p) c -> p t c", p=P)
    kn.sorted = dram(kn, "sorted_records", (EP, P))

    def build(r):
        def sync(e, ch):
            def load_rows(st):
                wait_step(e, r["hot"], st, 2)
                for q in range(2):
                    e.dma_start(r["rows"][:, st.par, q, :],
                                kn.lo_rows[q:q + 1, bass.ds(st.i * (GT * P), GT * P)].to_broadcast([P, GT * P])
                                ).then_inc(r["ld"][st.par], 16)

            def load_records(st):
                wait_free(e, r["sent"], st, GT)
                e.dma_start(r["rec"][:, st.par, :, 0:NREC], rec_tiles[:, bass.ds(st.i * GT, GT), :]
                            ).then_inc(r["rec_ld"][st.par], 16)
            e.wait_ge(r["cleared"], 1)
            run_steps(e, ch, [(load_rows, 0), (load_records, 1)], n)

        def vector(e, ch):
            e.memset(r["rec"][:, :, :, :], 0.0).then_inc(r["cleared"], 1)
            ch(e.memset(r["keep"][:, :, :, 1:], 1.0))
            ch(e.memset(r["keep"][:, :, :, 0:1], 0.0))
            ch(e.tensor_copy(r["before"][:, 1, :, :, GT], kn.start[:, :, :]))

            def hot(st):
                wait_step(e, r["placed"], st, 2)
                wait_load(e, r["ld"], st, 2)
                for q in range(2):
                    one_hots(kn, e, ch, r, st, q, "lo")
                    one_hots(kn, e, ch, r, st, q, "hi").then_inc(r["hot_part"], 1)
                e.tensor_scalar(r["ohT"][:, st.par, :, :], r["rows"][:, st.par, :, :], kn.pcol[:, 0:1], None,
                                ALU.is_equal).then_inc(r["hot"], 1)

            def mask(st):
                for u in range(4):
                    q, h = u // 2, u % 2
                    e.wait_ge(r["same_done"], st.i * 4 + (u + 1))
                    e.tensor_tensor(r["mask"][:, st.par, q, 4 * h:4 * h + 4, :], r["same"][:, u, :, :],
                                    kn.before[:, None, :].to_broadcast([P, 4, P]), ALU.mult
                                    ).then_inc(r["masked"], 1)

            def scan(st):
                ch.wait()
                ch(e.tensor_copy(r["own"][:, st.par, :, :, 0], r["before"][:, 1 - st.par, :, :, GT]))
                wait_step(e, r["own_ok"], st)
                ch.wait()
                ch(e.tensor_tensor_scan(r["before"][:, st.par, :, :, :].rearrange("p q k t -> p (q k t)"),
                                        r["keep"][:, :, :, :].rearrange("p q k t -> p (q k t)"),
                                        r["own"][:, st.par, :, :, :].rearrange("p q k t -> p (q k t)"),
                                        0.0, ALU.mult, ALU.add))
                ch.wait()
                e.sem_inc(r["scanned"], 1)

            def place(st):
                wait_step(e, r["ranked"], st)
                wait_load(e, r["rec_ld"], st, 1)
                wait_free(e, r["sent"], st, GT)
                ch.wait()
                for q in range(2):
                    ch(e.tensor_tensor(r["pick"][:, q, :, :], r["rank"][:, q, :, 0:NB],
                                       r["ohhi"][:, st.par, q, :, :], ALU.mult))
                tiles = kn.kin[:, :, bass.ds(st.i * GT, GT)]
                ch(e.tensor_copy(r["rec"][:, st.par, :, W_DST:W_SRC + 1].rearrange("p t q -> p q t"), tiles))
                ch.wait()
                ch(e.tensor_reduce(r["pos"][:, :, :], r["pick"][:, :, :, :], AX, ALU.add))
                ch.wait()
                ch(e.tensor_copy(r["idx"][:, st.par, :], r["pos"][:, 0, :]))
                e.tensor_scalar(r["rec"][:, st.par, :, W_POS], r["pos"][:, 1, :], BIG, None, ALU.add
                                ).then_inc(r["placed"], 1)
            run_steps(e, ch, [(hot, 0), (place, 1), (mask, 0), (scan, 0)], n)

        def scalar(e, ch):
            def own(st):
                wait_step(e, r["counted"], st)
                wait_step(e, r["scanned"], st, 2)
                for q in range(2):
                    ins = e.activation(r["own"][:, st.par, q, :, 1:].rearrange("p k t -> p t k"),
                                       r["count"][:, q, 0:GT * NB].rearrange("p (t k) -> p t k", k=NB), ACT.Copy)
                ins.then_inc(r["own_ok"], 1)
            run_steps(e, ch, [(own, 0)], n)

        def tensor(e, ch):
            def count(st):
                wait_step(e, r["own_ok"], st, 1)
                for q in range(2):
                    e.wait_ge(r["hot_part"], st.i * 2 + (q + 1))
                    for j in range(GT):
                        ins = e.matmul(r["count"][:, q, j * NB:(j + 1) * NB], r["ohlo"][:, st.par, q, j, :],
                                       r["ohhi"][:, st.par, q, j, :], start=True, stop=True)
                ins.then_inc(r["counted"], 1)

            def same(st):
                wait_step(e, r["hot"], st)
                for u in range(4):
                    q, h = u // 2, u % 2
                    v = st.i * 4 + (u - 3)
                    if not isinstance(v, int) or v > 0:
                        e.wait_ge(r["masked"], v)
                    for j in range(4):
                        t = r["ohT"][:, st.par, q, (4 * h + j) * P:(4 * h + j + 1) * P]
                        ins = e.matmul(r["same"][:, u, j, :], t, t, start=True, stop=True)
                    ins.then_inc(r["same_done"], 1)

            def rank(st):
                wait_step(e, r["placed"], st, 1)
                e.wait_ge(r["masked"], st.i * 4 + 4)
                wait_step(e, r["scanned"], st)
                for j in range(GT):
                    for q in range(2):
                        out = r["rank"][:, q, j, 0:NB]
                        e.matmul(out, r["ohT"][:, st.par, q, j * P:(j + 1) * P], r["before"][:, st.par, q, :, j],
                                 start=True, stop=False, skip_group_check=True)
                        ins = e.matmul(out, r["mask"][:, st.par, q, j, :], r["ohhi"][:, st.par, q, j, :],
                                       start=False, stop=True, skip_group_check=True)
                ins.then_inc(r["ranked"], 1)
            run_steps(e, ch, [(count, 0), (same, 0), (rank, 0)], n)

        def gpsimd(e, ch):
            def send(st):
                wait_step(e, r["placed"], st)
                take_waits(e, kn.tally)
                for j in range(GT):
                    e.indirect_dma_start(kn.sorted[:, :],
                                         bass.IndirectOffsetOnAxis(ap=r["idx"][:, st.par, j:j + 1], axis=0),
                                         r["rec"][:, st.par, j, :], None, bounds_check=EP - 1
                                         ).then_inc(r["sent"][st.par], 16)
            run_steps(e, ch, [(send, 0)], n)
            for j in range(2):
                e.wait_ge(r["sent"][j], 16 * GT * (n // 2))
        return dict(sync=sync, vector=vector, scalar=scalar, tensor=tensor, gpsimd=gpsimd)
    phase(kn, "sort", build, psums=[("same", [P, 4, 4, P], F32), ("rank", [P, 2, GT, 64], F32), ("count", [P, 2, BANK], F32)],
               sbufs=[("rows", [P, 2, 2, GT * P], BF16), ("rec", [P, 2, GT, P], F32), ("ohlo", [P, 2, 2, GT, P], BF16),
                      ("ohhi", [P, 2, 2, GT, NB], BF16), ("ohT", [P, 2, 2, GT * P], F32),
                      ("mask", [P, 2, 2, GT, P], BF16), ("pick", [P, 2, GT, NB], F32), ("pos", [P, 2, GT], F32),
                      ("idx", [P, 2, GT], I32), ("own", [P, 2, 2, NB, GT + 1], F32), ("before", [P, 2, 2, NB, GT + 1], F32),
                      ("keep", [P, 2, NB, GT + 1], F32)],
               sems=["cleared", "hot_part", "hot", "counted", "own_ok", "scanned", "same_done", "masked", "ranked", "placed"],
               pairs=["ld", "rec_ld", "sent"])

def slot_columns(kn):
    chunk = 98
    srt = kn.sorted.rearrange("(t p) c -> p t c", p=P)
    meta = flat(kn, kn.MT).rearrange("p (t c) -> p t c", c=META)

    def build(r):
        def sync(e, ch):
            for n, t in ((kn.W, kn.ins["mats"]), (kn.V, kn.ins["vecs"])):
                e.dma_start(n[tuple([slice(None)] * len(t.shape))], t).then_inc(r["wld"], 16)
            e.dma_start(kn.R[:, :, :].rearrange("p r h -> p (r h)"),
                        kn.ins["rows"].to_broadcast([P, len(ROWS) * H])).then_inc(r["wld"], 16)
            for c in range(T // chunk):
                e.dma_start(meta[:, c * chunk:(c + 1) * chunk, :], srt[:, c * chunk:(c + 1) * chunk, CM:CM + META]
                            ).then_inc(r["ld"], 16)
            e.wait_ge(r["ld"], 16 * (T // chunk))
            e.wait_ge(r["wld"], 48)

        def vector(e, ch):
            e.wait_ge(r["ld"], 16 * (T // chunk))


            def pick(st):
                tiles = slot_values(kn, e, kn.slot_regs["vector"], st, 0)
                for j in range(G):
                    ch(e.tensor_copy(r["m"][:, bass.ds((st.i * G + j) * META, META)],
                                     meta[:, bass.ds(tiles[j], 1), :].rearrange("p a c -> p (a c)")))
            run_steps(e, ch, [(pick, 0)], STEPS // 2)
            ch.wait()
            e.wait_ge(r["other_half"], 1)
            m = r["m"][:, :].rearrange("p (s c) -> p s c", c=META)
            ch(e.tensor_tensor(kn.local[:, 0, :], m[:, :, 4], kn.local[:, 0, :], ALU.subtract))
            ch(e.tensor_copy(kn.src_of[:, :], m[:, :, 5]))
            ch(e.tensor_copy(kn.wt[:, :], m[:, :, 3]))
            ch(e.tensor_tensor(r["a"][:, 0, :], m[:, :, 0], m[:, :, 0], ALU.mult))
            ch(e.tensor_tensor(r["a"][:, 1, :], m[:, :, 1], m[:, :, 1], ALU.mult))
            ch(e.tensor_tensor(r["a"][:, 2, :], m[:, :, 2], m[:, :, 2], ALU.mult))
            ch.wait()
            ch(e.tensor_tensor(r["a"][:, 0, :], r["a"][:, 0, :], r["a"][:, 1, :], ALU.add))
            ch.wait()
            ch(e.tensor_scalar(r["a"][:, 1, :], kn.local[:, 0, :], float(P), None, ALU.is_lt))
            ch.wait()
            ch(e.scalar_tensor_tensor(r["a"][:, 1, :], kn.local[:, 0, :], 0.0, r["a"][:, 1, :], ALU.is_ge, ALU.mult))
            e.tensor_tensor(r["a"][:, 0, :], r["a"][:, 0, :], r["a"][:, 2, :], ALU.add).then_inc(r["sq"], 1)
            ch.wait()
            ch(e.scalar_tensor_tensor(kn.place[:, :], r["a"][:, 1, :], -BIG, m[:, :, 6], ALU.mult, ALU.add))
            e.wait_ge(r["root"], 1)
            ch(e.tensor_scalar(kn.cut[:, :], r["a"][:, 0, :], 10.0, None, ALU.is_le))
            e.tensor_scalar(r["a"][:, 2, :], r["a"][:, 0, :], 10.0, None, ALU.min).then_inc(r["capped"], 1)
            e.wait_ge(r["cosine"], 1)
            ch(e.tensor_scalar(r["a"][:, 0, :], r["a"][:, 2, :], 1.0, 0.5, ALU.add, ALU.mult))
            ch.wait()
            ch(e.tensor_tensor(kn.cut[:, :], kn.cut[:, :], r["a"][:, 0, :], ALU.mult))
            ch.wait()

        def scalar(e, ch):
            e.wait_ge(r["ld"], 16 * (T // chunk))

            def pick(st):
                tiles = slot_values(kn, e, kn.slot_regs["scalar"], st, 0, STEPS // 2)
                for j in range(G):
                    ch(e.activation(r["m"][:, bass.ds((st.i * G + j + SLOTS // 2) * META, META)],
                                    meta[:, bass.ds(tiles[j], 1), :].rearrange("p a c -> p (a c)"), ACT.Copy))
            run_steps(e, ch, [(pick, 0)], STEPS // 2)
            ch.wait()
            e.sem_inc(r["other_half"], 1)
            e.wait_ge(r["sq"], 1)
            e.activation(r["a"][:, 0, :], r["a"][:, 0, :], ACT.Sqrt).then_inc(r["root"], 1)
            e.wait_ge(r["capped"], 1)
            e.activation(r["a"][:, 2, :], r["a"][:, 2, :], ACT.Sin, bias=kn.hp1[:, 0:1],
                         scale=-3.141592653589793 / 10.0).then_inc(r["cosine"], 1)
        return dict(sync=sync, vector=vector, scalar=scalar)
    phase(kn, "slots", build, sbufs=[("m", [P, SLOTS * META], F32), ("a", [P, 3, SLOTS], F32)],
               sems=["ld", "wld", "other_half", "sq", "root", "capped", "cosine"])

def mat(kn, name, rows=P):
    return kn.W[0:rows, MATS.index(name), :]

def vec(kn, name):
    i = VECS.index(name)
    return kn.V[:, i:i + 1]

def row(kn, name):
    return kn.R[:, ROWS.index(name), :]

def block(kn, t, b):
    return flat(kn, t)[:, bass.ds(b * P, P)]

def layernorm(kn, name, src=None, dst=None, func=ACT.Relu):
    src, dst = src or kn.X, dst or kn.Hn

    def build(r):
        def vector(e, ch):
            def stats(st):
                ch(e.bn_stats(r["six"][:, bass.ds(st.i * 6, 6)], block(kn, src, st.i)))
            run_steps(e, ch, [(stats, 0)], NB)
            ch.wait()
            for b in range(NB):
                ch(e.bn_aggr(r["mv"][:, 2 * b:2 * b + 2], r["six"][:, 6 * b:6 * b + 6]))
            ch.wait()
            mv = r["mv"][:, :].rearrange("p (b k) -> p b k", k=2)
            e.tensor_copy(r["var"][:, :], mv[:, :, 1]).then_inc(r["var_ok"], 1)
            e.wait_ge(r["std"], 1)
            ch(e.reciprocal(r["rstd"][:, :], r["var"][:, :]))
            ch.wait()
            e.scalar_tensor_tensor(r["shift"][:, :], mv[:, :, 0], -1.0, r["rstd"][:, :], ALU.mult, ALU.mult
                                   ).then_inc(r["scales"], 1)

        def scalar(e, ch):
            e.wait_ge(r["var_ok"], 1)
            e.activation(r["var"][:, :], r["var"][:, :], ACT.Sqrt, bias=kn.eps1[:, 0:1]).then_inc(r["std"], 1)
            e.wait_ge(r["scales"], 1)

            def norm(st):
                ch(e.activation(block(kn, dst, st.i), block(kn, src, st.i), func,
                                bias=r["shift"][:, bass.ds(st.i, 1)], scale=r["rstd"][:, bass.ds(st.i, 1)]))
            run_steps(e, ch, [(norm, 0)], NB)
            ch.wait()
        return dict(vector=vector, scalar=scalar)
    phase(kn, name, build, sbufs=[("six", [P, 6 * NB], F32), ("mv", [P, 2 * NB], F32), ("var", [P, NB], F32),
                                   ("rstd", [P, NB], F32), ("shift", [P, NB], F32)],
               sems=["var_ok", "std", "scales"])

def l0_nodes(kn):
    def build(r):
        def tensor(e, ch):
            def turn(st):
                wait_step(e, r["fetched"], st)
                wait_step(e, r["hT_ok"], st, 2)
                e.transpose(r["pA"][:, st.par, 0:P], r["hb"][:, st.par, :], kn.ident[:, :]).then_inc(r["turned"], 1)

            def lin(st):
                wait_step(e, r["hT_ok"], st)
                wait_step(e, r["xl_ok"], st, 2)
                e.matmul(r["pB"][:, st.par, 0:P], r["hT"][:, st.par, :], mat(kn, "W_lin"), start=True, stop=True
                         ).then_inc(r["lin_ok"], 1)

            def turn_xl(st):
                wait_step(e, r["xl_ok"], st)
                wait_step(e, r["xlT_ok"], st, 2)
                e.transpose(r["pC"][:, st.par, 0:P], r["xl"][:, st.par, :], kn.ident[:, :]).then_inc(r["xl_turned"], 1)

            def att(st):
                wait_step(e, r["xlT_ok"], st)
                wait_step(e, r["s_ok"], st, 2)
                e.matmul(r["pD"][:, st.par, 0:2 * HEADS], r["xlT"][:, st.par, :], mat(kn, "W_att")[:, 0:2 * HEADS],
                         start=True, stop=True).then_inc(r["att_ok"], 1)
            run_steps(e, ch, [(turn, 0), (lin, 0), (turn_xl, 1), (att, 1)], NB)

        def scalar(e, ch):
            def fetch(st):
                wait_step(e, r["turned"], st, 2)
                e.activation(r["hb"][:, st.par, :], block(kn, kn.Hn, st.i), ACT.Copy).then_inc(r["fetched"], 1)

            def copy_h(st):
                wait_step(e, r["turned"], st)
                wait_step(e, r["lin_ok"], st, 2)
                e.activation(r["hT"][:, st.par, :], r["pA"][:, st.par, 0:P], ACT.Copy).then_inc(r["hT_ok"], 1)

            def copy_xl(st):
                wait_step(e, r["xl_turned"], st)
                wait_step(e, r["att_ok"], st, 2)
                e.activation(r["xlT"][:, st.par, :], r["pC"][:, st.par, 0:P], ACT.Copy).then_inc(r["xlT_ok"], 1)
            run_steps(e, ch, [(fetch, 0), (copy_h, 0), (copy_xl, 1)], NB)

        def vector(e, ch):
            def xl(st):
                wait_step(e, r["lin_ok"], st)
                wait_step(e, r["xl_turned"], st, 2)
                ch(e.tensor_tensor(block(kn, kn.TB, st.i), r["pB"][:, st.par, 0:P], row(kn, "b_lin"), ALU.add))
                e.tensor_tensor(r["xl"][:, st.par, :], r["pB"][:, st.par, 0:P], row(kn, "b_lin"), ALU.add
                                ).then_inc(r["xl_ok"], 1)

            def s(st):
                wait_step(e, r["att_ok"], st)
                e.tensor_tensor(kn.sij[:, bass.ds(st.i * 2 * HEADS, 2 * HEADS)], r["pD"][:, st.par, 0:2 * HEADS],
                                row(kn, "b_att")[:, 0:2 * HEADS], ALU.add).then_inc(r["s_ok"], 1)
            run_steps(e, ch, [(xl, 0), (s, 1)], NB)
            e.wait_ge(r["s_ok"], NB)
            sij = kn.sij[:, :].rearrange("p (b k) -> p b k", k=2 * HEADS)
            ch(e.memset(r["first"][:, :, 4:5], 1.0))
            ch(e.memset(r["first"][:, :, 6:8], 0.0))
            ch(e.tensor_copy(r["first"][:, :, 0:4], sij[:, :, 0:4]))
            ch(e.tensor_scalar(r["first"][:, :, 5], kn.iota[:, 0:NB], float(P), kn.pcol[:, 0:1], ALU.mult, ALU.add))
            ch(e.memset(kn.MT[:, :, :], 0.0))
            ch(e.tensor_scalar(r["none"][:, :], kn.count[:, 1, :], 0.0, None, ALU.is_equal))
            ch.wait()
            e.scalar_tensor_tensor(r["at"][:, :], r["none"][:, :], BIG, kn.start[:, 1, :], ALU.mult, ALU.add
                                   ).then_inc(r["rows_ok"], 1)

        def sync(e, ch):
            e.wait_ge(r["rows_ok"], 1)
            e.dma_start(kn.firsts.rearrange("(p c) k -> p (c k)", p=P), flat(kn, kn.MT)).then_inc(r["zeroed"], 16)
            e.wait_ge(r["zeroed"], 16)

        def gpsimd(e, ch):
            e.wait_ge(r["zeroed"], 16)
            for b in range(NB):
                e.indirect_dma_start(kn.firsts[:, :], bass.IndirectOffsetOnAxis(ap=r["at"][:, b:b + 1], axis=0),
                                     r["first"][:, b, :], None, bounds_check=EP - 1, oob_is_err=False
                                     ).then_inc(r["sent"], 16)
            e.wait_ge(r["sent"], 16 * NB)
        return dict(tensor=tensor, scalar=scalar, vector=vector, sync=sync, gpsimd=gpsimd)
    kn.firsts = dram(kn, "firsts", (EP, 8))
    phase(kn, "l0n", build, psums=[(n, [P, 2, BANK], F32) for n in ("pA", "pB", "pC", "pD")],
               sbufs=[("hb", [P, 2, P], F32), ("xl", [P, 2, P], F32), ("hT", [P, 2, P], F32),
                      ("xlT", [P, 2, P], F32), ("first", [P, NB, 8], F32),
                      ("none", [P, NB], F32), ("at", [P, NB], I32)],
               sems=["fetched", "turned", "hT_ok", "lin_ok", "xl_ok", "xl_turned", "xlT_ok", "att_ok", "s_ok", "rows_ok",
                     "zeroed", "sent"])

def hot_stage(kn, e, r, q, free, back=2, iota=None):
    iota = kn.iota if iota is None else iota

    def hot(st):
        wait_step(e, free, st, back)
        for j in range(G):
            ins = e.tensor_scalar(r["oh"][:, st.par, j, :], iota[:, :],
                                  kn.local[:, q, bass.ds(st.i * G + j, 1)], None, ALU.is_equal)
        ins.then_inc(r["hot"], 1)
    return hot

def turn_hot_stage(kn, e, r, banks=2, ident=None):
    ident = kn.ident if ident is None else ident
    def turn(st):
        wait_step(e, r["hot"], st)
        wait_step(e, r["ohT_ok"], st, banks)
        for j in range(G):
            ins = e.transpose(r["pT"][:, st.par % banks, j, :], r["oh"][:, st.par, j, :], ident[:, :])
        ins.then_inc(r["turned"], 1)
    return turn

def copy_hot_stage(kn, e, r, used, banks=2):
    def copy(st):
        wait_step(e, r["turned"], st)
        wait_step(e, used, st, 2)
        e.activation(r["ohT"][:, st.par, :, :], r["pT"][:, st.par % banks, 0:G, :], ACT.Copy
                     ).then_inc(r["ohT_ok"], 1)
    return copy

def slot_values(kn, e, regs, st, which, first=0):
    e.load(regs, kn.slot_reg[which:which + 1, bass.ds(st.i * G + first * G, G)])
    return [e.snap(g, min_val=0, max_val=(T if which % 64 == 0 else NB) - 1) for g in regs]

def add_stage(kn, e, ch, r, q):

    def add(st):
        blocks = slot_values(kn, e, kn.slot_regs["vector"], st, 64 * q + 32)
        wait_step(e, r["summed"], st)
        for j in range(G):
            ch.wait()
            acc = block(kn, kn.AC, blocks[j])
            ins = e.tensor_tensor(acc, acc, r["pR"][:, st.par, j, :], ALU.add)
            if j < G - 1:
                ch(ins)
        ins.then_inc(r["added"], 1)
        e.wait_ge(r["added"], st.i + 1)
    return add

def l0_scores(kn):
    kn.sj_src = dram(kn, "sj_src", (EP, HEADS))
    kn.slot_sj = flat(kn, kn.MT)[:, 0:SLOTS * HEADS]

    def build(r):
        def vector(e, ch):
            hot = hot_stage(kn, e, r, 0, r["turned"], iota=kn.iotab)

            def idx(st):
                wait_free(e, r["sent"], st, G)
                e.tensor_copy(r["idx"][:, st.par, :], kn.place[:, bass.ds(st.i * G, G)]).then_inc(r["idx_ok"], 1)
            run_steps(e, ch, [(hot, 0), (idx, 0)], STEPS)

        def tensor(e, ch):
            turn = turn_hot_stage(kn, e, r, ident=kn.identb)


            def pick(st):
                blocks = slot_values(kn, e, kn.slot_regs["tensor"], st, 32)
                wait_step(e, r["ohT_ok"], st)
                wait_step(e, r["kept"], st, 2)
                for j in range(G):
                    ins = e.matmul(r["pS"][:, st.par, j * HEADS:(j + 1) * HEADS], r["ohT"][:, st.par, j, :],
                                   kn.sij[:, bass.ds(blocks[j] * (2 * HEADS) + HEADS, HEADS)], start=True, stop=True)
                ins.then_inc(r["picked"], 1)
            run_steps(e, ch, [(turn, 0), (pick, 1)], STEPS)

        def scalar(e, ch):
            copy = copy_hot_stage(kn, e, r, r["picked"])

            def keep(st):
                wait_step(e, r["picked"], st)
                e.activation(kn.slot_sj[:, bass.ds(st.i * G * HEADS, G * HEADS)],
                             r["pS"][:, st.par, 0:G * HEADS], ACT.Copy).then_inc(r["kept"], 1)
                wait_free(e, r["sent"], st, G)
                e.activation(r["out"][:, st.par, :, :].rearrange("p j k -> p (j k)"), r["pS"][:, st.par, 0:G * HEADS], ACT.Copy).then_inc(r["out_ok"], 1)
            run_steps(e, ch, [(copy, 0), (keep, 1)], STEPS)

        def gpsimd(e, ch):
            def send(st):
                wait_step(e, r["out_ok"], st)
                wait_step(e, r["idx_ok"], st)
                take_waits(e, kn.tally)
                for j in range(G):
                    e.indirect_dma_start(kn.sj_src[:, :],
                                         bass.IndirectOffsetOnAxis(ap=r["idx"][:, st.par, j:j + 1], axis=0),
                                         r["out"][:, st.par, j, :], None, bounds_check=EP - 1, oob_is_err=False
                                         ).then_inc(r["sent"][st.par], 16)
            run_steps(e, ch, [(send, 0)], STEPS)
            for j in range(2):
                e.wait_ge(r["sent"][j], 16 * G * (STEPS // 2))
        return dict(vector=vector, tensor=tensor, scalar=scalar, gpsimd=gpsimd)
    phase(kn, "l0s", build, psums=[("pT", [P, 2, 2 * G, P], BF16), ("pS", [P, 2, BANK], F32)],
               sbufs=[("oh", [P, 2, G, P], BF16), ("ohT", [P, 2, G, P], F32), ("out", [P, 2, G, HEADS], F32),
                      ("idx", [P, 2, G], I32)],
               sems=["hot", "turned", "ohT_ok", "picked", "kept", "out_ok", "idx_ok"], pairs=["sent"])

def l0_segments(kn):
    kn.run_ml = dram(kn, "run_ml", (EP, 2 * HEADS))
    kn.src_sorted = dram(kn, "src_sorted", (EP,))
    fl = flat(kn, kn.AC)
    firsts = fl.rearrange("p (c k) -> p c k", k=8)
    d0 = fl[:, 0:HEADS * T].rearrange("p (k c) -> p k c", k=HEADS)
    d1 = fl[:, HEADS * T:2 * HEADS * T].rearrange("p (k c) -> p k c", k=HEADS)
    hl = flat(kn, kn.Hn)
    sj = hl[:, 0:HEADS * T].rearrange("p (c k) -> p c k", k=HEADS)
    si = hl[:, HEADS * T:2 * HEADS * T].rearrange("p (k c) -> p k c", k=HEADS)
    both = hl.rearrange("p (c k) -> p c k", k=2 * HEADS)

    def build(r):
        turns = [0]

        def sync(e, ch):
            e.dma_start(fl, kn.firsts.rearrange("(p c) k -> p (c k)", p=P)).then_inc(r["ld"], 16)
            e.dma_start(hl[:, 0:HEADS * T], kn.sj_src.rearrange("(p c) k -> p (c k)", p=P)).then_inc(r["ld"], 16)
            e.wait_ge(r["keys_ok"], 1)
            e.dma_start(kn.src_sorted.rearrange("(p c) -> p c", p=P), r["keyrow"][:, :]).then_inc(r["st"], 16)
            e.wait_ge(r["both_ok"], 1)
            e.dma_start(kn.run_ml.rearrange("(p c) k -> p (c k)", p=P), hl).then_inc(r["st"], 16)
            e.wait_ge(r["st"], 32)

        n_carry = 4

        def tensor(e, ch):
            for i in range(n_carry):
                e.wait_ge(r["ends_ok"], i + 1)
                e.transpose(r["pa"][0:HEADS, 0:P], r["ends"][:, 0:HEADS], kn.ident[:, :])
                e.transpose(r["pb"][0:HEADS, 0:P], r["ends"][:, HEADS:2 * HEADS], kn.ident[:, :]).then_inc(r["rows_ok"], 1)
                e.wait_ge(r["carried"], i + 1)
                e.transpose(r["pc"][:, 0:HEADS], r["crow"][0:HEADS, 0:P], kn.ident[0:HEADS, 0:HEADS]
                            ).then_inc(r["back"], 1)

        def vector(e, ch):
            def carry(op0, op1, init):
                i = turns[0]
                turns[0] += 1
                ch.wait()
                e.tensor_copy(r["ends"][:, 0:1], r["ends"][:, 0:1]).then_inc(r["ends_ok"], 1)
                e.wait_ge(r["rows_ok"], i + 1)
                ch(e.tensor_copy(r["arow"][0:HEADS, :], r["pa"][0:HEADS, 0:P]))
                ch(e.memset(r["crow"][0:HEADS, 0:1], init))
                ch.wait()
                e.tensor_tensor_scan(r["crow"][0:HEADS, 1:P + 1], r["arow"][0:HEADS, :], r["pb"][0:HEADS, 0:P], init,
                                     op0, op1).then_inc(r["carried"], 1)
                e.wait_ge(r["back"], i + 1)
                ch(e.tensor_copy(r["carry"][:, :], r["pc"][:, 0:HEADS]))
                ch.wait()

            e.wait_ge(r["ld"], 32)
            ch(e.tensor_scalar(r["cont"][:, :], firsts[:, :, 4], -1.0, 1.0, ALU.mult, ALU.add))
            ch(e.tensor_scalar(r["mask"][:, :], firsts[:, :, 4], NEG, None, ALU.mult))
            ch(e.tensor_reduce(r["any"][:, :], firsts[:, :, 4], AX, ALU.max))
            ch.wait()
            ch(e.tensor_scalar(r["through"][:, :], r["any"][:, :].to_broadcast([P, HEADS]), -1.0, 1.0, ALU.mult, ALU.add))
            ch.wait()
            for rep in range(2):
                for k in range(HEADS):
                    ch(e.tensor_tensor_scan(si[:, k, :], r["cont"][:, :], firsts[:, :, k],
                                            0.0 if rep == 0 else r["carry"][:, k:k + 1], ALU.mult, ALU.add))
                ch.wait()
                if rep == 0:
                    ch(e.tensor_copy(r["ends"][:, 0:HEADS], r["through"][:, :]))
                    ch(e.tensor_copy(r["ends"][:, HEADS:], si[:, :, T - 1]))
                    carry(ALU.mult, ALU.add, 0.0)
            ch(e.memset(r["zeros"][:, :], 0.0))
            ch.wait()
            for rep in range(2):
                ch(e.tensor_tensor_scan(r["keyrow"][:, :], r["zeros"][:, :], firsts[:, :, 5],
                                        0.0 if rep == 0 else r["carry"][:, 0:1], ALU.add, ALU.max))
                ch.wait()
                if rep == 0:
                    ch(e.memset(r["ends"][:, 0:HEADS], 0.0))
                    ch(e.tensor_copy(r["ends"][:, HEADS:], r["keyrow"][:, T - 1:T].to_broadcast([P, HEADS])))
                    carry(ALU.add, ALU.max, 0.0)
            e.tensor_copy(r["carry"][:, 0:1], r["carry"][:, 0:1]).then_inc(r["keys_ok"], 1)
            for k in range(HEADS):
                ch(e.tensor_tensor(r["al"][:, k, :], si[:, k, :], sj[:, :, k], ALU.add))
            ch.wait()
            ch(e.scalar_tensor_tensor(r["al"][:, :, :], r["al"][:, :, :], 0.2, r["al"][:, :, :], ALU.mult, ALU.max))
            ch.wait()
            for rep in range(2):
                for k in range(HEADS):
                    ch(e.tensor_tensor_scan(r["m"][:, k, 1:T + 1], r["mask"][:, :], r["al"][:, k, :],
                                            NEG if rep == 0 else r["carry"][:, k:k + 1], ALU.add, ALU.max))
                ch.wait()
                if rep == 0:
                    ch(e.tensor_scalar(r["ends"][:, 0:HEADS], r["any"][:, :].to_broadcast([P, HEADS]), NEG, None, ALU.mult))
                    ch(e.tensor_copy(r["ends"][:, HEADS:], r["m"][:, :, T]))
                    carry(ALU.add, ALU.max, NEG)
            ch(e.tensor_copy(r["m"][:, :, 0], r["carry"][:, :]))
            ch.wait()
            ch(e.tensor_tensor(d0, r["m"][:, :, 0:T], r["m"][:, :, 1:T + 1], ALU.subtract))
            ch(e.tensor_tensor(d1, r["al"][:, :, :], r["m"][:, :, 1:T + 1], ALU.subtract))
            ch(e.tensor_tensor(r["mm"][:, :], r["m"][:, :, 0], r["m"][:, :, T], ALU.subtract))
            ch.wait()
            ch(e.tensor_scalar(d0, d0, 0.0, None, ALU.min))
            e.tensor_scalar(r["mm"][:, :], r["mm"][:, :], 0.0, None, ALU.min).then_inc(r["diffs"], 1)
            e.wait_ge(r["exps"], 1)
            for k in range(HEADS):
                ch(e.tensor_tensor(d0[:, k, :], d0[:, k, :], r["cont"][:, :], ALU.mult))
            ch(e.tensor_tensor(r["ends"][:, 0:HEADS], r["mm"][:, :], r["through"][:, :], ALU.mult))
            ch.wait()
            for rep in range(2):
                for k in range(HEADS):
                    ch(e.tensor_tensor_scan(r["al"][:, k, :], d0[:, k, :], d1[:, k, :],
                                            0.0 if rep == 0 else r["carry"][:, k:k + 1], ALU.mult, ALU.add))
                ch.wait()
                if rep == 0:
                    ch(e.tensor_copy(r["ends"][:, HEADS:], r["al"][:, :, T - 1]))
                    carry(ALU.mult, ALU.add, 0.0)
            for k in range(HEADS):
                ch(e.tensor_copy(both[:, :, k], r["m"][:, k, 1:T + 1]))
                ins = e.tensor_copy(both[:, :, HEADS + k], r["al"][:, k, :])
                if k < HEADS - 1:
                    ch(ins)
            ins.then_inc(r["both_ok"], 1)

        def scalar(e, ch):
            e.wait_ge(r["diffs"], 1)
            ch(e.activation(d0, d0, ACT.Exp))
            ch(e.activation(d1, d1, ACT.Exp))
            e.activation(r["mm"][:, :], r["mm"][:, :], ACT.Exp).then_inc(r["exps"], 1)
        return dict(sync=sync, tensor=tensor, vector=vector, scalar=scalar)
    phase(kn, "l0g", build, psums=[(n, [P, BANK], F32) for n in ("pa", "pb", "pc")],
               sbufs=[("keyrow", [P, T], F32), ("cont", [P, T], F32), ("mask", [P, T], F32), ("zeros", [P, T], F32),
                      ("any", [P, 1], F32), ("through", [P, HEADS], F32), ("ends", [P, 2 * HEADS], F32),
                      ("arow", [HEADS, P], F32), ("crow", [HEADS, P + 1], F32), ("carry", [P, HEADS], F32),
                      ("mm", [P, HEADS], F32), ("al", [P, HEADS, T], F32), ("m", [P, HEADS, T + 1], F32)],
               sems=["ld", "st", "keys_ok", "both_ok", "ends_ok", "rows_ok", "carried", "back", "diffs", "exps"])

def l0_table(kn):
    kn.by_src = dram(kn, "l0_by_src", (NP, T1W))
    rows = T // 7

    def build(r):
        def sync(e, ch):
            e.dma_start(r["kr"][:, :, :], kn.src_sorted.rearrange("(k t p) -> t k p", p=P, k=7)).then_inc(r["kld"], 16)
            tab = kn.by_src.rearrange("(b p) c -> p b c", p=P)
            e.dma_start(tab[:, :, 0:H], kn.TB[:, :, :]).then_inc(r["st"], 16)
            e.wait_ge(r["small_ok"], 1)
            e.dma_start(tab[:, :, H:T1W], r["small"][:, :, :]).then_inc(r["st"], 16)
            e.wait_ge(r["st"], 32)

        def tensor(e, ch):
            e.wait_ge(r["kld"], 16)
            for k in range(7):
                ins = e.transpose(r["pk"][:, k // 4, (k % 4) * rows:(k % 4 + 1) * rows], r["kr"][:, k, :],
                                  kn.ident[0:rows, 0:rows])
            ins.then_inc(r["turned"], 1)

        def vector(e, ch):
            ch(e.tensor_tensor(r["f"][:, :], kn.start[:, 1, :], kn.count[:, 1, :], ALU.add))
            ch.wait()
            e.tensor_scalar(r["at"][:, :], r["f"][:, :], -1.0, 0.0, ALU.add, ALU.max).then_inc(r["at_ok"], 1)
            e.wait_ge(r["turned"], 1)
            ch(e.tensor_copy(r["key"][:, 0:4 * rows], r["pk"][:, 0, 0:4 * rows]))
            ch(e.tensor_copy(r["key"][:, 4 * rows:], r["pk"][:, 1, 0:3 * rows]))
            ch.wait()


            def pick(st):
                tiles = slot_values(kn, e, kn.slot_regs["vector"], st, 64)
                for j in range(G):
                    col = kn.local[:, 1, bass.ds(st.i * G + j, 1)]
                    ch(e.tensor_tensor(col, r["key"][:, bass.ds(tiles[j], 1)], col, ALU.subtract))
            e.sem_inc(r["keys_ok"], 1)
            run_steps(e, ch, [(pick, 0)], STEPS // 2)
            e.wait_ge(r["got"], 16 * NB)
            sij = kn.sij[:, :].rearrange("p (b k) -> p b k", k=2 * HEADS)
            ch(e.tensor_copy(r["small"][:, :, 0:HEADS], sij[:, :, 0:HEADS]))
            ch(e.tensor_copy(r["small"][:, :, HEADS:2 * HEADS], r["ml"][:, :, 0:HEADS]))
            ch(e.tensor_scalar(r["l"][:, :, :], r["ml"][:, :, HEADS:], 1e-16, None, ALU.add))
            ch.wait()
            e.reciprocal(r["small"][:, :, 2 * HEADS:], r["l"][:, :, :]).then_inc(r["small_ok"], 1)
            ch(e.memset(kn.AC[:, :, :], 0.0))
            ch.wait()

        def scalar(e, ch):
            e.wait_ge(r["keys_ok"], 1)

            def pick(st):
                tiles = slot_values(kn, e, kn.slot_regs["scalar"], st, 64, STEPS // 2)
                for j in range(G):
                    col = kn.local[:, 1, bass.ds(st.i * G + j + SLOTS // 2, 1)]
                    ch(e.activation(col, col, ACT.Identity, bias=r["key"][:, bass.ds(tiles[j], 1)], scale=-1.0))
            run_steps(e, ch, [(pick, 0)], STEPS // 2)
            ch.wait()

        def gpsimd(e, ch):
            e.wait_ge(r["at_ok"], 1)
            for b in range(NB):
                e.indirect_dma_start(r["ml"][:, b, :], None, kn.run_ml[:, :],
                                     bass.IndirectOffsetOnAxis(ap=r["at"][:, b:b + 1], axis=0), bounds_check=EP - 1
                                     ).then_inc(r["got"], 16)
            e.wait_ge(r["got"], 16 * NB)
        return dict(sync=sync, tensor=tensor, vector=vector, scalar=scalar, gpsimd=gpsimd)
    phase(kn, "l0t", build, psums=[("pk", [P, 2, BANK], F32)],
               sbufs=[("kr", [rows, 7, P], F32), ("key", [P, T], F32), ("f", [P, NB], F32), ("at", [P, NB], I32),
                      ("ml", [P, NB, 2 * HEADS], F32), ("l", [P, NB, HEADS], F32), ("small", [P, NB, 3 * HEADS], F32)],
               sems=["kld", "st", "small_ok", "turned", "keys_ok", "at_ok", "got"])

def gather_stage(kn, e, r, table, width, used):
    def gather(st):
        wait_step(e, r["idx_ok"], st)
        wait_step(e, used, st, 2)
        take_waits(e, kn.tally)
        for j in range(G):
            e.indirect_dma_start(r["rows"][:, st.par, j, 0:width], None, table[:, :],
                                 bass.IndirectOffsetOnAxis(ap=r["idx"][:, st.par, j:j + 1], axis=0),
                                 bounds_check=NP - 1).then_inc(r["got"][st.par], 16)
    return gather

def idx_stage(kn, e, r, columns, sems, n=G):
    def idx(st):
        wait_free(e, r[sems], st, n)
        e.tensor_copy(r["idx"][:, st.par, :], columns[:, bass.ds(st.i * G, G)]).then_inc(r["idx_ok"], 1)
    return idx

def l0_edges(kn):
    def build(r):
        def gpsimd(e, ch):
            run_steps(e, ch, [(gather_stage(kn, e, r, kn.by_src, T1W, r["msg_ok"]), 0)], STEPS)

        def vector(e, ch):
            idx = idx_stage(kn, e, r, kn.src_of, "got")
            hot = hot_stage(kn, e, r, 0, r["summed"])

            def alpha(st):
                wait_load(e, r["got"], st, G)
                a, rows = r["a"][:, st.par, :, :], r["rows"][:, st.par, :, :]
                sj = kn.slot_sj[:, bass.ds(st.i * G * HEADS, G * HEADS)].rearrange("p (j k) -> p j k", k=HEADS)
                ch.wait()
                ch(e.tensor_tensor(a, rows[:, :, H:H + HEADS], sj, ALU.add))
                ch.wait()
                ch(e.scalar_tensor_tensor(a, a, 0.2, a, ALU.mult, ALU.max))
                ch.wait()
                e.tensor_tensor(a, a, rows[:, :, H + HEADS:H + 2 * HEADS], ALU.subtract).then_inc(r["a_ok"], 1)

            def msg(st):
                wait_step(e, r["exp_ok"], st)
                wait_step(e, r["summed"], st, 2)
                a, rows = r["a"][:, st.par, :, :], r["rows"][:, st.par, :, :]
                ch(e.tensor_tensor(a, a, rows[:, :, H + 2 * HEADS:T1W], ALU.mult))
                ch.wait()
                e.tensor_tensor(r["msg"][:, st.par, :, :].rearrange("p j (k c) -> p j k c", k=HEADS),
                                rows[:, :, 0:H].rearrange("p j (k c) -> p j k c", k=HEADS),
                                a.unsqueeze(3).to_broadcast([P, G, HEADS, H // HEADS]), ALU.mult
                                ).then_inc(r["msg_ok"], 1)
            run_steps(e, ch, [(idx, 0), (hot, 0), (alpha, 1), (msg, 1), (add_stage(kn, e, ch, r, 0), 2)], STEPS)

        def scalar(e, ch):
            def exp(st):
                wait_step(e, r["a_ok"], st)
                e.activation(r["a"][:, st.par, :, :], r["a"][:, st.par, :, :], ACT.Exp).then_inc(r["exp_ok"], 1)
            run_steps(e, ch, [(exp, 0)], STEPS)

        def tensor(e, ch):
            def add(st):
                wait_step(e, r["hot"], st)
                wait_step(e, r["msg_ok"], st)
                wait_step(e, r["added"], st, 2)
                for j in range(G):
                    ins = e.matmul(r["pR"][:, st.par, j, :], r["oh"][:, st.par, j, :], r["msg"][:, st.par, j, :],
                                   start=True, stop=True)
                ins.then_inc(r["summed"], 1)
            run_steps(e, ch, [(add, 0)], STEPS)
        return dict(gpsimd=gpsimd, vector=vector, scalar=scalar, tensor=tensor)
    phase(kn, "l0e", build, psums=[("pR", [P, 2, G, P], F32)],
               sbufs=[("rows", [P, 2, G, T1W], F32), ("oh", [P, 2, G, P], F32), ("msg", [P, 2, G, H], F32),
                      ("a", [P, 2, G, HEADS], F32), ("idx", [P, 2, G], I32)],
               sems=["idx_ok", "hot", "a_ok", "exp_ok", "msg_ok", "summed", "added"], pairs=["got"])

def l0_close(kn):
    def build(r):
        def vector(e, ch):
            ch(e.tensor_scalar(r["none"][:, :], kn.count[:, 0, :], 0.0, None, ALU.is_equal))
            ch.wait()

            def add(st):
                x, xl, acc = (block(kn, t, st.i) for t in (kn.X, kn.TB, kn.AC))
                ch(e.scalar_tensor_tensor(acc, xl, r["none"][:, bass.ds(st.i, 1)], acc, ALU.mult, ALU.add))
                ch.wait()
                ch(e.tensor_tensor(x, x, acc, ALU.add))
            run_steps(e, ch, [(add, 0)], NB)
            ch.wait()
        return dict(vector=vector)
    phase(kn, "l0c", build, sbufs=[("none", [P, NB], F32)])

def log_part(kn, e, ch, out, src, bias=None):
    ch(e.activation(out, src, ACT.Abs, **({} if bias is None else {"bias": bias})))
    ch.wait()
    ch(e.activation(out, out, ACT.Exp, scale=-1.0))
    ch.wait()
    return e.activation(out, out, ACT.Ln, bias=kn.half1[:, 0:1], scale=0.5)

def fetch_stage(kn, e, r, src, name="fetched", buf="hb", used="turned"):
    def fetch(st):
        wait_step(e, r[used], st, 2)
        e.activation(r[buf][:, st.par, :], block(kn, src, st.i), ACT.Copy).then_inc(r[name], 1)
    return fetch

def l1_nodes(kn):
    def build(r):
        def tensor(e, ch):
            def turn(st):
                wait_step(e, r["fetched"], st)
                wait_step(e, r["xa_ok"], st, 2)
                e.transpose(r["pA"][:, st.par, 0:P], r["hb"][:, st.par, :], kn.ident[:, :]).then_inc(r["turned"], 1)

            def lin(st):
                wait_step(e, r["xa_ok"], st)
                wait_step(e, r["xi_ok"], st, 2)
                wait_step(e, r["y_ok"], st, 2)
                e.matmul(r["pB"][:, st.par, 0:P], mat(kn, "Wi"), r["xa"][:, st.par, :], start=True, stop=True)
                e.matmul(r["pC"][:, st.par, 0:P], r["xa"][:, st.par, :], mat(kn, "Wj"), start=True, stop=True
                         ).then_inc(r["lin_ok"], 1)
            run_steps(e, ch, [(turn, 0), (lin, 1)], NB)

        def scalar(e, ch):
            def part_a(st):
                wait_step(e, r["turned"], st)
                wait_step(e, r["xa_ok"], st, 2)
                log_part(kn, e, ch, r["la"][:, st.par, :], r["pA"][:, st.par, 0:P]).then_inc(r["la_ok"], 1)

            def part_b(st):
                wait_step(e, r["lin_ok"], st)
                wait_step(e, r["xi_ok"], st, 2)
                log_part(kn, e, ch, r["lb"][:, st.par, :], r["pB"][:, st.par, 0:P], vec(kn, "bi")).then_inc(r["lb_ok"], 1)

            def part_c(st):
                wait_step(e, r["y_ok"], st)
                wait_step(e, r["xj_ok"], st, 2)
                log_part(kn, e, ch, r["lc"][:, st.par, :], r["y"][:, st.par, :]).then_inc(r["lc_ok"], 1)
            run_steps(e, ch, [(fetch_stage(kn, e, r, kn.Hn), 0), (part_a, 0), (part_b, 1), (part_c, 1)], NB)

        def vector(e, ch):
            def xa(st):
                wait_step(e, r["la_ok"], st)
                wait_step(e, r["lin_ok"], st, 2)
                ch(e.tensor_copy(block(kn, kn.Hn, st.i), r["pA"][:, st.par, 0:P]))
                e.scalar_tensor_tensor(r["xa"][:, st.par, :], r["pA"][:, st.par, 0:P], 0.0, r["la"][:, st.par, :],
                                       ALU.max, ALU.add).then_inc(r["xa_ok"], 1)

            def y(st):
                wait_step(e, r["lin_ok"], st)
                wait_step(e, r["xj_ok"], st, 2)
                e.tensor_tensor(r["y"][:, st.par, :], r["pC"][:, st.par, 0:P], row(kn, "bj"), ALU.add
                                ).then_inc(r["y_ok"], 1)

            def xi(st):
                wait_step(e, r["lb_ok"], st)
                wait_step(e, r["xi_ok"], st, 2)
                ch(e.tensor_scalar(r["t"][:, st.par, :], r["pB"][:, st.par, 0:P], vec(kn, "bi"), 0.0, ALU.add, ALU.max))
                ch.wait()
                e.tensor_tensor(block(kn, kn.AC, st.i), r["t"][:, st.par, :], r["lb"][:, st.par, :], ALU.add
                                ).then_inc(r["xi_ok"], 1)

            def xj(st):
                wait_step(e, r["lc_ok"], st)
                e.scalar_tensor_tensor(block(kn, kn.TB, st.i), r["y"][:, st.par, :], 0.0, r["lc"][:, st.par, :],
                                       ALU.max, ALU.add).then_inc(r["xj_ok"], 1)
            run_steps(e, ch, [(xa, 0), (y, 1), (xi, 1), (xj, 1)], NB)
        return dict(tensor=tensor, scalar=scalar, vector=vector)
    phase(kn, "l1n", build, psums=[(n, [P, 2, BANK], F32) for n in ("pA", "pB", "pC")],
               sbufs=[(n, [P, 2, P], F32) for n in ("hb", "la", "lb", "lc", "xa", "y", "t")],
               sems=["fetched", "turned", "xa_ok", "xi_ok", "xj_ok", "y_ok", "lin_ok", "la_ok", "lb_ok", "lc_ok"])

def load_records(kn, e, r, column, width, used):

    def load(st):
        tiles = slot_values(kn, e, kn.slot_regs["sync"], st, 0)
        wait_step(e, used, st, 2)
        for j in range(G):
            e.dma_start(r["rec"][:, st.par, j, 0:width], kn.sorted[bass.ds(tiles[j] * P, P), column:column + width]
                        ).then_inc(r["ld"][st.par], 16)
    return load

def scatter_stage(kn, e, r):
    def send(st):
        wait_step(e, r["prod_ok"], st)
        wait_step(e, r["idx_ok"], st)
        take_waits(e, kn.tally)
        for j in range(G):
            e.indirect_dma_start(kn.products[:, :],
                                 bass.IndirectOffsetOnAxis(ap=r["idx"][:, st.par, j:j + 1], axis=0),
                                 r["prod"][:, st.par, j, :], None, bounds_check=EP - 1, oob_is_err=False
                                 ).then_inc(r["sent"][st.par], 16)
    return send

def scatter_all(kn, e, ch, r):
    run_steps(e, ch, [(scatter_stage(kn, e, r), 0)], STEPS)
    for j in range(2):
        e.wait_ge(r["sent"][j], 16 * G * (STEPS // 2))

def l1_edges(kn):
    def build(r):
        def sync(e, ch):
            run_steps(e, ch, [(load_records(kn, e, r, C64, A64, r["rec_turned"]), 0)], STEPS)

        def tensor(e, ch):
            turn_hot = turn_hot_stage(kn, e, r, ident=kn.identb)

            def turn_rec(st):
                wait_load(e, r["ld"], st, G)
                wait_step(e, r["dT_ok"], st, 2)
                take_waits(e, kn.tally)
                for j in range(G):
                    ins = e.transpose(r["pD"][0:A64, st.par, j, :], r["rec"][:, st.par, j, :], kn.ident[:, :])
                ins.then_inc(r["rec_turned"], 1)


            def mults(st):
                blocks = slot_values(kn, e, kn.slot_regs["tensor"], st, 32)
                wait_step(e, r["dT_ok"], st)
                wait_step(e, r["g_ok"], st, 2)
                for j in range(G):
                    ins = e.matmul(r["pG"][:, st.par, j, :], r["dT"][0:A64, st.par, j, :], mat(kn, "Wdesc", A64),
                                   start=True, stop=True)
                ins.then_inc(r["g_done"], 1)
                wait_step(e, r["ohT_ok"], st)
                wait_step(e, r["prod_ok"], st, 2)
                for j in range(G):
                    ins = e.matmul(r["pX"][:, st.par, j, :], r["ohT"][:, st.par, j, :], block(kn, kn.TB, blocks[j]),
                                   start=True, stop=True)
                ins.then_inc(r["picked"], 1)
            run_steps(e, ch, [(turn_rec, 0), (turn_hot, 0), (mults, 1)], STEPS)

        def scalar(e, ch):
            def copy_rec(st):
                wait_step(e, r["rec_turned"], st)
                wait_step(e, r["g_done"], st, 2)
                e.activation(r["dT"][0:A64, st.par, :, :], r["pD"][0:A64, st.par, :, :], ACT.Copy).then_inc(r["dT_ok"], 1)

            def copy_g(st):
                wait_step(e, r["g_done"], st)
                wait_step(e, r["prod_ok"], st, 2)
                e.activation(r["g"][:, st.par, :, :], r["pG"][:, st.par, :, :], ACT.Copy).then_inc(r["g_ok"], 1)
            run_steps(e, ch, [(copy_rec, 0), (copy_hot_stage(kn, e, r, r["picked"]), 0), (copy_g, 1)], STEPS)

        def vector(e, ch):
            def prod(st):
                wait_step(e, r["g_ok"], st)
                wait_step(e, r["picked"], st)
                wait_free(e, r["sent"], st, G)
                e.tensor_tensor(r["prod"][:, st.par, :, :], r["g"][:, st.par, :, :], r["pX"][:, st.par, :, :], ALU.mult
                                ).then_inc(r["prod_ok"], 1)
            run_steps(e, ch, [(hot_stage(kn, e, r, 0, r["turned"], iota=kn.iotab), 0), (prod, 1),
                              (idx_stage(kn, e, r, kn.place, "sent"), 1)], STEPS)

        def gpsimd(e, ch):
            scatter_all(kn, e, ch, r)
        return dict(sync=sync, tensor=tensor, scalar=scalar, vector=vector, gpsimd=gpsimd)
    phase(kn, "l1e", build, psums=[("pT", [P, 2, 2 * G, P], BF16)] + [(n, [P, 2, G, P], F32) for n in ("pD", "pG", "pX")],
               sbufs=[("rec", [P, 2, G, A64], F32), ("oh", [P, 2, G, P], BF16), ("ohT", [P, 2, G, P], F32),
                      ("dT", [A64, 2, G, P], F32), ("g", [P, 2, G, P], F32), ("prod", [P, 2, G, P], F32),
                      ("idx", [P, 2, G], I32)],
               sems=["hot", "turned", "ohT_ok", "rec_turned", "dT_ok", "g_done", "g_ok", "picked", "prod_ok", "idx_ok"],
               pairs=["ld", "sent"])

def sum_by_src(kn, name, clear=False):
    def rows(st, j):
        return flat(kn, kn.MT)[:, bass.ds((st.quad * G + j) * P, P)]

    def build(r):
        def sync(e, ch):
            def load(st):
                tiles = slot_values(kn, e, kn.slot_regs["sync"], st, 64)
                wait_step(e, r["summed"], st, 4)
                for j in range(G):
                    e.dma_start(rows(st, j), kn.products[bass.ds(tiles[j] * P, P), :]).then_inc(r[f"ld{st.quad}"], 16)
            run_steps(e, ch, [(load, 0)], STEPS, RING)

        def vector(e, ch):
            if clear:
                ch(e.memset(kn.AC[:, :, :], 0.0))
            run_steps(e, ch, [(hot_stage(kn, e, r, 1, r["summed"]), 0), (add_stage(kn, e, ch, r, 1), 2)], STEPS)

        def tensor(e, ch):
            def add(st):
                wait_step(e, r["hot"], st)
                e.wait_ge(r[f"ld{st.quad}"], st.fourth * (16 * G) + 16 * G)
                wait_step(e, r["added"], st, 2)
                for j in range(G):
                    ins = e.matmul(r["pR"][:, st.par, j, :], rows(st, j), r["oh"][:, st.par, j, :],
                                   start=True, stop=True)
                ins.then_inc(r["summed"], 1)
            run_steps(e, ch, [(add, 0)], STEPS, RING)
        return dict(sync=sync, vector=vector, tensor=tensor)
    phase(kn, name, build, psums=[("pR", [P, 2, G, P], F32)],
               sbufs=[("oh", [P, 2, G, P], F32)],
               sems=["hot", "summed", "added", "ld0", "ld1", "ld2", "ld3"])

def sec(kn, t, st):
    return flat(kn, t)[:, bass.ds(st.i * SEC, SEC)]

def ssp_all(kn, name, dst, src):
    def build(r):
        def scalar(e, ch):
            def part(st):
                wait_step(e, r["done"], st, 2)
                log_part(kn, e, ch, r["l"][:, st.par, :], sec(kn, src, st)).then_inc(r["l_ok"], 1)
            run_steps(e, ch, [(part, 0)], NSEC)

        def vector(e, ch):
            def whole(st):
                wait_step(e, r["l_ok"], st)
                e.scalar_tensor_tensor(sec(kn, dst, st), sec(kn, src, st), 0.0, r["l"][:, st.par, :], ALU.max, ALU.add
                                       ).then_inc(r["done"], 1)
            run_steps(e, ch, [(whole, 0)], NSEC)
            e.wait_ge(r["done"], NSEC)
        return dict(scalar=scalar, vector=vector)
    phase(kn, name, build, sbufs=[("l", [P, 2, SEC], F32)], sems=["l_ok", "done"])

def linear_ssp(kn, name, dst, src, w, b):
    def build(r):
        def tensor(e, ch):
            def lin(st):
                wait_step(e, r["done"], st, 2)
                e.matmul(r["p"][:, st.par, 0:SEC], mat(kn, w), sec(kn, src, st), start=True, stop=True
                         ).then_inc(r["lin_ok"], 1)
            run_steps(e, ch, [(lin, 0)], NSEC)

        def scalar(e, ch):
            def part(st):
                wait_step(e, r["lin_ok"], st)
                wait_step(e, r["done"], st, 2)
                log_part(kn, e, ch, r["l"][:, st.par, :], r["p"][:, st.par, 0:SEC], vec(kn, b)).then_inc(r["l_ok"], 1)
            run_steps(e, ch, [(part, 0)], NSEC)

        def vector(e, ch):
            def whole(st):
                wait_step(e, r["l_ok"], st)
                wait_step(e, r["done"], st, 2)
                ch(e.tensor_scalar(r["t"][:, st.par, :], r["p"][:, st.par, 0:SEC], vec(kn, b), 0.0, ALU.add, ALU.max))
                ch.wait()
                e.tensor_tensor(sec(kn, dst, st), r["t"][:, st.par, :], r["l"][:, st.par, :], ALU.add
                                ).then_inc(r["done"], 1)
            run_steps(e, ch, [(whole, 0)], NSEC)
            e.wait_ge(r["done"], NSEC)
        return dict(tensor=tensor, scalar=scalar, vector=vector)
    phase(kn, name, build, psums=[("p", [P, 2, BANK], F32)], sbufs=[("l", [P, 2, SEC], F32), ("t", [P, 2, SEC], F32)],
               sems=["lin_ok", "l_ok", "done"])

def linear_add(kn, name, dst, src, w, b, scale=None):
    def build(r):
        def tensor(e, ch):
            def lin(st):
                wait_step(e, r["done"], st, 2)
                e.matmul(r["p"][:, st.par, 0:SEC], mat(kn, w), sec(kn, src, st), start=True, stop=True
                         ).then_inc(r["lin_ok"], 1)
            run_steps(e, ch, [(lin, 0)], NSEC)

        def vector(e, ch):
            def add(st):
                d = sec(kn, dst, st)
                if scale is not None:
                    ch(e.tensor_scalar(d, d, vec(kn, scale), None, ALU.mult))
                    ch.wait()
                wait_step(e, r["lin_ok"], st)
                e.scalar_tensor_tensor(d, r["p"][:, st.par, 0:SEC], vec(kn, b), d, ALU.add, ALU.add
                                       ).then_inc(r["done"], 1)
            run_steps(e, ch, [(add, 0)], NSEC)
            e.wait_ge(r["done"], NSEC)
        return dict(tensor=tensor, vector=vector)
    phase(kn, name, build, psums=[("p", [P, 2, BANK], F32)], sems=["lin_ok", "done"])

def residual(kn, name, m, w1, b1, w2, b2):
    ssp_all(kn, name + "y", kn.MT, m)
    linear_ssp(kn, name + "h", kn.TB, kn.MT, w1, b1)
    linear_add(kn, name + "m", m, kn.TB, w2, b2)

def l1_layers(kn):
    for k in range(3):
        residual(kn, f"ri{k}", kn.AC, f"Wri1_{k}", f"bri1_{k}", f"Wri2_{k}", f"bri2_{k}")
    ssp_all(kn, "msg", kn.MT, kn.AC)
    linear_add(kn, "dense", kn.Hn, kn.MT, "Wd", "bd", "u")
    for k in range(2):
        residual(kn, f"ra{k}", kn.Hn, f"Wra1_{k}", f"bra1_{k}", f"Wra2_{k}", f"bra2_{k}")

def add_turned(kn, name, src, also=None):
    def build(r):
        def scalar(e, ch):
            run_steps(e, ch, [(fetch_stage(kn, e, r, src), 0)], NB)

        def tensor(e, ch):
            def turn(st):
                wait_step(e, r["fetched"], st)
                wait_step(e, r["added"], st, 2)
                e.transpose(r["pA"][:, st.par, 0:P], r["hb"][:, st.par, :], kn.ident[:, :]).then_inc(r["turned"], 1)
            run_steps(e, ch, [(turn, 0)], NB)

        def vector(e, ch):
            def add(st):
                x = block(kn, kn.X, st.i)
                if also is not None:
                    ch(e.tensor_tensor(x, x, block(kn, also, st.i), ALU.add))
                    ch.wait()
                wait_step(e, r["turned"], st)
                e.tensor_tensor(x, x, r["pA"][:, st.par, 0:P], ALU.add).then_inc(r["added"], 1)
            run_steps(e, ch, [(add, 0)], NB)
            ch(e.memset(kn.AC[:, :, :], 0.0))
            ch.wait()
            e.wait_ge(r["added"], NB)
        return dict(scalar=scalar, tensor=tensor, vector=vector)
    phase(kn, name, build, psums=[("pA", [P, 2, BANK], F32)], sbufs=[("hb", [P, 2, P], F32)],
               sems=["fetched", "turned", "added"])

def tables(kn, name, w_table, w_rows=None, bias=None, rows=None):
    def build(r):
        def tensor(e, ch):
            def turn(st):
                wait_step(e, r["fetched"], st)
                wait_step(e, r["hT_ok"], st, 2)
                e.transpose(r["pA"][:, st.par, 0:P], r["hb"][:, st.par, :], kn.ident[:, :]).then_inc(r["turned"], 1)

            def lin(st):
                wait_step(e, r["hT_ok"], st)
                wait_step(e, r["tab_ok"], st, 2)
                if w_rows:
                    e.matmul(r["pC"][:, st.par, 0:P], r["hT"][:, st.par, :], mat(kn, w_rows), start=True, stop=True)
                e.matmul(r["pB"][:, st.par, 0:P], r["hT"][:, st.par, :], mat(kn, w_table), start=True, stop=True
                         ).then_inc(r["lin_ok"], 1)
            run_steps(e, ch, [(turn, 0), (lin, 1)], NB)

        def scalar(e, ch):
            def copy(st):
                wait_step(e, r["turned"], st)
                wait_step(e, r["lin_ok"], st, 2)
                e.activation(r["hT"][:, st.par, :], r["pA"][:, st.par, 0:P], ACT.Copy).then_inc(r["hT_ok"], 1)
            run_steps(e, ch, [(fetch_stage(kn, e, r, kn.Hn), 0), (copy, 0)], NB)

        def vector(e, ch):
            def out(st):
                wait_step(e, r["lin_ok"], st)
                if w_rows:
                    wait_free(e, r["st"], st, 1)
                    ch(e.tensor_tensor(r["a"][:, st.par, :], r["pC"][:, st.par, 0:P], row(kn, bias), ALU.add))
                e.tensor_copy(block(kn, kn.TB, st.i), r["pB"][:, st.par, 0:P]).then_inc(r["tab_ok"], 1)
            run_steps(e, ch, [(out, 0)], NB)
            e.wait_ge(r["tab_ok"], NB)

        def sync(e, ch):
            def store(st):
                wait_step(e, r["tab_ok"], st)
                e.dma_start(rows[bass.ds(st.i * P, P), :], r["a"][:, st.par, :]).then_inc(r["st"][st.par], 16)
            run_steps(e, ch, [(store, 0)], NB)
            e.wait_ge(r["st"][0], 16 * (NB - NB // 2))
            e.wait_ge(r["st"][1], 16 * (NB // 2))
        d = dict(tensor=tensor, scalar=scalar, vector=vector)
        if w_rows:
            d["sync"] = sync
        return d
    phase(kn, name, build, psums=[(n, [P, 2, BANK], F32) for n in ("pA", "pB", "pC")],
               sbufs=[(n, [P, 2, P], F32) for n in ("hb", "hT", "a")],
               sems=["fetched", "turned", "hT_ok", "lin_ok", "tab_ok"], pairs=["st"])

def l2_edges(kn):
    def one_hot(st, j):
        return flat(kn, kn.MT)[:, bass.ds((st.ring * G + j) * P, P)]

    def build(r):
        def gpsimd(e, ch):
            def gather(st):
                wait_step(e, r["idx_ok"], st)
                wait_step(e, r["v_ok"], st, 4)
                take_waits(e, kn.tally)
                for j in range(G):
                    e.indirect_dma_start(r["rows"][:, st.quad, j, :], None, kn.l2_rows[:, :],
                                         bass.IndirectOffsetOnAxis(ap=r["idx"][:, st.par, j:j + 1], axis=0),
                                         bounds_check=NP - 1).then_inc(r["got"][st.par], 16)
            run_steps(e, ch, [(gather, 0)], STEPS, RING)

        def tensor(e, ch):
            def turn(st):
                wait_step(e, r["hot"], st)
                wait_step(e, r["ohT_ok"], st, 2)
                for j in range(G):
                    ins = e.transpose(r["pT"][:, st.par, j, :], one_hot(st, j), kn.ident[:, :])
                ins.then_inc(r["turned"], 1)

            def v(st):
                blocks = slot_values(kn, e, kn.slot_regs["tensor"], st, 32)
                wait_load(e, r["got"], st, G)
                wait_step(e, r["normed"], st, 4)
                e.matmul(r["pV"][:, st.quad, :, :].rearrange("p j c -> p (j c)"), kn.ident[:, :],
                         r["rows"][:, st.quad, :, :].rearrange("p j c -> p (j c)"), start=True, stop=False,
                         skip_group_check=True)
                wait_step(e, r["ohT_ok"], st)
                for j in range(G):
                    ins = e.matmul(r["pV"][:, st.quad, j, :], r["ohT"][:, st.par, j, :], block(kn, kn.TB, blocks[j]),
                                   start=False, stop=(j == G - 1), skip_group_check=True)
                ins.then_inc(r["v_ok"], 1)

            def add(st):
                wait_step(e, r["z_ok"], st)
                wait_step(e, r["added"], st, 2)
                for j in range(G):
                    ins = e.matmul(r["pR"][:, st.par, j, :], one_hot(st, j), r["z"][:, st.quad, j, :],
                                   start=True, stop=True)
                ins.then_inc(r["summed"], 1)
            run_steps(e, ch, [(turn, 1), (v, 2), (add, 6)], STEPS, RING)

        def scalar(e, ch):
            def root(st):
                wait_step(e, r["stats"], st)
                e.activation(r["std"][:, st.par, :], r["mv"][:, st.par, :, 1], ACT.Sqrt, bias=kn.eps1[:, 0:1]
                             ).then_inc(r["std_ok"], 1)

            def norm(st):
                wait_step(e, r["scales"], st)
                wait_step(e, r["summed"], st, 4)
                for j in range(G):
                    ins = e.activation(r["z"][:, st.quad, j, :], r["pV"][:, st.quad, j, :], ACT.Identity,
                                       bias=r["shift"][:, st.par, j:j + 1], scale=r["rstd"][:, st.par, j:j + 1])
                ins.then_inc(r["normed"], 1)
            run_steps(e, ch, [(copy_hot_stage(kn, e, r, r["v_ok"]), 1), (root, 3), (norm, 4)], STEPS, RING)

        def vector(e, ch):
            def hot(st):
                wait_step(e, r["summed"], st, RING)
                for j in range(G):
                    ins = e.tensor_scalar(one_hot(st, j), kn.iota[:, :], kn.local[:, 0, bass.ds(st.i * G + j, 1)], None,
                                          ALU.is_equal)
                ins.then_inc(r["hot"], 1)

            def stats(st):
                wait_step(e, r["v_ok"], st)
                wait_step(e, r["normed"], st, 2)
                ch.wait()
                for j in range(G):
                    ch(e.bn_stats(r["six"][:, st.par, j, :], r["pV"][:, st.quad, j, :]))
                ch.wait()
                take_waits(e, kn.tally)
                for j in range(G):
                    ins = e.bn_aggr(r["mv"][:, st.par, j, :], r["six"][:, st.par, j, :])
                    if j < G - 1:
                        ch(ins)
                ins.then_inc(r["stats"], 1)

            def scales(st):
                wait_step(e, r["std_ok"], st)
                wait_step(e, r["normed"], st, 2)
                ch(e.reciprocal(r["rstd"][:, st.par, :], r["std"][:, st.par, :]))
                ch.wait()
                e.scalar_tensor_tensor(r["shift"][:, st.par, :], r["mv"][:, st.par, :, 0], -1.0, r["rstd"][:, st.par, :],
                                       ALU.mult, ALU.mult).then_inc(r["scales"], 1)

            def act(st):
                wait_step(e, r["normed"], st)
                z = r["z"][:, st.quad, :, :]
                ch(e.tensor_tensor(z, z, row(kn, "msg_g").unsqueeze(1).to_broadcast([P, G, H]), ALU.mult))
                ch.wait()
                ch(e.tensor_tensor(z, z, row(kn, "msg_beta").unsqueeze(1).to_broadcast([P, G, H]), ALU.add))
                ch.wait()
                for j in range(G):
                    ins = e.tensor_scalar(r["z"][:, st.quad, j, :], r["z"][:, st.quad, j, :], 0.0,
                                          kn.wt[:, bass.ds(st.i * G + j, 1)], ALU.max, ALU.mult)
                ins.then_inc(r["z_ok"], 1)
            run_steps(e, ch, [(scales, 4), (hot, 0), (stats, 3), (act, 5), (idx_stage(kn, e, r, kn.src_of, "got"), 0),
                              (add_stage(kn, e, ch, r, 0), 7)], STEPS, RING)
        return dict(gpsimd=gpsimd, tensor=tensor, scalar=scalar, vector=vector)
    phase(kn, "l2e", build, psums=[("pT", [P, 2, G, P], F32), ("pV", [P, 4, G, P], F32), ("pR", [P, 2, G, P], F32)],
               sbufs=[("rows", [P, 4, G, H], F32), ("ohT", [P, 2, G, P], F32),
                      ("z", [P, 4, G, H], F32), ("six", [P, 2, G, 6], F32), ("mv", [P, 2, G, 2], F32),
                      ("std", [P, 2, G], F32), ("rstd", [P, 2, G], F32), ("shift", [P, 2, G], F32), ("idx", [P, 2, G], I32)],
               sems=["idx_ok", "hot", "turned", "ohT_ok", "v_ok", "stats", "std_ok", "scales", "normed", "z_ok",
                     "summed", "added"], pairs=["got"])

def l2_update(kn):
    def build(r):
        def vector(e, ch):
            ch(e.tensor_scalar(r["f"][:, :], kn.count[:, 0, :], 1e-8, None, ALU.add))
            ch(e.tensor_scalar(r["valid"][:, :], kn.count[:, 0, :], 0.0, None, ALU.is_gt))
            ch.wait()
            ch(e.reciprocal(r["f"][:, :], r["f"][:, :]))
            ch.wait()
            ch(e.tensor_tensor(r["f"][:, :], r["f"][:, :], r["valid"][:, :], ALU.mult))
            ch.wait()

            def mean(st):
                wait_step(e, r["turned"], st, 2)
                e.tensor_scalar(r["mb"][:, st.par, :], block(kn, kn.AC, st.i), r["f"][:, bass.ds(st.i, 1)], None,
                                ALU.mult).then_inc(r["mean_ok"], 1)

            def out(st):
                wait_step(e, r["lin_ok"], st)
                e.tensor_tensor(block(kn, kn.TB, st.i), r["pC"][:, st.par, 0:P], row(kn, "upd_b"), ALU.add
                                ).then_inc(r["out_ok"], 1)
            run_steps(e, ch, [(mean, 0), (out, 1)], NB)
            e.wait_ge(r["out_ok"], NB)

        def tensor(e, ch):
            def turn(st):
                wait_step(e, r["fetched"], st)
                wait_step(e, r["mean_ok"], st)
                wait_step(e, r["T_ok"], st, 2)
                e.transpose(r["pA"][:, st.par, 0:P], r["hb"][:, st.par, :], kn.ident[:, :])
                e.transpose(r["pA"][:, st.par, P:2 * P], r["mb"][:, st.par, :], kn.ident[:, :]).then_inc(r["turned"], 1)

            def lin(st):
                wait_step(e, r["T_ok"], st)
                wait_step(e, r["out_ok"], st, 2)
                e.matmul(r["pC"][:, st.par, 0:P], r["T"][:, st.par, 0:P], mat(kn, "upd_top"), start=True, stop=False)
                e.matmul(r["pC"][:, st.par, 0:P], r["T"][:, st.par, P:2 * P], mat(kn, "upd_bottom"), start=False,
                         stop=True).then_inc(r["lin_ok"], 1)
            run_steps(e, ch, [(turn, 0), (lin, 1)], NB)

        def scalar(e, ch):
            def copy(st):
                wait_step(e, r["turned"], st)
                wait_step(e, r["lin_ok"], st, 2)
                e.activation(r["T"][:, st.par, :], r["pA"][:, st.par, 0:2 * P], ACT.Copy).then_inc(r["T_ok"], 1)
            run_steps(e, ch, [(fetch_stage(kn, e, r, kn.Hn), 0), (copy, 0)], NB)
        return dict(vector=vector, tensor=tensor, scalar=scalar)
    phase(kn, "l2u", build, psums=[(n, [P, 2, BANK], F32) for n in ("pA", "pC")],
               sbufs=[("hb", [P, 2, P], F32), ("mb", [P, 2, P], F32), ("T", [P, 2, 2 * P], F32), ("f", [P, NB], F32),
                      ("valid", [P, NB], F32)],
               sems=["fetched", "mean_ok", "turned", "T_ok", "lin_ok", "out_ok"])

def l2_close(kn):
    X, Hn, MT, AC = (t[:, :, :] for t in (kn.X, kn.Hn, kn.MT, kn.AC))

    def over(name):
        return row(kn, name).unsqueeze(1).to_broadcast([P, NB, H])

    def build(r):
        def vector(e, ch):
            ch(e.tensor_tensor(AC, Hn, over("gate_w"), ALU.mult))
            ch(e.tensor_tensor(MT, MT, over("upd_g"), ALU.mult))
            ch(e.tensor_tensor(X, X, Hn, ALU.add))
            ch.wait()
            ch(e.tensor_reduce(r["z"][:, :], AC, AX, ALU.add))
            ch(e.tensor_tensor(MT, MT, over("upd_beta"), ALU.add))
            ch.wait()
            e.tensor_scalar(r["z"][:, :], r["z"][:, :], row(kn, "gate_b")[:, 0:1], None, ALU.add).then_inc(r["z_ok"], 1)
            ch(e.scalar_tensor_tensor(MT, MT, 0.0, Hn, ALU.max, ALU.subtract))
            e.wait_ge(r["exp_ok"], 1)
            ch(e.tensor_scalar(r["z"][:, :], r["z"][:, :], 1.0, None, ALU.add))
            ch.wait()
            ch(e.reciprocal(r["g"][:, :], r["z"][:, :]))
            ch.wait()
            ch(e.tensor_tensor(MT, MT, r["g"][:, :].unsqueeze(2).to_broadcast([P, NB, H]), ALU.mult))
            ch.wait()
            ch(e.tensor_tensor(X, X, MT, ALU.add))
            ch.wait()

        def scalar(e, ch):
            e.wait_ge(r["z_ok"], 1)
            e.activation(r["z"][:, :], r["z"][:, :], ACT.Exp, scale=-1.0).then_inc(r["exp_ok"], 1)
        return dict(vector=vector, scalar=scalar)
    phase(kn, "l2c", build, sbufs=[("z", [P, NB], F32), ("g", [P, NB], F32)], sems=["z_ok", "exp_ok"])

def l3_edges(kn):
    ring = lambda t, st: flat(kn, t)[:, bass.ds(st.ring * G * P, G * P)]
    hidden, logs = kn.AC, kn.MT

    def build(r):
        def sync(e, ch):
            run_steps(e, ch, [(load_records(kn, e, r, 0, A50, r["rec_turned"]), 0)], STEPS)

        def tensor(e, ch):
            turn_hot = turn_hot_stage(kn, e, r, 1, kn.identb)

            def turn_rec(st):
                wait_load(e, r["ld"], st, G)
                wait_step(e, r["dT_ok"], st, 1)
                take_waits(e, kn.tally)
                for j in range(G):
                    ins = e.transpose(r["pD"][0:A50, j, :], r["rec"][:, st.par, j, :], kn.ident[:, :])
                ins.then_inc(r["rec_turned"], 1)

            def hid(st):
                wait_step(e, r["dT_ok"], st)
                wait_step(e, r["y_ok"], st, 2)
                e.matmul(r["pH"][:, st.par, :], mat(kn, "mlp_w1", A50),
                         r["dT"][0:A50, st.par, :, :].rearrange("p j c -> p (j c)"), start=True, stop=True
                         ).then_inc(r["h_done"], 1)

            def mults(st):
                blocks = slot_values(kn, e, kn.slot_regs["tensor"], st, 32)
                wait_step(e, r["s_ok"], st)
                wait_step(e, r["w_ok"], st, 2)
                for j in range(G):
                    ins = e.matmul(r["pW"][:, st.par, j, :], ring(hidden, st)[:, j * P:(j + 1) * P], mat(kn, "mlp_w2"),
                                   start=True, stop=True)
                ins.then_inc(r["w_done"], 1)
                wait_step(e, r["ohT_ok"], st)
                wait_step(e, r["prod_ok"], st, 2)
                for j in range(G):
                    ins = e.matmul(r["pX"][:, st.par, j, :], r["ohT"][:, st.par, j, :], block(kn, kn.TB, blocks[j]),
                                   start=True, stop=True)
                ins.then_inc(r["picked"], 1)
            run_steps(e, ch, [(turn_rec, 0), (hid, 1), (turn_hot, 5), (mults, 6)], STEPS, RING)

        def scalar(e, ch):
            def copy_rec(st):
                wait_step(e, r["rec_turned"], st)
                wait_step(e, r["h_done"], st, 2)
                e.activation(r["dT"][0:A50, st.par, :, :], r["pD"][0:A50, :, :], ACT.Copy).then_inc(r["dT_ok"], 1)

            def y(st):
                wait_step(e, r["h_done"], st)
                wait_step(e, r["w_done"], st, RING)
                e.activation(ring(hidden, st), r["pH"][:, st.par, :], ACT.Identity, bias=vec(kn, "mlp_b1")
                             ).then_inc(r["y_ok"], 1)

            def exp(st):
                wait_step(e, r["n_ok"], st)
                e.activation(ring(logs, st), ring(logs, st), ACT.Exp).then_inc(r["e_ok"], 1)

            def log(sts):
                for st in sts:
                    wait_step(e, r["e_ok"], st)
                    e.activation(ring(logs, st), ring(logs, st), ACT.Ln, bias=kn.half1[:, 0:1], scale=0.5
                                 ).then_inc(r["l_ok"], 1)
            run_steps(e, ch, [(copy_rec, 0), (copy_hot_stage(kn, e, r, r["picked"], 1), 5), (y, 1), (exp, 1),
                              (log, QUAD, QUAD)], STEPS, RING)

        def vector(e, ch):
            def minus_abs(st):
                wait_step(e, r["y_ok"], st)
                wait_step(e, r["s_ok"], st, RING)
                e.scalar_tensor_tensor(ring(logs, st), ring(hidden, st), -1.0, ring(hidden, st), ALU.mult, ALU.min
                                       ).then_inc(r["n_ok"], 1)

            def ssp(st):
                wait_step(e, r["l_ok"], st)
                e.scalar_tensor_tensor(ring(hidden, st), ring(hidden, st), 0.0, ring(logs, st), ALU.max, ALU.add
                                       ).then_inc(r["s_ok"], 1)

            def prod(st):
                wait_step(e, r["w_done"], st)
                wait_free(e, r["sent"], st, G)
                e.tensor_tensor(r["prod"][:, st.par, :, :], r["pW"][:, st.par, :, :],
                                row(kn, "mlp_b2").unsqueeze(1).to_broadcast([P, G, H]), ALU.add).then_inc(r["w_ok"], 1)
                wait_step(e, r["picked"], st)
                wait_step(e, r["w_ok"], st)
                for j in range(G):
                    out = r["prod"][:, st.par, j, :]
                    ins = e.scalar_tensor_tensor(out, r["pX"][:, st.par, j, :], kn.cut[:, bass.ds(st.i * G + j, 1)], out,
                                                 ALU.mult, ALU.mult)
                ins.then_inc(r["prod_ok"], 1)
            run_steps(e, ch, [(hot_stage(kn, e, r, 0, r["turned"], iota=kn.iotab), 4), (minus_abs, 1), (ssp, 5), (prod, 7),
                              (idx_stage(kn, e, r, kn.place, "sent"), 7)], STEPS, RING)

        def gpsimd(e, ch):
            scatter_all(kn, e, ch, r)
        return dict(sync=sync, tensor=tensor, scalar=scalar, vector=vector, gpsimd=gpsimd)
    phase(kn, "l3e", build, psums=[("pT", [P, 1, 2 * G, P], BF16), ("pD", [P, G, P], F32), ("pH", [P, 2, BANK], F32),
                                    ("pW", [P, 2, G, P], F32), ("pX", [P, 2, G, P], F32)],
               sbufs=[("rec", [P, 2, G, A50], F32), ("oh", [P, 2, G, P], BF16), ("ohT", [P, 2, G, P], F32),
                      ("dT", [A50, 2, G, P], F32), ("prod", [P, 2, G, P], F32), ("idx", [P, 2, G], I32)],
               sems=["hot", "turned", "ohT_ok", "rec_turned", "dT_ok", "h_done", "y_ok", "n_ok", "e_ok", "l_ok", "s_ok",
                     "w_done", "picked", "w_ok", "prod_ok", "idx_ok"], pairs=["ld", "sent"])

def store(kn):
    def build(r):
        def sync(e, ch):
            full = (N // P) * P
            e.dma_start(kn.out[0:full, :].rearrange("(b p) h -> p b h", p=P), kn.X[:, 0:N // P, :]).then_inc(r["st"], 16)
            e.dma_start(kn.out[full:N, :], kn.X[0:N - full, N // P, :]).then_inc(r["st"], 16)
            e.wait_ge(r["st"], 32)
        return dict(sync=sync)
    phase(kn, "store", build, sems=["st"])


def layout(inp):
    import numpy as np
    f = {k: np.asarray(v) for k, v in inp.items()}
    a = {}
    a["x"] = f["x"]
    rec = np.zeros((EP, NREC), np.float32)
    rec[:E, 0:A50] = f["edge_attr_50"]
    rec[:E, C64:C64 + A64] = f["edge_attr_64"]
    rec[:E, CM:CM + A3] = f["edge_attr_3"]
    rec[:E, CM + A3] = f["edge_weight"]
    a["rec"] = rec
    for n in ("src", "dst"):
        lin = np.full((EP,), PAD_KEY, np.int32)
        lin[:E] = f[n]
        a[n + "_lin"] = lin
        a[n + "_tiles"] = np.ascontiguousarray(lin.reshape(T, P).T)
    t = lambda n: f[n].T
    m = {"W_lin": f["L0_gnn_W_lin"], "Wi": t("L1_gnn_Wi"), "Wj": t("L1_gnn_Wj"), "Wd": t("L1_gnn_Wd"),
         "msg_top": f["L2_gnn_msg_w"][:H], "msg_bottom": f["L2_gnn_msg_w"][H:], "upd_top": f["L2_gnn_upd_w"][:H],
         "upd_bottom": f["L2_gnn_upd_w"][H:], "lin1": t("L3_gnn_lin1_w"), "lin2": t("L3_gnn_lin2_w"),
         "mlp_w2": t("L3_gnn_mlp_w2"), "mlp_w1": t("L3_gnn_mlp_w1"), "Wdesc": t("L1_gnn_Wdesc")}
    v = {"bi": f["L1_gnn_bi"], "bd": f["L1_gnn_bd"], "u": f["L1_gnn_u"], "mlp_b1": f["L3_gnn_mlp_b1"],
         "lin2_b": f["L3_gnn_lin2_b"]}
    for k, n in (("ri1", 3), ("ri2", 3), ("ra1", 2), ("ra2", 2)):
        for i in range(n):
            m[f"W{k}_{i}"] = f["L1_gnn_W" + k][i].T
            v[f"b{k}_{i}"] = f["L1_gnn_b" + k][i]
    att = f["L0_gnn_W_att"]
    m["W_att"] = np.concatenate([att[:H], att[H:]], axis=1)
    a["mats"] = np.zeros((P, len(MATS), H), np.float32)
    for i, n in enumerate(MATS):
        a["mats"][:m[n].shape[0], i, :m[n].shape[1]] = m[n]
    a["vecs"] = np.ascontiguousarray(np.stack([v[n] for n in VECS], axis=1))
    w = {"b_lin": f["L0_gnn_b_lin"], "bj": f["L1_gnn_bj"], "mlp_b2": f["L3_gnn_mlp_b2"], "b_att": f["L0_gnn_b_att"],
         "gate_w": f["L2_gnn_gate_w"][:, 0], "gate_b": f["L2_gnn_gate_b"]}
    for n in ("msg_b", "msg_g", "msg_beta", "upd_b", "upd_g", "upd_beta"):
        w[n] = f["L2_gnn_" + n]
    a["rows"] = np.zeros((1, len(ROWS) * H), np.float32)
    for i, n in enumerate(ROWS):
        a["rows"][0, i * H:i * H + w[n].size] = w[n]
    return a


def build_program(nc, ins, out, upto="all", dump=None):
    kn = Buffers()
    kn.nc, kn.ins, kn.out = nc, ins, out
    kn.tally = nc.alloc_semaphore("tally")
    kn.slot_regs = {n: [e.alloc_register(f"slot{j}") for j in range(G)]
                    for n, e in (("vector", nc.vector), ("tensor", nc.tensor), ("scalar", nc.scalar), ("sync", nc.sync))}
    with ExitStack() as ctx:
        setup(kn, ctx)
        constants(kn)
        with ExitStack() as keys_ctx:
            kn.keys_ctx = keys_ctx
            split_keys(kn)
            histogram(kn)
            if upto == "hist":
                dump(kn, "count", kn.count[:, :, :]); return

            offsets(kn)
            if upto == "off":
                dump(kn, "start", kn.start[:, :, :]); dump(kn, "slot", kn.slot_reg[:, :]); return
            sort(kn)
            if upto == "sort":
                dump(kn, "srt", kn.sorted); return
        node_buffers(kn, ctx)
        slot_columns(kn)
        with ExitStack() as l0:
            kn.sij = l0.enter_context(nc.sbuf_tensor("sij", [P, NB * 2 * HEADS], F32))
            layernorm(kn, "ln0")
            l0_nodes(kn)
            l0_scores(kn)
            if upto == "l0s":
                dump(kn, "h", kn.Hn[:, :, :]); dump(kn, "xl", kn.TB[:, :, :]); dump(kn, "sij", kn.sij[:, :]); dump(kn, "sj_src", kn.sj_src)
                dump(kn, "firsts", kn.firsts); dump(kn, "cut", kn.cut[:, :]); dump(kn, "place", kn.place[:, :]); return
            l0_segments(kn)
            l0_table(kn)
            if upto == "l0t":
                dump(kn, "by_src", kn.by_src); dump(kn, "keys", kn.src_sorted); return
            l0_edges(kn)
        l0_close(kn)
        if upto == "l0":
            dump(kn, "ac0", kn.AC[:, :, :]); dump(kn, "x1", kn.X[:, :, :]); return
        kn.products = dram(kn, "products", (EP, H))
        layernorm(kn, "ln1")
        l1_nodes(kn)
        if upto == "l1n":
            dump(kn, "xj", kn.TB[:, :, :]); dump(kn, "xi", kn.AC[:, :, :]); return
        l1_edges(kn)
        sum_by_src(kn, "l1r")
        if upto == "l1r":
            dump(kn, "ac1", kn.AC[:, :, :]); return
        l1_layers(kn)
        add_turned(kn, "l1c", kn.Hn)
        if upto == "l1":
            dump(kn, "x2", kn.X[:, :, :]); return
        layernorm(kn, "ln2")
        kn.l2_rows = dram(kn, "l2_rows", (NP, H))
        tables(kn, "l2t", "msg_bottom", "msg_top", "msg_b", kn.l2_rows)
        l2_edges(kn)
        if upto == "l2e":
            dump(kn, "ac2", kn.AC[:, :, :]); return
        l2_update(kn)
        layernorm(kn, "ln2b", kn.TB, kn.MT, ACT.Identity)
        l2_close(kn)
        if upto == "l2":
            dump(kn, "x3", kn.X[:, :, :]); return
        layernorm(kn, "ln3")
        tables(kn, "l3t", "lin1")
        l3_edges(kn)
        sum_by_src(kn, "l3r", clear=True)
        if upto == "l3r":
            dump(kn, "ac3", kn.AC[:, :, :]); return
        linear_ssp(kn, "l3o", kn.MT, kn.AC, "lin2", "lin2_b")
        add_turned(kn, "l3c", kn.MT, kn.Hn)
        store(kn)


_ORDER = ["x", "rec", "src_lin", "dst_lin", "src_tiles", "dst_tiles", "mats", "vecs", "rows"]


def kernel(**inputs):
    import numpy as _np
    import concourse.bacc as _bacc
    from concourse import mybir as _mybir
    from concourse.bass_utils import run_bass_kernel_spmd as _run

    nc = _bacc.Bacc("TRN2", target_bir_lowering=False, num_devices=1)
    arrays = layout(inputs)
    args = {n: nc.dram_tensor(n, arrays[n].shape, _mybir.dt.from_np(arrays[n].dtype), kind="ExternalInput").ap()
            for n in _ORDER}
    out = nc.dram_tensor("out", (N, H), F32, kind="ExternalOutput").ap()
    build_program(nc, args, out)
    r = _run(nc, [arrays], core_ids=[0])
    return r.results[0]["out"]
```

```python
from contextlib import ExitStack

import concourse.bass as bass
from concourse import mybir

ALU = mybir.AluOpType
ACT = mybir.ActivationFunctionType
F32 = mybir.dt.float32
BF16 = mybir.dt.bfloat16
I32 = mybir.dt.int32
AX = mybir.AxisListType.X

P = 128
N = 6250
E = 100000
NB = -(-N // P)
NP = NB * P
GT = 8
T = 784
EP = T * P
PAD_KEY = NP - 1
SLOTS = T + NB - 1
G = 4
STEPS = SLOTS // G
H = 128
HEADS = 4
A50, A64, A3 = 50, 64, 3
C64 = A50
CM = A50 + A64
NREC = CM + A3 + 1
W_DST, W_SRC, W_POS = NREC, NREC + 1, NREC + 2
RING = 8
QUAD = 4
META = 8
BIG = 131072.0
NEG = -1.0e30
EPS = 1e-5
SEC = 448
NSEC = NP // SEC
T1W = H + 3 * HEADS
MATS = ["W_lin", "Wi", "Wj", "Wri1_0", "Wri1_1", "Wri1_2", "Wri2_0", "Wri2_1", "Wri2_2", "Wd", "Wra1_0", "Wra1_1",
        "Wra2_0", "Wra2_1", "msg_top", "msg_bottom", "upd_top", "upd_bottom", "lin1", "lin2", "mlp_w2", "mlp_w1",
        "Wdesc", "W_att"]
VECS = ["bi", "bri1_0", "bri1_1", "bri1_2", "bri2_0", "bri2_1", "bri2_2", "bd", "u", "bra1_0", "bra1_1", "bra2_0",
        "bra2_1", "mlp_b1", "lin2_b"]
ROWS = ["b_lin", "bj", "msg_b", "msg_g", "msg_beta", "upd_b", "upd_g", "upd_beta", "gate_w", "mlp_b2", "b_att", "gate_b"]
BANK = 512
assert SLOTS % (2 * G) == 0 and T % GT == 0 and NP % SEC == 0 and EP < BIG


class Step:

    def __init__(self, i, half, par, fourth, quad, ring):
        self.i, self.half, self.par, self.fourth, self.quad, self.ring = i, half, par, fourth, quad, ring


class Chain:

    def __init__(self, eng, sem):
        self.eng, self.sem = eng, sem
        self.done, self.loop, self.per = 0, None, 0

    def __call__(self, ins):
        ins.then_inc(self.sem, 1)
        self.done += 1
        return ins

    def wait(self, back=0):
        n = self.done - back
        if n <= 0:
            return
        self.eng.wait_ge(self.sem, n if self.loop is None else self.loop * self.per + n)


def run_steps(eng, chain, stages, n, unroll=2):
    lag = max(t[1] for t in stages)
    first = max(lag + 2, 2)
    while (n - first) % unroll:
        first += 1

    def one(r, k=None):
        for t in stages:
            c, size = r - t[1], (t[2] if len(t) > 2 else 1)
            if c % size or (k is None and not 0 <= c < n):
                continue
            steps = []
            for i in range(c, c + size):
                if k is None:
                    steps.append(Step(i, i // 2, i % 2, i // 4, i % 4, i % RING))
                else:
                    steps.append(Step(unroll * k + i, (unroll // 2) * k + i // 2, i % 2, (unroll // 4) * k + i // 4,
                                      i % 4, i % RING))
            t[0](steps if len(t) > 2 else steps[0])

    if n < first + 2 * unroll:
        for r in range(n + lag):
            one(r)
        return
    for r in range(first):
        one(r)
    rounds = (n - first) // unroll
    for u in range(unroll):
        before = chain.done
        one(first + u)
        chain.per = chain.per + chain.done - before if u else chain.done - before
    first += unroll
    with eng.Fori(0, rounds - 1) as k:
        chain.loop = k
        start = chain.done
        for u in range(unroll):
            one(first + u, k)
        assert chain.done - start == chain.per
    chain.loop = None
    chain.done = start + chain.per * (rounds - 1)
    for r in range(n, n + lag):
        one(r)


def wait_step(eng, sem, st, back=0):
    v = st.i + (1 - back)
    if isinstance(v, int) and v <= 0:
        return
    eng.wait_ge(sem, v)


def take_waits(eng, tally):
    eng.sem_inc(tally, 1)


def wait_load(eng, sems, st, n):
    eng.wait_ge(sems[st.par], st.half * (16 * n) + 16 * n)


def wait_free(eng, sems, st, n):
    if isinstance(st.half, int) and st.half == 0:
        return
    eng.wait_ge(sems[st.par], st.half * (16 * n))


class Buffers:
    pass


def dram(kn, name, shape, dt=F32):
    return kn.nc.dram_tensor(name, shape, dt, kind="Internal").ap()

def phase(kn, name, build, psums=(), sbufs=(), sems=(), pairs=()):
    nc = kn.nc
    with ExitStack() as ctx:
        res, used = {}, []
        for n, shape, dt in psums:
            res[n] = ctx.enter_context(nc.psum_tensor(f"{name}_{n}", shape, dt))
        for n, shape, dt in sbufs:
            res[n] = ctx.enter_context(nc.sbuf_tensor(f"{name}_{n}", shape, dt))
        for n in sems:
            res[n] = nc.alloc_semaphore(f"{name}_{n}")
            used.append(res[n])
        for n in pairs:
            res[n] = [nc.alloc_semaphore(f"{name}_{n}{j}") for j in range(2)]
            used += res[n]
        bodies = build(res)
        own = {n: nc.alloc_semaphore(f"{name}_{n}_own") for n in bodies}
        used += list(own.values())
        with nc.Block() as block:
            for eng_name, body in bodies.items():
                def run(eng, body=body, sem=own[eng_name]):
                    body(eng, Chain(eng, sem))

                {"sync": block.sync, "tensor": block.tensor, "vector": block.vector,
                 "scalar": block.scalar, "gpsimd": block.gpsimd}[eng_name](run)
        nc.clear_and_free_semaphores(used)
        nc.all_engine_barrier()

def setup(kn, ctx):
    nc = kn.nc

    def sb(name, shape, dt=F32):
        return ctx.enter_context(nc.sbuf_tensor(name, shape, dt))

    kn.X = sb("x_nodes", [P, NB, H])
    kn.ident = sb("ident", [P, P])
    kn.identb = sb("identb", [P, P], BF16)
    kn.ones = sb("ones", [P, P])
    kn.before = sb("before", [P, P])
    kn.beforeb = sb("beforeb", [P, P], BF16)
    kn.iota = sb("iota", [P, P])
    kn.iotab = sb("iotab", [P, P], BF16)
    kn.pcol = sb("pcol", [P, 1])
    kn.zero1 = sb("zero1", [P, 1])
    kn.half1 = sb("half1", [P, 1])
    kn.eps1 = sb("eps1", [P, 1])
    kn.hp1 = sb("half_pi", [P, 1])
    kn.start = sb("start", [P, 2, NB])
    kn.count = sb("count", [P, 2, NB])
    kn.slot_reg = sb("slot_reg", [P, SLOTS], I32)
    kn.local = sb("local", [P, 2, SLOTS])

def node_buffers(kn, ctx):
    def sb(name, shape, dt=F32):
        return ctx.enter_context(kn.nc.sbuf_tensor(name, shape, dt))

    kn.place = sb("k_place", [P, SLOTS], I32)
    kn.src_of = sb("k_src_of", [P, SLOTS], I32)
    kn.wt = sb("k_wt", [P, SLOTS])
    kn.cut = sb("k_cut", [P, SLOTS])
    kn.W = sb("k_weights", [P, len(MATS), H])
    kn.V = sb("k_vectors", [P, len(VECS)])
    kn.R = sb("k_rows", [P, len(ROWS), H])
    kn.Hn = sb("h_nodes", [P, NB, H])
    kn.AC = sb("acc", [P, NB, H])
    kn.TB = sb("table", [P, NB, H])
    kn.MT = sb("spare", [P, NB, H])

def flat(kn, t):
    return t[:, :, :].rearrange("p b h -> p (b h)")

def constants(kn):
    ins = kn.ins

    def build(r):
        def gpsimd(e, ch):
            ch(e.iota(r["ii"][:, :], [[1, P]], base=0, channel_multiplier=0))
            ch(e.iota(r["ip"][:, :], [[0, 1]], base=0, channel_multiplier=1))
            ch.wait()
            ch(e.tensor_copy(kn.iota[:, :], r["ii"][:, :]))
            e.tensor_copy(kn.pcol[:, :], r["ip"][:, :]).then_inc(r["ready"], 1)

        def vector(e, ch):
            ch(e.memset(kn.ones[:, :], 1.0))
            ch(e.memset(kn.zero1[:, :], 0.0))
            ch(e.memset(kn.half1[:, :], 0.5))
            ch(e.memset(kn.eps1[:, :], EPS))
            ch(e.memset(kn.hp1[:, :], 1.5707963267948966))
            e.wait_ge(r["ready"], 1)
            ch(e.tensor_copy(kn.iotab[:, :], kn.iota[:, :]))
            ch(e.tensor_scalar(kn.ident[:, :], kn.iota[:, :], kn.pcol[:, 0:1], None, ALU.is_equal))
            ch(e.tensor_scalar(kn.before[:, :], kn.iota[:, :], kn.pcol[:, 0:1], None, ALU.is_gt))
            ch.wait()
            ch(e.tensor_copy(kn.identb[:, :], kn.ident[:, :]))
            ch(e.tensor_copy(kn.beforeb[:, :], kn.before[:, :]))
            ch.wait()

        def sync(e, ch):
            full = (N // P) * P
            e.dma_start(kn.X[:, 0:N // P, :], ins["x"][0:full, :].rearrange("(b p) h -> p b h", p=P)).then_inc(r["ld"], 16)
            e.dma_start(kn.X[0:N - full, N // P, :], ins["x"][full:N, :]).then_inc(r["ld"], 16)
            e.wait_ge(r["ld"], 32)

        return dict(gpsimd=gpsimd, vector=vector, sync=sync)
    def build0(r):
        def vector(e, ch):
            ch(e.memset(kn.X[:, NB - 1, :], 0.0))
            ch.wait()
        return dict(vector=vector)
    phase(kn, "clear", build0)
    phase(kn, "const", build, sbufs=[("ii", [P, P], I32), ("ip", [P, 1], I32)], sems=["ready", "ld"])

def split_keys(kn):
    kn.lo_rows = dram(kn, "lo_rows", (2, EP), BF16)
    kn.khi = kn.keys_ctx.enter_context(kn.nc.sbuf_tensor("khi", [P, 2, T], F32))
    kn.klo = kn.keys_ctx.enter_context(kn.nc.sbuf_tensor("klo", [P, 2, T], F32))
    kn.kin = kn.keys_ctx.enter_context(kn.nc.sbuf_tensor("kin", [P, 2, T], I32))
    kn.klob = kn.keys_ctx.enter_context(kn.nc.sbuf_tensor("klob", [P, 2, T], BF16))
    kn.khib = kn.keys_ctx.enter_context(kn.nc.sbuf_tensor("khib", [P, 2, T], BF16))

    def build(r):
        def sync(e, ch):
            for q, n in enumerate(("dst", "src")):
                e.dma_start(kn.kin[:, q, :], kn.ins[n + "_tiles"]).then_inc(r["ld"], 16)
                e.dma_start(r["lin"][:, q, :], kn.ins[n + "_lin"].rearrange("(p c) -> p c", p=P)).then_inc(r["ld"], 16)
            e.wait_ge(r["lo"], 1)
            for q in range(2):
                e.dma_start(kn.lo_rows[q].rearrange("(p c) -> p c", p=P), r["linb"][:, q, :]).then_inc(r["st"], 16)
            e.wait_ge(r["st"], 32)

        def vector(e, ch):
            e.wait_ge(r["ld"], 64)
            ch(e.tensor_scalar(r["a"][:, :, :], kn.kin[:, :, :], 127, None, ALU.bitwise_and))
            ch(e.tensor_scalar(r["b"][:, :, :], kn.kin[:, :, :], 7, None, ALU.logical_shift_right))
            ch(e.tensor_scalar(r["c"][:, :, :], r["lin"][:, :, :], 127, None, ALU.bitwise_and))
            ch.wait()
            ch(e.tensor_copy(kn.klo[:, :, :], r["a"][:, :, :]))
            ch(e.tensor_copy(kn.khi[:, :, :], r["b"][:, :, :]))
            ch(e.tensor_copy(kn.klob[:, :, :], r["a"][:, :, :]))
            ch(e.tensor_copy(kn.khib[:, :, :], r["b"][:, :, :]))
            e.tensor_copy(r["linb"][:, :, :], r["c"][:, :, :]).then_inc(r["lo"], 1)
            ch.wait()
        return dict(sync=sync, vector=vector)
    phase(kn, "keys", build, sbufs=[("lin", [P, 2, T], I32), ("linb", [P, 2, T], BF16), ("a", [P, 2, T], I32),
                                     ("b", [P, 2, T], I32), ("c", [P, 2, T], I32)], sems=["ld", "lo", "st"])

def one_hots(kn, e, r, st, what, at=None):
    at = st.par if at is None else at
    w = P if what == "lo" else NB
    src = kn.klob if what == "lo" else kn.khib
    tiles = src[:, :, bass.ds(st.i * GT, GT)]
    return e.tensor_tensor(r["oh" + what][:, at, :, :, :], tiles.unsqueeze(3).to_broadcast([P, 2, GT, w]),
                           kn.iotab[:, None, None, 0:w].to_broadcast([P, 2, GT, w]), ALU.is_equal)

def histogram(kn):
    n = T // GT

    def build(r):
        def vector(e, ch):
            def hot(st):
                wait_step(e, r["pe"], st, 2)
                one_hots(kn, e, r, st, "lo")
                one_hots(kn, e, r, st, "hi").then_inc(r["hot"], 1)
            run_steps(e, ch, [(hot, 0)], n)
            e.wait_ge(r["pe"], n)
            for q in range(2):
                ch(e.tensor_copy(kn.count[:, q, :], r["hist"][:, q, 0:NB]))
            ch.wait()

        def tensor(e, ch):
            def add(st, first=False):
                wait_step(e, r["hot"], st)
                for j in range(GT):
                    for q in range(2):
                        f = isinstance(st.i, int) and st.i == 0 and j == 0
                        ins = e.matmul(r["hist"][:, q, 0:NB], r["ohlo"][:, st.par, q, j, :],
                                       r["ohhi"][:, st.par, q, j, :], start=f, stop=False, skip_group_check=True)
                ins.then_inc(r["pe"], 1)
            run_steps(e, ch, [(add, 0)], n)
        return dict(vector=vector, tensor=tensor)
    phase(kn, "hist", build, psums=[("hist", [P, 2, 512], F32)],
               sbufs=[("ohlo", [P, 2, 2, GT, P], BF16), ("ohhi", [P, 2, 2, GT, NB], BF16)], sems=["hot", "pe"])

def offsets(kn):
    half = SLOTS // 2
    nt = -(-T // P)

    def build(r):
        def tensor(e, ch):
            e.matmul(r["small"][:, 0:2 * NB], kn.before[:, :], kn.count[:, :, :].rearrange("p q b -> p (q b)"),
                     start=True, stop=True)
            e.matmul(r["small"][:, 2 * NB:4 * NB], kn.ones[:, :],
                     kn.count[:, :, :].rearrange("p q b -> p (q b)"), start=True, stop=True,
                     skip_group_check=True).then_inc(r["sums"], 1)
            for q in range(2):
                e.wait_ge(r["less"], q + 1)
                for h in range(2):
                    for c in range(nt):
                        ins = e.matmul(r["tiles"][:, q, h, 0:half], kn.ones[:, :],
                                       r["lt"][:, q, c, h * half:(h + 1) * half], start=(c == 0), stop=(c == nt - 1))
                ins.then_inc(r["counted"], 1)

        def gpsimd(e, ch):
            e.iota(r["is"][:, :], [[1, SLOTS]], base=0, channel_multiplier=0).then_inc(r["iota"], 1)

        def vector(e, ch):
            e.wait_ge(r["iota"], 1)
            ch(e.tensor_copy(r["s"][:, :], r["is"][:, :]))
            for c in range(nt):
                ch(e.tensor_scalar(r["last"][:, c:c + 1], kn.pcol[:, 0:1], float(P), float(P * P * c + P - 1),
                                   ALU.mult, ALU.add))
            e.wait_ge(r["sums"], 1)
            ch(e.tensor_copy(r["tot"][:, :], r["small"][:, 2 * NB:4 * NB]))
            ch.wait()
            for q in range(2):
                ch(e.tensor_tensor_scan(r["upto"][:, q, :], kn.ones[:, 0:NB], r["tot"][:, q * NB:(q + 1) * NB], 0.0,
                                        ALU.mult, ALU.add))
            ch.wait()
            ch(e.tensor_tensor(r["excl"][:, :], r["upto"][:, :, :].rearrange("p q b -> p (q b)"), r["tot"][:, :],
                               ALU.subtract))
            ch.wait()
            ch(e.tensor_tensor(kn.start[:, :, :].rearrange("p q b -> p (q b)"), r["small"][:, 0:2 * NB],
                               r["excl"][:, :], ALU.add))
            for q in range(2):
                for c in range(nt):
                    ch(e.tensor_scalar(r["le"][:, q, c, :], r["upto"][:, q, 0:NB - 1], r["last"][:, c:c + 1], None,
                                       ALU.is_le))
            ch.wait()
            for q in range(2):
                ch(e.tensor_reduce(r["blk"][:, q, :], r["le"][:, q, :, :], AX, ALU.add))
            for c in range(nt):
                ch(e.tensor_scalar(r["t"][:, c:c + 1], kn.pcol[:, 0:1], float(P * c), None, ALU.add))
            ch.wait()
            for q in range(2):
                ch(e.tensor_tensor(r["val"][:, q, :], r["blk"][:, q, :], r["t"][:, :], ALU.add))
            ch.wait()
            for q in range(2):
                for c in range(nt):
                    ins = e.tensor_scalar(r["lt"][:, q, c, :], r["s"][:, :], r["val"][:, q, c:c + 1], None, ALU.is_gt)
                ins.then_inc(r["less"], 1)
            e.wait_ge(r["counted"], 2)
            for q in range(2):
                for h in range(2):
                    cols = slice(h * half, (h + 1) * half)
                    ch(e.tensor_copy(kn.slot_reg[64 * q:64 * q + 32, cols], r["tiles"][0:32, q, h, 0:half]))
                    ch(e.scalar_tensor_tensor(r["b"][:, q, cols], r["tiles"][:, q, h, 0:half], -1.0, r["s"][:, cols],
                                              ALU.mult, ALU.add))
            ch.wait()
            for q in range(2):
                ch(e.tensor_copy(kn.slot_reg[64 * q + 32:64 * q + 64, :], r["b"][0:32, q, :]))
                ch(e.tensor_scalar(kn.local[:, q, :], r["b"][:, q, :], float(P), None, ALU.mult))
            ch.wait()
        return dict(tensor=tensor, gpsimd=gpsimd, vector=vector)
    phase(kn, "offsets", build, psums=[("small", [P, 512], F32), ("tiles", [P, 2, 2, 512], F32)],
               sbufs=[("is", [P, SLOTS], I32), ("s", [P, SLOTS], F32), ("last", [P, nt], F32), ("tot", [P, 2 * NB], F32),
                      ("upto", [P, 2, NB], F32), ("excl", [P, 2 * NB], F32), ("le", [P, 2, nt, NB - 1], F32),
                      ("blk", [P, 2, nt], F32), ("t", [P, nt], F32), ("val", [P, 2, nt], F32),
                      ("lt", [P, 2, nt, SLOTS], F32), ("b", [P, 2, SLOTS], F32)],
               sems=["sums", "iota", "less", "counted"])

def sort(kn):
    n = T // GT
    rec_tiles = kn.ins["rec"].rearrange("(t p) c -> p t c", p=P)
    kn.sorted = dram(kn, "sorted_records", (EP, P))

    def build(r):
        def sync(e, ch):
            def load_rows(st):
                wait_step(e, r["hot"], st, 2)
                for q in range(2):
                    e.dma_start(r["rows"][:, st.par, q, :],
                                kn.lo_rows[q:q + 1, bass.ds(st.i * (GT * P), GT * P)].to_broadcast([P, GT * P])
                                ).then_inc(r["ld"][st.par], 16)

            run_steps(e, ch, [(load_rows, 0)], n)

        def vector(e, ch):
            e.memset(r["rec"][:, :, :, :], 0.0).then_inc(r["cleared"], 1)
            ch(e.memset(r["keep"][:, :, :, 1:], 1.0))
            ch(e.memset(r["keep"][:, :, :, 0:1], 0.0))
            ch(e.tensor_copy(r["before"][:, 1, :, :, GT], kn.start[:, :, :]))

            def hot(st):
                wait_step(e, r["counted"], st, 2)
                wait_step(e, r["placed"], st, 4)
                one_hots(kn, e, r, st, "lo")
                one_hots(kn, e, r, st, "hi", st.quad).then_inc(r["hot_part"], 1)
                wait_load(e, r["ld"], st, 2)
                wait_step(e, r["ranked"], st, 2)
                e.tensor_scalar(r["ohT"][:, st.par, :, :], r["rows"][:, st.par, :, :], kn.pcol[:, 0:1], None,
                                ALU.is_equal).then_inc(r["hot"], 1)

            def mask(st):
                for u in range(4):
                    q, h = u // 2, u % 2
                    e.wait_ge(r["same_done"], st.i * 4 + (u + 1))
                    e.tensor_tensor(r["mask"][:, st.par, q, 4 * h:4 * h + 4, :], r["same"][:, u, :, :],
                                    kn.before[:, None, :].to_broadcast([P, 4, P]), ALU.mult
                                    ).then_inc(r["masked"], 1)

            def scan(st):
                ch.wait()
                ch(e.tensor_copy(r["own"][:, st.par, :, :, 0], r["before"][:, 1 - st.par, :, :, GT]))
                wait_step(e, r["own_ok"], st)
                ch.wait()
                ch(e.tensor_tensor_scan(r["before"][:, st.par, :, :, :].rearrange("p q k t -> p (q k t)"),
                                        r["keep"][:, :, :, :].rearrange("p q k t -> p (q k t)"),
                                        r["own"][:, st.par, :, :, :].rearrange("p q k t -> p (q k t)"),
                                        0.0, ALU.mult, ALU.add))
                ch.wait()
                e.sem_inc(r["scanned"], 1)

            def place(st):
                wait_step(e, r["ranked"], st)
                wait_load(e, r["rec_ld"], st, 1)
                wait_free(e, r["sent"], st, GT)
                ch.wait()
                ch(e.tensor_tensor(r["pick"][:, :, :, :], r["rank"][:, :, :, 0:NB], r["ohhi"][:, st.quad, :, :, :], ALU.mult))
                tiles = kn.kin[:, :, bass.ds(st.i * GT, GT)]
                ch(e.tensor_copy(r["rec"][:, st.par, :, W_DST:W_SRC + 1].rearrange("p t q -> p q t"), tiles))
                ch.wait()
                ch(e.tensor_reduce(r["pos"][:, :, :], r["pick"][:, :, :, :], AX, ALU.add))
                ch.wait()
                ch(e.tensor_copy(r["idx"][:, st.par, :], r["pos"][:, 0, :]))
                e.tensor_scalar(r["rec"][:, st.par, :, W_POS], r["pos"][:, 1, :], BIG, None, ALU.add
                                ).then_inc(r["placed"], 1)
            run_steps(e, ch, [(hot, 0), (place, 2), (mask, 1), (scan, 1)], n, 4)

        def scalar(e, ch):
            def own(st):
                wait_step(e, r["counted"], st)
                wait_step(e, r["scanned"], st, 2)
                for q in range(2):
                    ins = e.activation(r["own"][:, st.par, q, :, 1:].rearrange("p k t -> p t k"),
                                       r["count"][:, q, 0:GT * NB].rearrange("p (t k) -> p t k", k=NB), ACT.Copy)
                ins.then_inc(r["own_ok"], 1)

            def load_records(st):
                wait_free(e, r["sent"], st, GT)
                e.dma_start(r["rec"][:, st.par, :, 0:NREC], rec_tiles[:, bass.ds(st.i * GT, GT), :]
                            ).then_inc(r["rec_ld"][st.par], 16)
            e.wait_ge(r["cleared"], 1)
            run_steps(e, ch, [(own, 0), (load_records, 1)], n)

        def tensor(e, ch):
            def count(st):
                wait_step(e, r["own_ok"], st, 1)
                wait_step(e, r["hot_part"], st)
                for q in range(2):
                    for j in range(GT):
                        ins = e.matmul(r["count"][:, q, j * NB:(j + 1) * NB], r["ohlo"][:, st.par, q, j, :],
                                       r["ohhi"][:, st.quad, q, j, :], start=True, stop=True)
                ins.then_inc(r["counted"], 1)

            def same(st):
                wait_step(e, r["hot"], st)
                for u in range(4):
                    q, h = u // 2, u % 2
                    v = st.i * 4 + (u - 3)
                    if not isinstance(v, int) or v > 0:
                        e.wait_ge(r["masked"], v)
                    for j in range(4):
                        t = r["ohT"][:, st.par, q, (4 * h + j) * P:(4 * h + j + 1) * P]
                        ins = e.matmul(r["same"][:, u, j, :], t, t, start=True, stop=True)
                    ins.then_inc(r["same_done"], 1)

            def rank(st):
                wait_step(e, r["placed"], st, 1)
                e.wait_ge(r["masked"], st.i * 4 + 4)
                wait_step(e, r["scanned"], st)
                for j in range(GT):
                    for q in range(2):
                        out = r["rank"][:, q, j, 0:NB]
                        e.matmul(out, r["ohT"][:, st.par, q, j * P:(j + 1) * P], r["before"][:, st.par, q, :, j],
                                 start=True, stop=False, skip_group_check=True)
                        ins = e.matmul(out, r["mask"][:, st.par, q, j, :], r["ohhi"][:, st.quad, q, j, :],
                                       start=False, stop=True, skip_group_check=True)
                ins.then_inc(r["ranked"], 1)
            run_steps(e, ch, [(count, 0), (same, 0), (rank, 1)], n, 4)

        def gpsimd(e, ch):
            def send(st):
                wait_step(e, r["placed"], st)
                take_waits(e, kn.tally)
                for j in range(GT):
                    e.indirect_dma_start(kn.sorted[:, :],
                                         bass.IndirectOffsetOnAxis(ap=r["idx"][:, st.par, j:j + 1], axis=0),
                                         r["rec"][:, st.par, j, :], None, bounds_check=EP - 1
                                         ).then_inc(r["sent"][st.par], 16)
            run_steps(e, ch, [(send, 0)], n)
            for j in range(2):
                e.wait_ge(r["sent"][j], 16 * GT * (n // 2))
        return dict(sync=sync, vector=vector, scalar=scalar, tensor=tensor, gpsimd=gpsimd)
    phase(kn, "sort", build, psums=[("same", [P, 4, 4, P], F32), ("rank", [P, 2, GT, 64], F32), ("count", [P, 2, BANK], F32)],
               sbufs=[("rows", [P, 2, 2, GT * P], BF16), ("rec", [P, 2, GT, P], F32), ("ohlo", [P, 2, 2, GT, P], BF16),
                      ("ohhi", [P, 4, 2, GT, NB], BF16), ("ohT", [P, 2, 2, GT * P], F32),
                      ("mask", [P, 2, 2, GT, P], BF16), ("pick", [P, 2, GT, NB], F32), ("pos", [P, 2, GT], F32),
                      ("idx", [P, 2, GT], I32), ("own", [P, 2, 2, NB, GT + 1], F32), ("before", [P, 2, 2, NB, GT + 1], F32),
                      ("keep", [P, 2, NB, GT + 1], F32)],
               sems=["cleared", "hot_part", "hot", "counted", "own_ok", "scanned", "same_done", "masked", "ranked", "placed"],
               pairs=["ld", "rec_ld", "sent"])

def slot_columns(kn):
    chunk = 98
    srt = kn.sorted.rearrange("(t p) c -> p t c", p=P)
    meta = flat(kn, kn.MT).rearrange("p (t c) -> p t c", c=META)

    def build(r):
        def sync(e, ch):
            for n, t in ((kn.W, kn.ins["mats"]), (kn.V, kn.ins["vecs"])):
                e.dma_start(n[tuple([slice(None)] * len(t.shape))], t).then_inc(r["wld"], 16)
            e.dma_start(kn.R[:, :, :].rearrange("p r h -> p (r h)"),
                        kn.ins["rows"].to_broadcast([P, len(ROWS) * H])).then_inc(r["wld"], 16)
            for c in range(T // chunk):
                e.dma_start(meta[:, c * chunk:(c + 1) * chunk, :], srt[:, c * chunk:(c + 1) * chunk, CM:CM + META]
                            ).then_inc(r["ld"], 16)
            e.wait_ge(r["ld"], 16 * (T // chunk))
            e.wait_ge(r["wld"], 48)

        def vector(e, ch):
            e.wait_ge(r["ld"], 16 * (T // chunk))


            def pick(st):
                tiles = slot_values(kn, e, kn.slot_regs["vector"], st, 0)
                for j in range(G):
                    ch(e.tensor_copy(r["m"][:, bass.ds((st.i * G + j) * META, META)],
                                     meta[:, bass.ds(tiles[j], 1), :].rearrange("p a c -> p (a c)")))
            run_steps(e, ch, [(pick, 0)], STEPS // 2)
            ch.wait()
            e.wait_ge(r["other_half"], 1)
            m = r["m"][:, :].rearrange("p (s c) -> p s c", c=META)
            ch(e.tensor_tensor(kn.local[:, 0, :], m[:, :, 4], kn.local[:, 0, :], ALU.subtract))
            ch(e.tensor_copy(kn.src_of[:, :], m[:, :, 5]))
            ch(e.tensor_copy(kn.wt[:, :], m[:, :, 3]))
            ch(e.tensor_tensor(r["a"][:, 0, :], m[:, :, 0], m[:, :, 0], ALU.mult))
            ch(e.tensor_tensor(r["a"][:, 1, :], m[:, :, 1], m[:, :, 1], ALU.mult))
            ch(e.tensor_tensor(r["a"][:, 2, :], m[:, :, 2], m[:, :, 2], ALU.mult))
            ch.wait()
            ch(e.tensor_tensor(r["a"][:, 0, :], r["a"][:, 0, :], r["a"][:, 1, :], ALU.add))
            ch.wait()
            ch(e.tensor_scalar(r["a"][:, 1, :], kn.local[:, 0, :], float(P), None, ALU.is_lt))
            ch.wait()
            ch(e.scalar_tensor_tensor(r["a"][:, 1, :], kn.local[:, 0, :], 0.0, r["a"][:, 1, :], ALU.is_ge, ALU.mult))
            e.tensor_tensor(r["a"][:, 0, :], r["a"][:, 0, :], r["a"][:, 2, :], ALU.add).then_inc(r["sq"], 1)
            ch.wait()
            ch(e.scalar_tensor_tensor(kn.place[:, :], r["a"][:, 1, :], -BIG, m[:, :, 6], ALU.mult, ALU.add))
            e.wait_ge(r["root"], 1)
            ch(e.tensor_scalar(kn.cut[:, :], r["a"][:, 0, :], 10.0, None, ALU.is_le))
            e.tensor_scalar(r["a"][:, 2, :], r["a"][:, 0, :], 10.0, None, ALU.min).then_inc(r["capped"], 1)
            e.wait_ge(r["cosine"], 1)
            ch(e.tensor_scalar(r["a"][:, 0, :], r["a"][:, 2, :], 1.0, 0.5, ALU.add, ALU.mult))
            ch.wait()
            ch(e.tensor_tensor(kn.cut[:, :], kn.cut[:, :], r["a"][:, 0, :], ALU.mult))
            ch.wait()

        def scalar(e, ch):
            e.wait_ge(r["ld"], 16 * (T // chunk))

            def pick(st):
                tiles = slot_values(kn, e, kn.slot_regs["scalar"], st, 0, STEPS // 2)
                for j in range(G):
                    ch(e.activation(r["m"][:, bass.ds((st.i * G + j + SLOTS // 2) * META, META)],
                                    meta[:, bass.ds(tiles[j], 1), :].rearrange("p a c -> p (a c)"), ACT.Copy))
            run_steps(e, ch, [(pick, 0)], STEPS // 2)
            ch.wait()
            e.sem_inc(r["other_half"], 1)
            e.wait_ge(r["sq"], 1)
            e.activation(r["a"][:, 0, :], r["a"][:, 0, :], ACT.Sqrt).then_inc(r["root"], 1)
            e.wait_ge(r["capped"], 1)
            e.activation(r["a"][:, 2, :], r["a"][:, 2, :], ACT.Sin, bias=kn.hp1[:, 0:1],
                         scale=-3.141592653589793 / 10.0).then_inc(r["cosine"], 1)
        return dict(sync=sync, vector=vector, scalar=scalar)
    phase(kn, "slots", build, sbufs=[("m", [P, SLOTS * META], F32), ("a", [P, 3, SLOTS], F32)],
               sems=["ld", "wld", "other_half", "sq", "root", "capped", "cosine"])

def mat(kn, name, rows=P):
    return kn.W[0:rows, MATS.index(name), :]

def vec(kn, name):
    i = VECS.index(name)
    return kn.V[:, i:i + 1]

def row(kn, name):
    return kn.R[:, ROWS.index(name), :]

def block(kn, t, b):
    return flat(kn, t)[:, bass.ds(b * P, P)]

def layernorm(kn, name, src=None, dst=None, func=ACT.Relu):
    src, dst = src or kn.X, dst or kn.Hn

    def build(r):
        def vector(e, ch):
            def stats(st):
                ch(e.bn_stats(r["six"][:, bass.ds(st.i * 6, 6)], block(kn, src, st.i)))
            run_steps(e, ch, [(stats, 0)], NB)
            ch.wait()
            for b in range(NB):
                ch(e.bn_aggr(r["mv"][:, 2 * b:2 * b + 2], r["six"][:, 6 * b:6 * b + 6]))
            ch.wait()
            mv = r["mv"][:, :].rearrange("p (b k) -> p b k", k=2)
            e.tensor_copy(r["var"][:, :], mv[:, :, 1]).then_inc(r["var_ok"], 1)
            e.wait_ge(r["std"], 1)
            ch(e.reciprocal(r["rstd"][:, :], r["var"][:, :]))
            ch.wait()
            e.scalar_tensor_tensor(r["shift"][:, :], mv[:, :, 0], -1.0, r["rstd"][:, :], ALU.mult, ALU.mult
                                   ).then_inc(r["scales"], 1)

        def scalar(e, ch):
            e.wait_ge(r["var_ok"], 1)
            e.activation(r["var"][:, :], r["var"][:, :], ACT.Sqrt, bias=kn.eps1[:, 0:1]).then_inc(r["std"], 1)
            e.wait_ge(r["scales"], 1)

            def norm(st):
                ch(e.activation(block(kn, dst, st.i), block(kn, src, st.i), func,
                                bias=r["shift"][:, bass.ds(st.i, 1)], scale=r["rstd"][:, bass.ds(st.i, 1)]))
            run_steps(e, ch, [(norm, 0)], NB)
            ch.wait()
        return dict(vector=vector, scalar=scalar)
    phase(kn, name, build, sbufs=[("six", [P, 6 * NB], F32), ("mv", [P, 2 * NB], F32), ("var", [P, NB], F32),
                                   ("rstd", [P, NB], F32), ("shift", [P, NB], F32)],
               sems=["var_ok", "std", "scales"])

def l0_nodes(kn):
    def build(r):
        def tensor(e, ch):
            def turn(st):
                wait_step(e, r["fetched"], st)
                wait_step(e, r["hT_ok"], st, 2)
                e.transpose(r["pA"][:, st.par, 0:P], r["hb"][:, st.par, :], kn.ident[:, :]).then_inc(r["turned"], 1)

            def lin(st):
                wait_step(e, r["hT_ok"], st)
                wait_step(e, r["xl_ok"], st, 2)
                e.matmul(r["pB"][:, st.par, 0:P], r["hT"][:, st.par, :], mat(kn, "W_lin"), start=True, stop=True
                         ).then_inc(r["lin_ok"], 1)

            def turn_xl(st):
                wait_step(e, r["xl_ok"], st)
                wait_step(e, r["xlT_ok"], st, 2)
                e.transpose(r["pC"][:, st.par, 0:P], r["xl"][:, st.par, :], kn.ident[:, :]).then_inc(r["xl_turned"], 1)

            def att(st):
                wait_step(e, r["xlT_ok"], st)
                wait_step(e, r["s_ok"], st, 2)
                e.matmul(r["pD"][:, st.par, 0:2 * HEADS], r["xlT"][:, st.par, :], mat(kn, "W_att")[:, 0:2 * HEADS],
                         start=True, stop=True).then_inc(r["att_ok"], 1)
            run_steps(e, ch, [(turn, 0), (lin, 0), (turn_xl, 1), (att, 1)], NB)

        def scalar(e, ch):
            def fetch(st):
                wait_step(e, r["turned"], st, 2)
                e.activation(r["hb"][:, st.par, :], block(kn, kn.Hn, st.i), ACT.Copy).then_inc(r["fetched"], 1)

            def copy_h(st):
                wait_step(e, r["turned"], st)
                wait_step(e, r["lin_ok"], st, 2)
                e.activation(r["hT"][:, st.par, :], r["pA"][:, st.par, 0:P], ACT.Copy).then_inc(r["hT_ok"], 1)

            def copy_xl(st):
                wait_step(e, r["xl_turned"], st)
                wait_step(e, r["att_ok"], st, 2)
                e.activation(r["xlT"][:, st.par, :], r["pC"][:, st.par, 0:P], ACT.Copy).then_inc(r["xlT_ok"], 1)
            run_steps(e, ch, [(fetch, 0), (copy_h, 0), (copy_xl, 1)], NB)

        def vector(e, ch):
            def xl(st):
                wait_step(e, r["lin_ok"], st)
                wait_step(e, r["xl_turned"], st, 2)
                ch(e.tensor_tensor(block(kn, kn.TB, st.i), r["pB"][:, st.par, 0:P], row(kn, "b_lin"), ALU.add))
                e.tensor_tensor(r["xl"][:, st.par, :], r["pB"][:, st.par, 0:P], row(kn, "b_lin"), ALU.add
                                ).then_inc(r["xl_ok"], 1)

            def s(st):
                wait_step(e, r["att_ok"], st)
                e.tensor_tensor(kn.sij[:, bass.ds(st.i * 2 * HEADS, 2 * HEADS)], r["pD"][:, st.par, 0:2 * HEADS],
                                row(kn, "b_att")[:, 0:2 * HEADS], ALU.add).then_inc(r["s_ok"], 1)
            run_steps(e, ch, [(xl, 0), (s, 1)], NB)
            e.wait_ge(r["s_ok"], NB)
            sij = kn.sij[:, :].rearrange("p (b k) -> p b k", k=2 * HEADS)
            ch(e.memset(r["first"][:, :, 4:5], 1.0))
            ch(e.memset(r["first"][:, :, 6:8], 0.0))
            ch(e.tensor_copy(r["first"][:, :, 0:4], sij[:, :, 0:4]))
            ch(e.tensor_scalar(r["first"][:, :, 5], kn.iota[:, 0:NB], float(P), kn.pcol[:, 0:1], ALU.mult, ALU.add))
            ch(e.memset(kn.MT[:, :, :], 0.0))
            ch(e.tensor_scalar(r["none"][:, :], kn.count[:, 1, :], 0.0, None, ALU.is_equal))
            ch.wait()
            e.scalar_tensor_tensor(r["at"][:, :], r["none"][:, :], BIG, kn.start[:, 1, :], ALU.mult, ALU.add
                                   ).then_inc(r["rows_ok"], 1)

        def sync(e, ch):
            e.wait_ge(r["rows_ok"], 1)
            e.dma_start(kn.firsts.rearrange("(p c) k -> p (c k)", p=P), flat(kn, kn.MT)).then_inc(r["zeroed"], 16)
            e.wait_ge(r["zeroed"], 16)

        def gpsimd(e, ch):
            e.wait_ge(r["zeroed"], 16)
            for b in range(NB):
                e.indirect_dma_start(kn.firsts[:, :], bass.IndirectOffsetOnAxis(ap=r["at"][:, b:b + 1], axis=0),
                                     r["first"][:, b, :], None, bounds_check=EP - 1, oob_is_err=False
                                     ).then_inc(r["sent"], 16)
            e.wait_ge(r["sent"], 16 * NB)
        return dict(tensor=tensor, scalar=scalar, vector=vector, sync=sync, gpsimd=gpsimd)
    kn.firsts = dram(kn, "firsts", (EP, 8))
    phase(kn, "l0n", build, psums=[(n, [P, 2, BANK], F32) for n in ("pA", "pB", "pC", "pD")],
               sbufs=[("hb", [P, 2, P], F32), ("xl", [P, 2, P], F32), ("hT", [P, 2, P], F32),
                      ("xlT", [P, 2, P], F32), ("first", [P, NB, 8], F32),
                      ("none", [P, NB], F32), ("at", [P, NB], I32)],
               sems=["fetched", "turned", "hT_ok", "lin_ok", "xl_ok", "xl_turned", "xlT_ok", "att_ok", "s_ok", "rows_ok",
                     "zeroed", "sent"])

def hot_stage(kn, e, r, q, free, back=2, iota=None):
    iota = kn.iota if iota is None else iota

    def hot(st):
        wait_step(e, free, st, back)
        for j in range(G):
            ins = e.tensor_scalar(r["oh"][:, st.par, j, :], iota[:, :],
                                  kn.local[:, q, bass.ds(st.i * G + j, 1)], None, ALU.is_equal)
        ins.then_inc(r["hot"], 1)
    return hot

def scalar_hot_stage(kn, e, ch, r, q, one_hot, free, back):
    def hot(st):
        wait_step(e, free, st, back)
        for j in range(G):
            ch(e.activation(one_hot(st)[:, j, :], kn.iota[:, :], ACT.Abs, bias=kn.local[:, q, bass.ds(st.i * G + j, 1)],
                            scale=-1.0))
        ch.wait()
        e.activation(one_hot(st), one_hot(st), ACT.Relu, bias=kn.ones[:, 0:1], scale=-1.0).then_inc(r["hot"], 1)
    return hot

def turn_hot_stage(kn, e, r, banks=2, ident=None):
    ident = kn.ident if ident is None else ident
    def turn(st):
        wait_step(e, r["hot"], st)
        wait_step(e, r["ohT_ok"], st, banks)
        for j in range(G):
            ins = e.transpose(r["pT"][:, st.par % banks, j, :], r["oh"][:, st.par, j, :], ident[:, :])
        ins.then_inc(r["turned"], 1)
    return turn

def copy_hot_stage(kn, e, r, used, banks=2):
    def copy(st):
        wait_step(e, r["turned"], st)
        wait_step(e, used, st, 2)
        e.activation(r["ohT"][:, st.par, :, :], r["pT"][:, st.par % banks, 0:G, :], ACT.Copy
                     ).then_inc(r["ohT_ok"], 1)
    return copy

def slot_values(kn, e, regs, st, which, first=0):
    e.load(regs, kn.slot_reg[which:which + 1, bass.ds(st.i * G + first * G, G)])
    return [e.snap(g, min_val=0, max_val=(T if which % 64 == 0 else NB) - 1) for g in regs]

def add_stage(kn, e, ch, r, q):

    def add(st):
        blocks = slot_values(kn, e, kn.slot_regs["vector"], st, 64 * q + 32)
        wait_step(e, r["summed"], st)
        wait_step(e, r["added"], st, 1)
        for j in range(G):
            if j:
                ch.wait()
            acc = block(kn, kn.AC, blocks[j])
            ins = e.tensor_tensor(acc, acc, r["pR"][:, st.par, j, :], ALU.add)
            if j < G - 1:
                ch(ins)
        ins.then_inc(r["added"], 1)
    return add

def l0_scores(kn):
    kn.sj_src = dram(kn, "sj_src", (EP, HEADS))
    kn.slot_sj = flat(kn, kn.MT)[:, 0:SLOTS * HEADS]

    def build(r):
        def vector(e, ch):
            hot = hot_stage(kn, e, r, 0, r["turned"], iota=kn.iotab)

            def idx(st):
                wait_free(e, r["sent"], st, G)
                e.tensor_copy(r["idx"][:, st.par, :], kn.place[:, bass.ds(st.i * G, G)]).then_inc(r["idx_ok"], 1)
            run_steps(e, ch, [(hot, 0), (idx, 2)], STEPS)

        def tensor(e, ch):
            turn = turn_hot_stage(kn, e, r, ident=kn.identb)


            def pick(st):
                blocks = slot_values(kn, e, kn.slot_regs["tensor"], st, 32)
                wait_step(e, r["ohT_ok"], st)
                wait_step(e, r["kept"], st, 2)
                for j in range(G):
                    ins = e.matmul(r["pS"][:, st.par, j * HEADS:(j + 1) * HEADS], r["ohT"][:, st.par, j, :],
                                   kn.sij[:, bass.ds(blocks[j] * (2 * HEADS) + HEADS, HEADS)], start=True, stop=True)
                ins.then_inc(r["picked"], 1)
            run_steps(e, ch, [(turn, 1), (pick, 2)], STEPS)

        def scalar(e, ch):
            copy = copy_hot_stage(kn, e, r, r["picked"])

            def keep(st):
                wait_step(e, r["picked"], st)
                e.activation(kn.slot_sj[:, bass.ds(st.i * G * HEADS, G * HEADS)],
                             r["pS"][:, st.par, 0:G * HEADS], ACT.Copy).then_inc(r["kept"], 1)
                wait_free(e, r["sent"], st, G)
                e.activation(r["out"][:, st.par, :, :].rearrange("p j k -> p (j k)"), r["pS"][:, st.par, 0:G * HEADS], ACT.Copy).then_inc(r["out_ok"], 1)
            run_steps(e, ch, [(copy, 1), (keep, 2)], STEPS)

        def gpsimd(e, ch):
            def send(st):
                wait_step(e, r["out_ok"], st)
                wait_step(e, r["idx_ok"], st)
                take_waits(e, kn.tally)
                for j in range(G):
                    e.indirect_dma_start(kn.sj_src[:, :],
                                         bass.IndirectOffsetOnAxis(ap=r["idx"][:, st.par, j:j + 1], axis=0),
                                         r["out"][:, st.par, j, :], None, bounds_check=EP - 1, oob_is_err=False
                                         ).then_inc(r["sent"][st.par], 16)
            run_steps(e, ch, [(send, 0)], STEPS)
            for j in range(2):
                e.wait_ge(r["sent"][j], 16 * G * (STEPS // 2))
        return dict(vector=vector, tensor=tensor, scalar=scalar, gpsimd=gpsimd)
    phase(kn, "l0s", build, psums=[("pT", [P, 2, 2 * G, P], BF16), ("pS", [P, 2, BANK], F32)],
               sbufs=[("oh", [P, 2, G, P], BF16), ("ohT", [P, 2, G, P], F32), ("out", [P, 2, G, HEADS], F32),
                      ("idx", [P, 2, G], I32)],
               sems=["hot", "turned", "ohT_ok", "picked", "kept", "out_ok", "idx_ok"], pairs=["sent"])

def l0_segments(kn):
    kn.run_ml = dram(kn, "run_ml", (EP, 2 * HEADS))
    kn.src_sorted = dram(kn, "src_sorted", (EP,))
    fl = flat(kn, kn.AC)
    firsts = fl.rearrange("p (c k) -> p c k", k=8)
    d0 = fl[:, 0:HEADS * T].rearrange("p (k c) -> p k c", k=HEADS)
    d1 = fl[:, HEADS * T:2 * HEADS * T].rearrange("p (k c) -> p k c", k=HEADS)
    hl = flat(kn, kn.Hn)
    sj = hl[:, 0:HEADS * T].rearrange("p (c k) -> p c k", k=HEADS)
    si = hl[:, HEADS * T:2 * HEADS * T].rearrange("p (k c) -> p k c", k=HEADS)
    both = hl.rearrange("p (c k) -> p c k", k=2 * HEADS)

    def build(r):
        turns = [0]

        def sync(e, ch):
            e.dma_start(fl, kn.firsts.rearrange("(p c) k -> p (c k)", p=P)).then_inc(r["ld"], 16)
            e.dma_start(hl[:, 0:HEADS * T], kn.sj_src.rearrange("(p c) k -> p (c k)", p=P)).then_inc(r["ld"], 16)
            e.wait_ge(r["keys_ok"], 1)
            e.dma_start(kn.src_sorted.rearrange("(p c) -> p c", p=P), r["keyrow"][:, :]).then_inc(r["st"], 16)
            e.wait_ge(r["both_ok"], 1)
            e.dma_start(kn.run_ml.rearrange("(p c) k -> p (c k)", p=P), hl).then_inc(r["st"], 16)
            e.wait_ge(r["st"], 32)

        n_carry = 4

        def tensor(e, ch):
            for i in range(n_carry):
                e.wait_ge(r["ends_ok"], i + 1)
                e.transpose(r["pa"][0:HEADS, 0:P], r["ends"][:, 0:HEADS], kn.ident[:, :])
                e.transpose(r["pb"][0:HEADS, 0:P], r["ends"][:, HEADS:2 * HEADS], kn.ident[:, :]).then_inc(r["rows_ok"], 1)
                e.wait_ge(r["carried"], i + 1)
                e.transpose(r["pc"][:, 0:HEADS], r["crow"][0:HEADS, 0:P], kn.ident[0:HEADS, 0:HEADS]
                            ).then_inc(r["back"], 1)

        def vector(e, ch):
            def carry(op0, op1, init):
                i = turns[0]
                turns[0] += 1
                ch.wait()
                e.tensor_copy(r["ends"][:, 0:1], r["ends"][:, 0:1]).then_inc(r["ends_ok"], 1)
                e.wait_ge(r["rows_ok"], i + 1)
                ch(e.tensor_copy(r["arow"][0:HEADS, :], r["pa"][0:HEADS, 0:P]))
                ch(e.memset(r["crow"][0:HEADS, 0:1], init))
                ch.wait()
                e.tensor_tensor_scan(r["crow"][0:HEADS, 1:P + 1], r["arow"][0:HEADS, :], r["pb"][0:HEADS, 0:P], init,
                                     op0, op1).then_inc(r["carried"], 1)
                e.wait_ge(r["back"], i + 1)
                ch(e.tensor_copy(r["carry"][:, :], r["pc"][:, 0:HEADS]))
                ch.wait()

            e.wait_ge(r["ld"], 32)
            ch(e.tensor_scalar(r["cont"][:, :], firsts[:, :, 4], -1.0, 1.0, ALU.mult, ALU.add))
            ch(e.tensor_scalar(r["mask"][:, :], firsts[:, :, 4], NEG, None, ALU.mult))
            ch(e.tensor_reduce(r["any"][:, :], firsts[:, :, 4], AX, ALU.max))
            ch.wait()
            ch(e.tensor_scalar(r["through"][:, :], r["any"][:, :].to_broadcast([P, HEADS]), -1.0, 1.0, ALU.mult, ALU.add))
            ch.wait()
            for rep in range(2):
                for k in range(HEADS):
                    ch(e.tensor_tensor_scan(si[:, k, :], r["cont"][:, :], firsts[:, :, k],
                                            0.0 if rep == 0 else r["carry"][:, k:k + 1], ALU.mult, ALU.add))
                ch.wait()
                if rep == 0:
                    ch(e.tensor_copy(r["ends"][:, 0:HEADS], r["through"][:, :]))
                    ch(e.tensor_copy(r["ends"][:, HEADS:], si[:, :, T - 1]))
                    carry(ALU.mult, ALU.add, 0.0)
            ch(e.memset(r["zeros"][:, :], 0.0))
            ch.wait()
            for rep in range(2):
                ch(e.tensor_tensor_scan(r["keyrow"][:, :], r["zeros"][:, :], firsts[:, :, 5],
                                        0.0 if rep == 0 else r["carry"][:, 0:1], ALU.add, ALU.max))
                ch.wait()
                if rep == 0:
                    ch(e.memset(r["ends"][:, 0:HEADS], 0.0))
                    ch(e.tensor_copy(r["ends"][:, HEADS:], r["keyrow"][:, T - 1:T].to_broadcast([P, HEADS])))
                    carry(ALU.add, ALU.max, 0.0)
            e.tensor_copy(r["carry"][:, 0:1], r["carry"][:, 0:1]).then_inc(r["keys_ok"], 1)
            for k in range(HEADS):
                ch(e.tensor_tensor(r["al"][:, k, :], si[:, k, :], sj[:, :, k], ALU.add))
            ch.wait()
            ch(e.scalar_tensor_tensor(r["al"][:, :, :], r["al"][:, :, :], 0.2, r["al"][:, :, :], ALU.mult, ALU.max))
            ch.wait()
            for rep in range(2):
                for k in range(HEADS):
                    ch(e.tensor_tensor_scan(r["m"][:, k, 1:T + 1], r["mask"][:, :], r["al"][:, k, :],
                                            NEG if rep == 0 else r["carry"][:, k:k + 1], ALU.add, ALU.max))
                ch.wait()
                if rep == 0:
                    ch(e.tensor_scalar(r["ends"][:, 0:HEADS], r["any"][:, :].to_broadcast([P, HEADS]), NEG, None, ALU.mult))
                    ch(e.tensor_copy(r["ends"][:, HEADS:], r["m"][:, :, T]))
                    carry(ALU.add, ALU.max, NEG)
            ch(e.tensor_copy(r["m"][:, :, 0], r["carry"][:, :]))
            ch.wait()
            ch(e.tensor_tensor(d0, r["m"][:, :, 0:T], r["m"][:, :, 1:T + 1], ALU.subtract))
            ch(e.tensor_tensor(d1, r["al"][:, :, :], r["m"][:, :, 1:T + 1], ALU.subtract))
            ch(e.tensor_tensor(r["mm"][:, :], r["m"][:, :, 0], r["m"][:, :, T], ALU.subtract))
            ch.wait()
            ch(e.tensor_scalar(d0, d0, 0.0, None, ALU.min))
            e.tensor_scalar(r["mm"][:, :], r["mm"][:, :], 0.0, None, ALU.min).then_inc(r["diffs"], 1)
            e.wait_ge(r["exps"], 1)
            for k in range(HEADS):
                ch(e.tensor_tensor(d0[:, k, :], d0[:, k, :], r["cont"][:, :], ALU.mult))
            ch(e.tensor_tensor(r["ends"][:, 0:HEADS], r["mm"][:, :], r["through"][:, :], ALU.mult))
            ch.wait()
            for rep in range(2):
                for k in range(HEADS):
                    ch(e.tensor_tensor_scan(r["al"][:, k, :], d0[:, k, :], d1[:, k, :],
                                            0.0 if rep == 0 else r["carry"][:, k:k + 1], ALU.mult, ALU.add))
                ch.wait()
                if rep == 0:
                    ch(e.tensor_copy(r["ends"][:, HEADS:], r["al"][:, :, T - 1]))
                    carry(ALU.mult, ALU.add, 0.0)
            for k in range(HEADS):
                ch(e.tensor_copy(both[:, :, k], r["m"][:, k, 1:T + 1]))
                ins = e.tensor_copy(both[:, :, HEADS + k], r["al"][:, k, :])
                if k < HEADS - 1:
                    ch(ins)
            ins.then_inc(r["both_ok"], 1)

        def scalar(e, ch):
            e.wait_ge(r["diffs"], 1)
            ch(e.activation(d0, d0, ACT.Exp))
            ch(e.activation(d1, d1, ACT.Exp))
            e.activation(r["mm"][:, :], r["mm"][:, :], ACT.Exp).then_inc(r["exps"], 1)
        return dict(sync=sync, tensor=tensor, vector=vector, scalar=scalar)
    phase(kn, "l0g", build, psums=[(n, [P, BANK], F32) for n in ("pa", "pb", "pc")],
               sbufs=[("keyrow", [P, T], F32), ("cont", [P, T], F32), ("mask", [P, T], F32), ("zeros", [P, T], F32),
                      ("any", [P, 1], F32), ("through", [P, HEADS], F32), ("ends", [P, 2 * HEADS], F32),
                      ("arow", [HEADS, P], F32), ("crow", [HEADS, P + 1], F32), ("carry", [P, HEADS], F32),
                      ("mm", [P, HEADS], F32), ("al", [P, HEADS, T], F32), ("m", [P, HEADS, T + 1], F32)],
               sems=["ld", "st", "keys_ok", "both_ok", "ends_ok", "rows_ok", "carried", "back", "diffs", "exps"])

def l0_table(kn):
    kn.by_src = dram(kn, "l0_by_src", (NP, T1W))
    rows = T // 7

    def build(r):
        def sync(e, ch):
            e.dma_start(r["kr"][:, :, :], kn.src_sorted.rearrange("(k t p) -> t k p", p=P, k=7)).then_inc(r["kld"], 16)
            tab = kn.by_src.rearrange("(b p) c -> p b c", p=P)
            e.dma_start(tab[:, :, 0:H], kn.TB[:, :, :]).then_inc(r["st"], 16)
            e.wait_ge(r["small_ok"], 1)
            e.dma_start(tab[:, :, H:T1W], r["small"][:, :, :]).then_inc(r["st"], 16)
            e.wait_ge(r["st"], 32)

        def tensor(e, ch):
            e.wait_ge(r["kld"], 16)
            for k in range(7):
                ins = e.transpose(r["pk"][:, k // 4, (k % 4) * rows:(k % 4 + 1) * rows], r["kr"][:, k, :],
                                  kn.ident[0:rows, 0:rows])
            ins.then_inc(r["turned"], 1)

        def vector(e, ch):
            ch(e.tensor_tensor(r["f"][:, :], kn.start[:, 1, :], kn.count[:, 1, :], ALU.add))
            ch.wait()
            e.tensor_scalar(r["at"][:, :], r["f"][:, :], -1.0, 0.0, ALU.add, ALU.max).then_inc(r["at_ok"], 1)
            e.wait_ge(r["turned"], 1)
            ch(e.tensor_copy(r["key"][:, 0:4 * rows], r["pk"][:, 0, 0:4 * rows]))
            ch(e.tensor_copy(r["key"][:, 4 * rows:], r["pk"][:, 1, 0:3 * rows]))
            ch.wait()


            def pick(st):
                tiles = slot_values(kn, e, kn.slot_regs["vector"], st, 64)
                for j in range(G):
                    col = kn.local[:, 1, bass.ds(st.i * G + j, 1)]
                    ch(e.tensor_tensor(col, r["key"][:, bass.ds(tiles[j], 1)], col, ALU.subtract))
            e.sem_inc(r["keys_ok"], 1)
            run_steps(e, ch, [(pick, 0)], STEPS // 2)
            e.wait_ge(r["got"], 16 * NB)
            sij = kn.sij[:, :].rearrange("p (b k) -> p b k", k=2 * HEADS)
            ch(e.tensor_copy(r["small"][:, :, 0:HEADS], sij[:, :, 0:HEADS]))
            ch(e.tensor_copy(r["small"][:, :, HEADS:2 * HEADS], r["ml"][:, :, 0:HEADS]))
            ch(e.tensor_scalar(r["l"][:, :, :], r["ml"][:, :, HEADS:], 1e-16, None, ALU.add))
            ch.wait()
            e.reciprocal(r["small"][:, :, 2 * HEADS:], r["l"][:, :, :]).then_inc(r["small_ok"], 1)
            ch(e.memset(kn.AC[:, :, :], 0.0))
            ch.wait()

        def scalar(e, ch):
            e.wait_ge(r["keys_ok"], 1)

            def pick(st):
                tiles = slot_values(kn, e, kn.slot_regs["scalar"], st, 64, STEPS // 2)
                for j in range(G):
                    col = kn.local[:, 1, bass.ds(st.i * G + j + SLOTS // 2, 1)]
                    ch(e.activation(col, col, ACT.Identity, bias=r["key"][:, bass.ds(tiles[j], 1)], scale=-1.0))
            run_steps(e, ch, [(pick, 0)], STEPS // 2)
            ch.wait()

        def gpsimd(e, ch):
            e.wait_ge(r["at_ok"], 1)
            for b in range(NB):
                e.indirect_dma_start(r["ml"][:, b, :], None, kn.run_ml[:, :],
                                     bass.IndirectOffsetOnAxis(ap=r["at"][:, b:b + 1], axis=0), bounds_check=EP - 1
                                     ).then_inc(r["got"], 16)
            e.wait_ge(r["got"], 16 * NB)
        return dict(sync=sync, tensor=tensor, vector=vector, scalar=scalar, gpsimd=gpsimd)
    phase(kn, "l0t", build, psums=[("pk", [P, 2, BANK], F32)],
               sbufs=[("kr", [rows, 7, P], F32), ("key", [P, T], F32), ("f", [P, NB], F32), ("at", [P, NB], I32),
                      ("ml", [P, NB, 2 * HEADS], F32), ("l", [P, NB, HEADS], F32), ("small", [P, NB, 3 * HEADS], F32)],
               sems=["kld", "st", "small_ok", "turned", "keys_ok", "at_ok", "got"])

def gather_stage(kn, e, r, table, width, used):
    def gather(st):
        wait_step(e, r["idx_ok"], st)
        wait_step(e, used, st, 4)
        take_waits(e, kn.tally)
        for j in range(G):
            e.indirect_dma_start(r["rows"][:, st.quad, j, 0:width], None, table[:, :],
                                 bass.IndirectOffsetOnAxis(ap=r["idx"][:, st.par, j:j + 1], axis=0),
                                 bounds_check=NP - 1).then_inc(r["got"][st.par], 16)
    return gather

def idx_stage(kn, e, r, columns, sems, n=G):
    def idx(st):
        wait_free(e, r[sems], st, n)
        e.tensor_copy(r["idx"][:, st.par, :], columns[:, bass.ds(st.i * G, G)]).then_inc(r["idx_ok"], 1)
    return idx

def l0_edges(kn):
    def build(r):
        def gpsimd(e, ch):
            run_steps(e, ch, [(gather_stage(kn, e, r, kn.by_src, T1W, r["msg_ok"]), 0)], STEPS, RING)

        def vector(e, ch):
            idx = idx_stage(kn, e, r, kn.src_of, "got")
            hot = hot_stage(kn, e, r, 0, r["summed"])

            def alpha(st):
                wait_load(e, r["got"], st, G)
                wait_step(e, r["msg_ok"], st, 2)
                a, rows = r["a"][:, st.par, :, :], r["rows"][:, st.quad, :, :]
                sj = kn.slot_sj[:, bass.ds(st.i * G * HEADS, G * HEADS)].rearrange("p (j k) -> p j k", k=HEADS)
                ch.wait()
                ch(e.tensor_tensor(a, rows[:, :, H:H + HEADS], sj, ALU.add))
                ch.wait()
                ch(e.scalar_tensor_tensor(a, a, 0.2, a, ALU.mult, ALU.max))
                ch.wait()
                e.tensor_tensor(a, a, rows[:, :, H + HEADS:H + 2 * HEADS], ALU.subtract).then_inc(r["a_ok"], 1)

            def msg(st):
                wait_step(e, r["exp_ok"], st)
                wait_step(e, r["summed"], st, 2)
                a, rows = r["a"][:, st.par, :, :], r["rows"][:, st.quad, :, :]
                ch(e.tensor_tensor(a, a, rows[:, :, H + 2 * HEADS:T1W], ALU.mult))
                ch.wait()
                e.tensor_tensor(r["msg"][:, st.par, :, :].rearrange("p j (k c) -> p j k c", k=HEADS),
                                rows[:, :, 0:H].rearrange("p j (k c) -> p j k c", k=HEADS),
                                a.unsqueeze(3).to_broadcast([P, G, HEADS, H // HEADS]), ALU.mult
                                ).then_inc(r["msg_ok"], 1)
            run_steps(e, ch, [(idx, 0), (hot, 2), (alpha, 2), (msg, 3), (add_stage(kn, e, ch, r, 0), 4)], STEPS, RING)
            e.wait_ge(r["added"], STEPS)

        def scalar(e, ch):
            def exp(st):
                wait_step(e, r["a_ok"], st)
                e.activation(r["a"][:, st.par, :, :], r["a"][:, st.par, :, :], ACT.Exp).then_inc(r["exp_ok"], 1)
            run_steps(e, ch, [(exp, 0)], STEPS)

        def tensor(e, ch):
            def add(st):
                wait_step(e, r["hot"], st)
                wait_step(e, r["msg_ok"], st)
                wait_step(e, r["added"], st, 2)
                for j in range(G):
                    ins = e.matmul(r["pR"][:, st.par, j, :], r["oh"][:, st.par, j, :], r["msg"][:, st.par, j, :],
                                   start=True, stop=True)
                ins.then_inc(r["summed"], 1)
            run_steps(e, ch, [(add, 0)], STEPS)
        return dict(gpsimd=gpsimd, vector=vector, scalar=scalar, tensor=tensor)
    phase(kn, "l0e", build, psums=[("pR", [P, 2, G, P], F32)],
               sbufs=[("rows", [P, 4, G, T1W], F32), ("oh", [P, 2, G, P], F32), ("msg", [P, 2, G, H], F32),
                      ("a", [P, 2, G, HEADS], F32), ("idx", [P, 2, G], I32)],
               sems=["idx_ok", "hot", "a_ok", "exp_ok", "msg_ok", "summed", "added"], pairs=["got"])

def l0_close(kn):
    def build(r):
        def vector(e, ch):
            ch(e.tensor_scalar(r["none"][:, :], kn.count[:, 0, :], 0.0, None, ALU.is_equal))
            ch.wait()

            def add(st):
                x, xl, acc = (block(kn, t, st.i) for t in (kn.X, kn.TB, kn.AC))
                ch(e.scalar_tensor_tensor(acc, xl, r["none"][:, bass.ds(st.i, 1)], acc, ALU.mult, ALU.add))
                ch.wait()
                ch(e.tensor_tensor(x, x, acc, ALU.add))
            run_steps(e, ch, [(add, 0)], NB)
            ch.wait()
        return dict(vector=vector)
    phase(kn, "l0c", build, sbufs=[("none", [P, NB], F32)])

def fetch_stage(kn, e, r, src, name="fetched", buf="hb", used="turned"):
    def fetch(st):
        wait_step(e, r[used], st, 2)
        e.activation(r[buf][:, st.par, :], block(kn, src, st.i), ACT.Copy).then_inc(r[name], 1)
    return fetch

def turn_nodes(kn):
    def build(r):
        def scalar(e, ch):
            run_steps(e, ch, [(fetch_stage(kn, e, r, kn.Hn), 0)], NB)

        def tensor(e, ch):
            def turn(st):
                wait_step(e, r["fetched"], st)
                wait_step(e, r["copied"], st, 2)
                e.transpose(r["pA"][:, st.par, 0:P], r["hb"][:, st.par, :], kn.ident[:, :]).then_inc(r["turned"], 1)
            run_steps(e, ch, [(turn, 0)], NB)

        def vector(e, ch):
            def copy(st):
                wait_step(e, r["turned"], st)
                e.tensor_copy(block(kn, kn.Hn, st.i), r["pA"][:, st.par, 0:P]).then_inc(r["copied"], 1)
            run_steps(e, ch, [(copy, 0)], NB)
            e.wait_ge(r["copied"], NB)
        return dict(scalar=scalar, tensor=tensor, vector=vector)
    phase(kn, "l1f", build, psums=[("pA", [P, 2, BANK], F32)], sbufs=[("hb", [P, 2, P], F32)],
          sems=["fetched", "turned", "copied"])

def part(r, st):
    return r["part"][:, bass.ds(st.i * SEC, SEC)]

def log_sections(kn, e, ch, r, wait, done):
    def exp(st):
        wait(st)
        ch(e.activation(part(r, st), part(r, st), ACT.Exp))

    def log(st):
        e.activation(part(r, st), part(r, st), ACT.Ln, bias=kn.half1[:, 0:1], scale=0.5).then_inc(done, 1)
    run_steps(e, ch, [(exp, 0)], NSEC)
    ch.wait()
    run_steps(e, ch, [(log, 0)], NSEC)

def minus_abs_stage(kn, e, r, src, done):
    def minus_abs(st):
        e.scalar_tensor_tensor(part(r, st), sec(kn, src, st), -1.0, sec(kn, src, st), ALU.mult, ALU.min
                               ).then_inc(done, 1)
    return minus_abs

def ssp_stage(kn, e, r, dst, src, logs, done):
    def ssp(st):
        wait_step(e, logs, st)
        e.scalar_tensor_tensor(sec(kn, dst, st), sec(kn, src, st), 0.0, part(r, st), ALU.max, ALU.add).then_inc(done, 1)
    return ssp

def biased_stage(kn, e, ch, r, dst, b, done):
    def biased(st):
        wait_step(e, r["lin_ok"], st)
        ch(e.tensor_scalar(sec(kn, dst, st), r["p"][:, st.par, 0:SEC], vec(kn, b), None, ALU.add))
        ch.wait()
        e.scalar_tensor_tensor(part(r, st), sec(kn, dst, st), -1.0, sec(kn, dst, st), ALU.mult, ALU.min
                               ).then_inc(done, 1)
    return biased

def product_stage(kn, e, w, src, ready, free, bank, done):
    def lin(st):
        wait_step(e, ready, st)
        wait_step(e, free, st, 2)
        e.matmul(bank[:, st.par, 0:SEC], mat(kn, w), sec(kn, src, st), start=True, stop=True).then_inc(done, 1)
    return lin

def layers(kn, name, dst, src, w1, b1, w2, b2, scale=None):
    inner = kn.TB if w1 else kn.MT

    def build(r):
        def vector(e, ch):
            run_steps(e, ch, [(minus_abs_stage(kn, e, r, src, r["n1"]), 0)], NSEC)
            stages = [(ssp_stage(kn, e, r, kn.MT, src, r["log1"], r["ssp1"]), 0)]
            if w1:
                stages.append((biased_stage(kn, e, ch, r, kn.TB, b1, r["n2"]), 2))
                run_steps(e, ch, stages, NSEC)
                stages = [(ssp_stage(kn, e, r, kn.TB, kn.TB, r["log2"], r["ssp2"]), 0)]

            def add(st):
                d = sec(kn, dst, st)
                if scale is not None:
                    ch(e.tensor_scalar(d, d, vec(kn, scale), None, ALU.mult))
                    ch.wait()
                wait_step(e, r["out_ok"], st)
                e.scalar_tensor_tensor(d, r["q"][:, st.par, 0:SEC], vec(kn, b2), d, ALU.add, ALU.add
                                       ).then_inc(r["done"], 1)
            run_steps(e, ch, stages + [(add, 2)], NSEC)
            e.wait_ge(r["done"], NSEC)

        def scalar(e, ch):
            log_sections(kn, e, ch, r, lambda st: wait_step(e, r["n1"], st), r["log1"])
            if w1:
                log_sections(kn, e, ch, r, lambda st: wait_step(e, r["n2"], st), r["log2"])

        def tensor(e, ch):
            if w1:
                run_steps(e, ch, [(product_stage(kn, e, w1, kn.MT, r["ssp1"], r["n2"], r["p"], r["lin_ok"]), 0)], NSEC)
            run_steps(e, ch, [(product_stage(kn, e, w2, inner, r["ssp2" if w1 else "ssp1"], r["done"], r["q"],
                                             r["out_ok"]), 0)], NSEC)
        return dict(vector=vector, scalar=scalar, tensor=tensor)
    phase(kn, name, build, psums=[(n, [P, 2, BANK], F32) for n in ("p", "q")], sbufs=[("part", [P, NP], F32)],
          sems=["n1", "log1", "ssp1", "lin_ok", "n2", "log2", "ssp2", "out_ok", "done"])

def l1_nodes_i(kn):
    def build(r):
        def vector(e, ch):
            run_steps(e, ch, [(minus_abs_stage(kn, e, r, kn.Hn, r["n1"]), 0)], NSEC)
            run_steps(e, ch, [(ssp_stage(kn, e, r, kn.MT, kn.Hn, r["log1"], r["ssp1"]), 0),
                              (biased_stage(kn, e, ch, r, kn.AC, "bi", r["n2"]), 2)], NSEC)
            run_steps(e, ch, [(ssp_stage(kn, e, r, kn.AC, kn.AC, r["log2"], r["ssp2"]), 0)], NSEC)
            e.wait_ge(r["ssp2"], NSEC)

        def scalar(e, ch):
            log_sections(kn, e, ch, r, lambda st: wait_step(e, r["n1"], st), r["log1"])
            log_sections(kn, e, ch, r, lambda st: wait_step(e, r["n2"], st), r["log2"])

        def tensor(e, ch):
            run_steps(e, ch, [(product_stage(kn, e, "Wi", kn.MT, r["ssp1"], r["n2"], r["p"], r["lin_ok"]), 0)], NSEC)
        return dict(vector=vector, scalar=scalar, tensor=tensor)
    phase(kn, "l1i", build, psums=[("p", [P, 2, BANK], F32)], sbufs=[("part", [P, NP], F32)],
          sems=["n1", "log1", "ssp1", "lin_ok", "n2", "log2", "ssp2"])

def l1_nodes_j(kn):
    def build(r):
        def scalar(e, ch):
            run_steps(e, ch, [(fetch_stage(kn, e, r, kn.MT, used="lin_ok"), 0)], NB)
            e.wait_ge(r["n1"], NB)
            log_sections(kn, e, ch, r, lambda st: None, r["log1"])

        def tensor(e, ch):
            def lin(st):
                wait_step(e, r["fetched"], st)
                wait_step(e, r["n1"], st, 2)
                e.matmul(r["p"][:, st.par, 0:P], r["hb"][:, st.par, :], mat(kn, "Wj"), start=True, stop=True
                         ).then_inc(r["lin_ok"], 1)
            run_steps(e, ch, [(lin, 0)], NB)

        def vector(e, ch):
            def biased(st):
                wait_step(e, r["lin_ok"], st)
                ch(e.tensor_tensor(block(kn, kn.TB, st.i), r["p"][:, st.par, 0:P], row(kn, "bj"), ALU.add))
                ch.wait()
                e.scalar_tensor_tensor(r["part"][:, bass.ds(st.i * P, P)], block(kn, kn.TB, st.i), -1.0,
                                       block(kn, kn.TB, st.i), ALU.mult, ALU.min).then_inc(r["n1"], 1)
            run_steps(e, ch, [(biased, 0)], NB)
            run_steps(e, ch, [(ssp_stage(kn, e, r, kn.TB, kn.TB, r["log1"], r["ssp1"]), 0)], NSEC)
            e.wait_ge(r["ssp1"], NSEC)
        return dict(scalar=scalar, tensor=tensor, vector=vector)
    phase(kn, "l1j", build, psums=[("p", [P, 2, BANK], F32)], sbufs=[("part", [P, NP], F32), ("hb", [P, 2, P], F32)],
          sems=["fetched", "lin_ok", "n1", "log1", "ssp1"])

def load_records(kn, e, r, column, width, used):

    def load(st):
        tiles = slot_values(kn, e, kn.slot_regs["sync"], st, 0)
        wait_step(e, used, st, 2)
        for j in range(G):
            e.dma_start(r["rec"][:, st.par, j, 0:width], kn.sorted[bass.ds(tiles[j] * P, P), column:column + width]
                        ).then_inc(r["ld"][st.par], 16)
    return load

def scatter_stage(kn, e, r):
    def send(st):
        wait_step(e, r["prod_ok"], st)
        wait_step(e, r["idx_ok"], st)
        take_waits(e, kn.tally)
        for j in range(G):
            e.indirect_dma_start(kn.products[:, :],
                                 bass.IndirectOffsetOnAxis(ap=r["idx"][:, st.par, j:j + 1], axis=0),
                                 r["prod"][:, st.par, j, :], None, bounds_check=EP - 1, oob_is_err=False
                                 ).then_inc(r["sent"][st.par], 16)
    return send

def scatter_all(kn, e, ch, r):
    run_steps(e, ch, [(scatter_stage(kn, e, r), 0)], STEPS)
    for j in range(2):
        e.wait_ge(r["sent"][j], 16 * G * (STEPS // 2))

def l1_edges(kn):
    def build(r):
        def sync(e, ch):
            run_steps(e, ch, [(load_records(kn, e, r, C64, A64, r["rec_turned"]), 0)], STEPS)

        def tensor(e, ch):
            turn_hot = turn_hot_stage(kn, e, r, ident=kn.identb)

            def turn_rec(st):
                wait_load(e, r["ld"], st, G)
                wait_step(e, r["dT_ok"], st, 2)
                take_waits(e, kn.tally)
                for j in range(G):
                    ins = e.transpose(r["pD"][0:A64, st.par, j, :], r["rec"][:, st.par, j, :], kn.ident[:, :])
                ins.then_inc(r["rec_turned"], 1)


            def mults(st):
                blocks = slot_values(kn, e, kn.slot_regs["tensor"], st, 32)
                wait_step(e, r["dT_ok"], st)
                wait_step(e, r["g_ok"], st, 2)
                for j in range(G):
                    ins = e.matmul(r["pG"][:, st.par, j, :], r["dT"][0:A64, st.par, j, :], mat(kn, "Wdesc", A64),
                                   start=True, stop=True)
                ins.then_inc(r["g_done"], 1)
                wait_step(e, r["ohT_ok"], st)
                wait_step(e, r["prod_ok"], st, 2)
                for j in range(G):
                    ins = e.matmul(r["pX"][:, st.par, j, :], r["ohT"][:, st.par, j, :], block(kn, kn.TB, blocks[j]),
                                   start=True, stop=True)
                ins.then_inc(r["picked"], 1)
            run_steps(e, ch, [(turn_rec, 1), (turn_hot, 1), (mults, 2)], STEPS)

        def scalar(e, ch):
            def copy_rec(st):
                wait_step(e, r["rec_turned"], st)
                wait_step(e, r["g_done"], st, 2)
                e.activation(r["dT"][0:A64, st.par, :, :], r["pD"][0:A64, st.par, :, :], ACT.Copy).then_inc(r["dT_ok"], 1)

            def copy_g(st):
                wait_step(e, r["g_done"], st)
                wait_step(e, r["prod_ok"], st, 2)
                e.activation(r["g"][:, st.par, :, :], r["pG"][:, st.par, :, :], ACT.Copy).then_inc(r["g_ok"], 1)
            run_steps(e, ch, [(copy_rec, 1), (copy_hot_stage(kn, e, r, r["picked"]), 1), (copy_g, 2)], STEPS)

        def vector(e, ch):
            def prod(st):
                wait_step(e, r["g_ok"], st)
                wait_step(e, r["picked"], st)
                wait_free(e, r["sent"], st, G)
                e.tensor_tensor(r["prod"][:, st.par, :, :], r["g"][:, st.par, :, :], r["pX"][:, st.par, :, :], ALU.mult
                                ).then_inc(r["prod_ok"], 1)
            run_steps(e, ch, [(hot_stage(kn, e, r, 0, r["turned"], iota=kn.iotab), 0), (prod, 3),
                              (idx_stage(kn, e, r, kn.place, "sent"), 3)], STEPS)

        def gpsimd(e, ch):
            scatter_all(kn, e, ch, r)
        return dict(sync=sync, tensor=tensor, scalar=scalar, vector=vector, gpsimd=gpsimd)
    phase(kn, "l1e", build, psums=[("pT", [P, 2, 2 * G, P], BF16)] + [(n, [P, 2, G, P], F32) for n in ("pD", "pG", "pX")],
               sbufs=[("rec", [P, 2, G, A64], F32), ("oh", [P, 2, G, P], BF16), ("ohT", [P, 2, G, P], F32),
                      ("dT", [A64, 2, G, P], F32), ("g", [P, 2, G, P], F32), ("prod", [P, 2, G, P], F32),
                      ("idx", [P, 2, G], I32)],
               sems=["hot", "turned", "ohT_ok", "rec_turned", "dT_ok", "g_done", "g_ok", "picked", "prod_ok", "idx_ok"],
               pairs=["ld", "sent"])

def sum_by_src(kn, name, clear=False):
    def rows(st, j):
        return flat(kn, kn.MT)[:, bass.ds((st.quad * G + j) * P, P)]

    def build(r):
        def sync(e, ch):
            def load(st):
                tiles = slot_values(kn, e, kn.slot_regs["sync"], st, 64)
                wait_step(e, r["summed"], st, 4)
                for j in range(G):
                    e.dma_start(rows(st, j), kn.products[bass.ds(tiles[j] * P, P), :]).then_inc(r[f"ld{st.quad}"], 16)
            run_steps(e, ch, [(load, 0)], STEPS, RING)

        def vector(e, ch):
            if clear:
                ch(e.memset(kn.AC[:, :, :], 0.0))
                ch.wait()
            run_steps(e, ch, [(add_stage(kn, e, ch, r, 1), 0)], STEPS)
            e.wait_ge(r["added"], STEPS)

        def scalar(e, ch):
            run_steps(e, ch, [(scalar_hot_stage(kn, e, ch, r, 1, lambda st: r["oh"][:, st.par, :, :], r["summed"], 2), 0)],
                      STEPS)

        def tensor(e, ch):
            def add(st):
                wait_step(e, r["hot"], st)
                e.wait_ge(r[f"ld{st.quad}"], st.fourth * (16 * G) + 16 * G)
                wait_step(e, r["added"], st, 2)
                for j in range(G):
                    ins = e.matmul(r["pR"][:, st.par, j, :], rows(st, j), r["oh"][:, st.par, j, :],
                                   start=True, stop=True)
                ins.then_inc(r["summed"], 1)
            run_steps(e, ch, [(add, 0)], STEPS, RING)
        return dict(sync=sync, vector=vector, tensor=tensor, scalar=scalar)
    phase(kn, name, build, psums=[("pR", [P, 2, G, P], F32)],
               sbufs=[("oh", [P, 2, G, P], F32)],
               sems=["hot", "summed", "added", "ld0", "ld1", "ld2", "ld3"])

def sec(kn, t, st):
    return flat(kn, t)[:, bass.ds(st.i * SEC, SEC)]

def linear_ssp(kn, name, dst, src, w, b):
    def build(r):
        def vector(e, ch):
            run_steps(e, ch, [(biased_stage(kn, e, ch, r, dst, b, r["n1"]), 0)], NSEC)
            run_steps(e, ch, [(ssp_stage(kn, e, r, dst, dst, r["log1"], r["ssp1"]), 0)], NSEC)
            e.wait_ge(r["ssp1"], NSEC)

        def scalar(e, ch):
            log_sections(kn, e, ch, r, lambda st: wait_step(e, r["n1"], st), r["log1"])

        def tensor(e, ch):
            def lin(st):
                wait_step(e, r["n1"], st, 2)
                e.matmul(r["p"][:, st.par, 0:SEC], mat(kn, w), sec(kn, src, st), start=True, stop=True
                         ).then_inc(r["lin_ok"], 1)
            run_steps(e, ch, [(lin, 0)], NSEC)
        return dict(vector=vector, scalar=scalar, tensor=tensor)
    phase(kn, name, build, psums=[("p", [P, 2, BANK], F32)], sbufs=[("part", [P, NP], F32)],
          sems=["lin_ok", "n1", "log1", "ssp1"])

def l1_layers(kn):
    for k in range(3):
        layers(kn, f"ri{k}", kn.AC, kn.AC, f"Wri1_{k}", f"bri1_{k}", f"Wri2_{k}", f"bri2_{k}")
    layers(kn, "dense", kn.Hn, kn.AC, None, None, "Wd", "bd", "u")
    for k in range(2):
        layers(kn, f"ra{k}", kn.Hn, kn.Hn, f"Wra1_{k}", f"bra1_{k}", f"Wra2_{k}", f"bra2_{k}")

def add_turned(kn, name, src, also=None):
    def build(r):
        def scalar(e, ch):
            run_steps(e, ch, [(fetch_stage(kn, e, r, src), 0)], NB)

        def tensor(e, ch):
            def turn(st):
                wait_step(e, r["fetched"], st)
                wait_step(e, r["added"], st, 2)
                e.transpose(r["pA"][:, st.par, 0:P], r["hb"][:, st.par, :], kn.ident[:, :]).then_inc(r["turned"], 1)
            run_steps(e, ch, [(turn, 0)], NB)

        def vector(e, ch):
            def add(st):
                x = block(kn, kn.X, st.i)
                if also is not None:
                    ch(e.tensor_tensor(x, x, block(kn, also, st.i), ALU.add))
                    ch.wait()
                wait_step(e, r["turned"], st)
                e.tensor_tensor(x, x, r["pA"][:, st.par, 0:P], ALU.add).then_inc(r["added"], 1)
            run_steps(e, ch, [(add, 0)], NB)
            ch(e.memset(kn.AC[:, :, :], 0.0))
            ch.wait()
            e.wait_ge(r["added"], NB)
        return dict(scalar=scalar, tensor=tensor, vector=vector)
    phase(kn, name, build, psums=[("pA", [P, 2, BANK], F32)], sbufs=[("hb", [P, 2, P], F32)],
               sems=["fetched", "turned", "added"])

def tables(kn, name, w_table, w_rows=None, bias=None, rows=None):
    def build(r):
        def tensor(e, ch):
            def turn(st):
                wait_step(e, r["fetched"], st)
                wait_step(e, r["hT_ok"], st, 2)
                e.transpose(r["pA"][:, st.par, 0:P], r["hb"][:, st.par, :], kn.ident[:, :]).then_inc(r["turned"], 1)

            def lin(st):
                wait_step(e, r["hT_ok"], st)
                wait_step(e, r["tab_ok"], st, 2)
                if w_rows:
                    e.matmul(r["pC"][:, st.par, 0:P], r["hT"][:, st.par, :], mat(kn, w_rows), start=True, stop=True)
                e.matmul(r["pB"][:, st.par, 0:P], r["hT"][:, st.par, :], mat(kn, w_table), start=True, stop=True
                         ).then_inc(r["lin_ok"], 1)
            run_steps(e, ch, [(turn, 0), (lin, 1)], NB)

        def scalar(e, ch):
            def copy(st):
                wait_step(e, r["turned"], st)
                wait_step(e, r["lin_ok"], st, 2)
                e.activation(r["hT"][:, st.par, :], r["pA"][:, st.par, 0:P], ACT.Copy).then_inc(r["hT_ok"], 1)
            run_steps(e, ch, [(fetch_stage(kn, e, r, kn.Hn), 0), (copy, 0)], NB)

        def vector(e, ch):
            def out(st):
                wait_step(e, r["lin_ok"], st)
                if w_rows:
                    wait_free(e, r["st"], st, 1)
                    ch(e.tensor_tensor(r["a"][:, st.par, :], r["pC"][:, st.par, 0:P], row(kn, bias), ALU.add))
                e.tensor_copy(block(kn, kn.TB, st.i), r["pB"][:, st.par, 0:P]).then_inc(r["tab_ok"], 1)
            run_steps(e, ch, [(out, 0)], NB)
            e.wait_ge(r["tab_ok"], NB)

        def sync(e, ch):
            def store(st):
                wait_step(e, r["tab_ok"], st)
                e.dma_start(rows[bass.ds(st.i * P, P), :], r["a"][:, st.par, :]).then_inc(r["st"][st.par], 16)
            run_steps(e, ch, [(store, 0)], NB)
            e.wait_ge(r["st"][0], 16 * (NB - NB // 2))
            e.wait_ge(r["st"][1], 16 * (NB // 2))
        d = dict(tensor=tensor, scalar=scalar, vector=vector)
        if w_rows:
            d["sync"] = sync
        return d
    phase(kn, name, build, psums=[(n, [P, 2, BANK], F32) for n in ("pA", "pB", "pC")],
               sbufs=[(n, [P, 2, P], F32) for n in ("hb", "hT", "a")],
               sems=["fetched", "turned", "hT_ok", "lin_ok", "tab_ok"], pairs=["st"])

def l2_edges(kn):
    def one_hot(st, j):
        return flat(kn, kn.MT)[:, bass.ds((st.ring * G + j) * P, P)]

    def one_hots_of(st):
        return flat(kn, kn.MT)[:, bass.ds(st.ring * G * P, G * P)].rearrange("p (j c) -> p j c", j=G)

    def build(r):
        def gpsimd(e, ch):
            run_steps(e, ch, [(gather_stage(kn, e, r, kn.l2_rows, H, r["v_ok"]), 0)], STEPS, RING)

        def tensor(e, ch):
            def turn(st):
                wait_step(e, r["hot"], st)
                wait_step(e, r["ohT_ok"], st, 2)
                for j in range(G):
                    ins = e.transpose(r["pT"][:, st.par, j, :], one_hot(st, j), kn.ident[:, :])
                ins.then_inc(r["turned"], 1)

            def v(st):
                blocks = slot_values(kn, e, kn.slot_regs["tensor"], st, 32)
                wait_load(e, r["got"], st, G)
                wait_step(e, r["normed"], st, 4)
                e.matmul(r["pV"][:, st.quad, :, :].rearrange("p j c -> p (j c)"), kn.ident[:, :],
                         r["rows"][:, st.quad, :, :].rearrange("p j c -> p (j c)"), start=True, stop=False,
                         skip_group_check=True)
                wait_step(e, r["ohT_ok"], st)
                for j in range(G):
                    ins = e.matmul(r["pV"][:, st.quad, j, :], r["ohT"][:, st.par, j, :], block(kn, kn.TB, blocks[j]),
                                   start=False, stop=(j == G - 1), skip_group_check=True)
                ins.then_inc(r["v_ok"], 1)

            def add(st):
                wait_step(e, r["z_ok"], st)
                wait_step(e, r["added"], st, 2)
                for j in range(G):
                    ins = e.matmul(r["pR"][:, st.par, j, :], one_hot(st, j), r["z"][:, st.quad, j, :],
                                   start=True, stop=True)
                ins.then_inc(r["summed"], 1)
            run_steps(e, ch, [(turn, 1), (v, 2), (add, 6)], STEPS, RING)

        def scalar(e, ch):
            def root(st):
                wait_step(e, r["stats"], st)
                e.activation(r["std"][:, st.par, :], r["mv"][:, st.par, :, 1], ACT.Sqrt, bias=kn.eps1[:, 0:1]
                             ).then_inc(r["std_ok"], 1)

            def norm(st):
                wait_step(e, r["scales"], st)
                wait_step(e, r["summed"], st, 4)
                for j in range(G):
                    ins = e.activation(r["z"][:, st.quad, j, :], r["pV"][:, st.quad, j, :], ACT.Identity,
                                       bias=r["shift"][:, st.par, j:j + 1], scale=r["rstd"][:, st.par, j:j + 1])
                ins.then_inc(r["normed"], 1)
            hot = scalar_hot_stage(kn, e, ch, r, 0, one_hots_of, r["summed"], RING)
            run_steps(e, ch, [(root, 3), (norm, 4), (copy_hot_stage(kn, e, r, r["v_ok"]), 1), (hot, 0)], STEPS, RING)

        def vector(e, ch):
            def stats(st):
                wait_step(e, r["v_ok"], st)
                wait_step(e, r["normed"], st, 2)
                ch.wait()
                for j in range(G):
                    ch(e.bn_stats(r["six"][:, st.par, j, :], r["pV"][:, st.quad, j, :]))
                ch.wait()
                take_waits(e, kn.tally)
                for j in range(G):
                    ins = e.bn_aggr(r["mv"][:, st.par, j, :], r["six"][:, st.par, j, :])
                    if j < G - 1:
                        ch(ins)
                ins.then_inc(r["stats"], 1)

            def scales(st):
                wait_step(e, r["std_ok"], st)
                wait_step(e, r["normed"], st, 2)
                ch(e.reciprocal(r["rstd"][:, st.par, :], r["std"][:, st.par, :]))
                ch.wait()
                e.scalar_tensor_tensor(r["shift"][:, st.par, :], r["mv"][:, st.par, :, 0], -1.0, r["rstd"][:, st.par, :],
                                       ALU.mult, ALU.mult).then_inc(r["scales"], 1)

            def act(st):
                wait_step(e, r["normed"], st)
                z = r["z"][:, st.quad, :, :]
                ch(e.tensor_tensor(z, z, row(kn, "msg_g").unsqueeze(1).to_broadcast([P, G, H]), ALU.mult))
                ch.wait()
                ch(e.tensor_tensor(z, z, row(kn, "msg_beta").unsqueeze(1).to_broadcast([P, G, H]), ALU.add))
                ch.wait()
                for j in range(G):
                    ins = e.tensor_scalar(r["z"][:, st.quad, j, :], r["z"][:, st.quad, j, :], 0.0,
                                          kn.wt[:, bass.ds(st.i * G + j, 1)], ALU.max, ALU.mult)
                ins.then_inc(r["z_ok"], 1)
            run_steps(e, ch, [(scales, 4), (stats, 3), (act, 5), (idx_stage(kn, e, r, kn.src_of, "got"), 0),
                              (add_stage(kn, e, ch, r, 0), 7)], STEPS, RING)
            e.wait_ge(r["added"], STEPS)
        return dict(gpsimd=gpsimd, tensor=tensor, scalar=scalar, vector=vector)
    phase(kn, "l2e", build, psums=[("pT", [P, 2, G, P], F32), ("pV", [P, 4, G, P], F32), ("pR", [P, 2, G, P], F32)],
               sbufs=[("rows", [P, 4, G, H], F32), ("ohT", [P, 2, G, P], F32),
                      ("z", [P, 4, G, H], F32), ("six", [P, 2, G, 6], F32), ("mv", [P, 2, G, 2], F32),
                      ("std", [P, 2, G], F32), ("rstd", [P, 2, G], F32), ("shift", [P, 2, G], F32), ("idx", [P, 2, G], I32)],
               sems=["idx_ok", "hot", "turned", "ohT_ok", "v_ok", "stats", "std_ok", "scales", "normed", "z_ok",
                     "summed", "added"], pairs=["got"])

def l2_update(kn):
    def build(r):
        def vector(e, ch):
            ch(e.tensor_scalar(r["f"][:, :], kn.count[:, 0, :], 1e-8, None, ALU.add))
            ch(e.tensor_scalar(r["valid"][:, :], kn.count[:, 0, :], 0.0, None, ALU.is_gt))
            ch.wait()
            ch(e.reciprocal(r["f"][:, :], r["f"][:, :]))
            ch.wait()
            ch(e.tensor_tensor(r["f"][:, :], r["f"][:, :], r["valid"][:, :], ALU.mult))
            ch.wait()

            def mean(st):
                wait_step(e, r["turned"], st, 2)
                e.tensor_scalar(r["mb"][:, st.par, :], block(kn, kn.AC, st.i), r["f"][:, bass.ds(st.i, 1)], None,
                                ALU.mult).then_inc(r["mean_ok"], 1)

            def out(st):
                wait_step(e, r["lin_ok"], st)
                e.tensor_tensor(block(kn, kn.TB, st.i), r["pC"][:, st.par, 0:P], row(kn, "upd_b"), ALU.add
                                ).then_inc(r["out_ok"], 1)
            run_steps(e, ch, [(mean, 0), (out, 1)], NB)
            e.wait_ge(r["out_ok"], NB)

        def tensor(e, ch):
            def turn(st):
                wait_step(e, r["fetched"], st)
                wait_step(e, r["mean_ok"], st)
                wait_step(e, r["T_ok"], st, 2)
                e.transpose(r["pA"][:, st.par, 0:P], r["hb"][:, st.par, :], kn.ident[:, :])
                e.transpose(r["pA"][:, st.par, P:2 * P], r["mb"][:, st.par, :], kn.ident[:, :]).then_inc(r["turned"], 1)

            def lin(st):
                wait_step(e, r["T_ok"], st)
                wait_step(e, r["out_ok"], st, 2)
                e.matmul(r["pC"][:, st.par, 0:P], r["T"][:, st.par, 0:P], mat(kn, "upd_top"), start=True, stop=False)
                e.matmul(r["pC"][:, st.par, 0:P], r["T"][:, st.par, P:2 * P], mat(kn, "upd_bottom"), start=False,
                         stop=True).then_inc(r["lin_ok"], 1)
            run_steps(e, ch, [(turn, 0), (lin, 1)], NB)

        def scalar(e, ch):
            def copy(st):
                wait_step(e, r["turned"], st)
                wait_step(e, r["lin_ok"], st, 2)
                e.activation(r["T"][:, st.par, :], r["pA"][:, st.par, 0:2 * P], ACT.Copy).then_inc(r["T_ok"], 1)
            run_steps(e, ch, [(fetch_stage(kn, e, r, kn.Hn), 0), (copy, 0)], NB)
        return dict(vector=vector, tensor=tensor, scalar=scalar)
    phase(kn, "l2u", build, psums=[(n, [P, 2, BANK], F32) for n in ("pA", "pC")],
               sbufs=[("hb", [P, 2, P], F32), ("mb", [P, 2, P], F32), ("T", [P, 2, 2 * P], F32), ("f", [P, NB], F32),
                      ("valid", [P, NB], F32)],
               sems=["fetched", "mean_ok", "turned", "T_ok", "lin_ok", "out_ok"])

def l2_close(kn):
    X, Hn, MT, AC = (t[:, :, :] for t in (kn.X, kn.Hn, kn.MT, kn.AC))

    def over(name):
        return row(kn, name).unsqueeze(1).to_broadcast([P, NB, H])

    def build(r):
        def vector(e, ch):
            ch(e.tensor_tensor(AC, Hn, over("gate_w"), ALU.mult))
            ch(e.tensor_tensor(MT, MT, over("upd_g"), ALU.mult))
            ch(e.tensor_tensor(X, X, Hn, ALU.add))
            ch.wait()
            ch(e.tensor_reduce(r["z"][:, :], AC, AX, ALU.add))
            ch(e.tensor_tensor(MT, MT, over("upd_beta"), ALU.add))
            ch.wait()
            e.tensor_scalar(r["z"][:, :], r["z"][:, :], row(kn, "gate_b")[:, 0:1], None, ALU.add).then_inc(r["z_ok"], 1)
            ch(e.scalar_tensor_tensor(MT, MT, 0.0, Hn, ALU.max, ALU.subtract))
            e.wait_ge(r["exp_ok"], 1)
            ch(e.tensor_scalar(r["z"][:, :], r["z"][:, :], 1.0, None, ALU.add))
            ch.wait()
            ch(e.reciprocal(r["g"][:, :], r["z"][:, :]))
            ch.wait()
            ch(e.tensor_tensor(MT, MT, r["g"][:, :].unsqueeze(2).to_broadcast([P, NB, H]), ALU.mult))
            ch.wait()
            ch(e.tensor_tensor(X, X, MT, ALU.add))
            ch.wait()

        def scalar(e, ch):
            e.wait_ge(r["z_ok"], 1)
            e.activation(r["z"][:, :], r["z"][:, :], ACT.Exp, scale=-1.0).then_inc(r["exp_ok"], 1)
        return dict(vector=vector, scalar=scalar)
    phase(kn, "l2c", build, sbufs=[("z", [P, NB], F32), ("g", [P, NB], F32)], sems=["z_ok", "exp_ok"])

def l3_edges(kn):
    ring = lambda t, st: flat(kn, t)[:, bass.ds(st.ring * G * P, G * P)]
    hidden, logs = kn.AC, kn.MT

    def build(r):
        def sync(e, ch):
            run_steps(e, ch, [(load_records(kn, e, r, 0, A50, r["rec_turned"]), 0)], STEPS)

        def tensor(e, ch):
            turn_hot = turn_hot_stage(kn, e, r, 1, kn.identb)

            def turn_rec(st):
                wait_load(e, r["ld"], st, G)
                wait_step(e, r["dT_ok"], st, 1)
                take_waits(e, kn.tally)
                for j in range(G):
                    ins = e.transpose(r["pD"][0:A50, j, :], r["rec"][:, st.par, j, :], kn.ident[:, :])
                ins.then_inc(r["rec_turned"], 1)

            def hid(st):
                wait_step(e, r["dT_ok"], st)
                wait_step(e, r["y_ok"], st, 2)
                e.matmul(r["pH"][:, st.par, :], mat(kn, "mlp_w1", A50),
                         r["dT"][0:A50, st.par, :, :].rearrange("p j c -> p (j c)"), start=True, stop=True
                         ).then_inc(r["h_done"], 1)

            def mults(st):
                blocks = slot_values(kn, e, kn.slot_regs["tensor"], st, 32)
                wait_step(e, r["s_ok"], st)
                wait_step(e, r["w_ok"], st, 2)
                for j in range(G):
                    ins = e.matmul(r["pW"][:, st.par, j, :], ring(hidden, st)[:, j * P:(j + 1) * P], mat(kn, "mlp_w2"),
                                   start=True, stop=True)
                ins.then_inc(r["w_done"], 1)
                wait_step(e, r["ohT_ok"], st)
                wait_step(e, r["prod_ok"], st, 2)
                for j in range(G):
                    ins = e.matmul(r["pX"][:, st.par, j, :], r["ohT"][:, st.par, j, :], block(kn, kn.TB, blocks[j]),
                                   start=True, stop=True)
                ins.then_inc(r["picked"], 1)
            run_steps(e, ch, [(turn_rec, 0), (hid, 1), (turn_hot, 5), (mults, 6)], STEPS, RING)

        def scalar(e, ch):
            def copy_rec(st):
                wait_step(e, r["rec_turned"], st)
                wait_step(e, r["h_done"], st, 2)
                e.activation(r["dT"][0:A50, st.par, :, :], r["pD"][0:A50, :, :], ACT.Copy).then_inc(r["dT_ok"], 1)

            def y(st):
                wait_step(e, r["h_done"], st)
                wait_step(e, r["w_done"], st, RING)
                e.activation(ring(hidden, st), r["pH"][:, st.par, :], ACT.Identity, bias=vec(kn, "mlp_b1")
                             ).then_inc(r["y_ok"], 1)

            def exp(st):
                wait_step(e, r["n_ok"], st)
                e.activation(ring(logs, st), ring(logs, st), ACT.Exp).then_inc(r["e_ok"], 1)

            def log(sts):
                for st in sts:
                    wait_step(e, r["e_ok"], st)
                    e.activation(ring(logs, st), ring(logs, st), ACT.Ln, bias=kn.half1[:, 0:1], scale=0.5
                                 ).then_inc(r["l_ok"], 1)
            run_steps(e, ch, [(copy_rec, 0), (copy_hot_stage(kn, e, r, r["picked"], 1), 5), (y, 1), (exp, 1),
                              (log, QUAD, QUAD)], STEPS, RING)

        def vector(e, ch):
            def minus_abs(st):
                wait_step(e, r["y_ok"], st)
                wait_step(e, r["s_ok"], st, RING)
                e.scalar_tensor_tensor(ring(logs, st), ring(hidden, st), -1.0, ring(hidden, st), ALU.mult, ALU.min
                                       ).then_inc(r["n_ok"], 1)

            def ssp(st):
                wait_step(e, r["l_ok"], st)
                e.scalar_tensor_tensor(ring(hidden, st), ring(hidden, st), 0.0, ring(logs, st), ALU.max, ALU.add
                                       ).then_inc(r["s_ok"], 1)

            def prod(st):
                wait_step(e, r["w_done"], st)
                wait_free(e, r["sent"], st, G)
                e.tensor_tensor(r["prod"][:, st.par, :, :], r["pW"][:, st.par, :, :],
                                row(kn, "mlp_b2").unsqueeze(1).to_broadcast([P, G, H]), ALU.add).then_inc(r["w_ok"], 1)
                wait_step(e, r["picked"], st)
                wait_step(e, r["w_ok"], st)
                for j in range(G):
                    out = r["prod"][:, st.par, j, :]
                    ins = e.scalar_tensor_tensor(out, r["pX"][:, st.par, j, :], kn.cut[:, bass.ds(st.i * G + j, 1)], out,
                                                 ALU.mult, ALU.mult)
                ins.then_inc(r["prod_ok"], 1)
            run_steps(e, ch, [(hot_stage(kn, e, r, 0, r["turned"], iota=kn.iotab), 4), (minus_abs, 1), (ssp, 5), (prod, 7),
                              (idx_stage(kn, e, r, kn.place, "sent"), 7)], STEPS, RING)

        def gpsimd(e, ch):
            scatter_all(kn, e, ch, r)
        return dict(sync=sync, tensor=tensor, scalar=scalar, vector=vector, gpsimd=gpsimd)
    phase(kn, "l3e", build, psums=[("pT", [P, 1, 2 * G, P], BF16), ("pD", [P, G, P], F32), ("pH", [P, 2, BANK], F32),
                                    ("pW", [P, 2, G, P], F32), ("pX", [P, 2, G, P], F32)],
               sbufs=[("rec", [P, 2, G, A50], F32), ("oh", [P, 2, G, P], BF16), ("ohT", [P, 2, G, P], F32),
                      ("dT", [A50, 2, G, P], F32), ("prod", [P, 2, G, P], F32), ("idx", [P, 2, G], I32)],
               sems=["hot", "turned", "ohT_ok", "rec_turned", "dT_ok", "h_done", "y_ok", "n_ok", "e_ok", "l_ok", "s_ok",
                     "w_done", "picked", "w_ok", "prod_ok", "idx_ok"], pairs=["ld", "sent"])

def store(kn):
    def build(r):
        def sync(e, ch):
            full = (N // P) * P
            e.dma_start(kn.out[0:full, :].rearrange("(b p) h -> p b h", p=P), kn.X[:, 0:N // P, :]).then_inc(r["st"], 16)
            e.dma_start(kn.out[full:N, :], kn.X[0:N - full, N // P, :]).then_inc(r["st"], 16)
            e.wait_ge(r["st"], 32)
        return dict(sync=sync)
    phase(kn, "store", build, sems=["st"])


def layout(inp):
    import numpy as np
    f = {k: np.asarray(v) for k, v in inp.items()}
    a = {}
    a["x"] = f["x"]
    rec = np.zeros((EP, NREC), np.float32)
    rec[:E, 0:A50] = f["edge_attr_50"]
    rec[:E, C64:C64 + A64] = f["edge_attr_64"]
    rec[:E, CM:CM + A3] = f["edge_attr_3"]
    rec[:E, CM + A3] = f["edge_weight"]
    a["rec"] = rec
    for n in ("src", "dst"):
        lin = np.full((EP,), PAD_KEY, np.int32)
        lin[:E] = f[n]
        a[n + "_lin"] = lin
        a[n + "_tiles"] = np.ascontiguousarray(lin.reshape(T, P).T)
    t = lambda n: f[n].T
    m = {"W_lin": f["L0_gnn_W_lin"], "Wi": t("L1_gnn_Wi"), "Wj": t("L1_gnn_Wj"), "Wd": t("L1_gnn_Wd"),
         "msg_top": f["L2_gnn_msg_w"][:H], "msg_bottom": f["L2_gnn_msg_w"][H:], "upd_top": f["L2_gnn_upd_w"][:H],
         "upd_bottom": f["L2_gnn_upd_w"][H:], "lin1": t("L3_gnn_lin1_w"), "lin2": t("L3_gnn_lin2_w"),
         "mlp_w2": t("L3_gnn_mlp_w2"), "mlp_w1": t("L3_gnn_mlp_w1"), "Wdesc": t("L1_gnn_Wdesc")}
    v = {"bi": f["L1_gnn_bi"], "bd": f["L1_gnn_bd"], "u": f["L1_gnn_u"], "mlp_b1": f["L3_gnn_mlp_b1"],
         "lin2_b": f["L3_gnn_lin2_b"]}
    for k, n in (("ri1", 3), ("ri2", 3), ("ra1", 2), ("ra2", 2)):
        for i in range(n):
            m[f"W{k}_{i}"] = f["L1_gnn_W" + k][i].T
            v[f"b{k}_{i}"] = f["L1_gnn_b" + k][i]
    att = f["L0_gnn_W_att"]
    m["W_att"] = np.concatenate([att[:H], att[H:]], axis=1)
    a["mats"] = np.zeros((P, len(MATS), H), np.float32)
    for i, n in enumerate(MATS):
        a["mats"][:m[n].shape[0], i, :m[n].shape[1]] = m[n]
    a["vecs"] = np.ascontiguousarray(np.stack([v[n] for n in VECS], axis=1))
    w = {"b_lin": f["L0_gnn_b_lin"], "bj": f["L1_gnn_bj"], "mlp_b2": f["L3_gnn_mlp_b2"], "b_att": f["L0_gnn_b_att"],
         "gate_w": f["L2_gnn_gate_w"][:, 0], "gate_b": f["L2_gnn_gate_b"]}
    for n in ("msg_b", "msg_g", "msg_beta", "upd_b", "upd_g", "upd_beta"):
        w[n] = f["L2_gnn_" + n]
    a["rows"] = np.zeros((1, len(ROWS) * H), np.float32)
    for i, n in enumerate(ROWS):
        a["rows"][0, i * H:i * H + w[n].size] = w[n]
    return a


def build_program(nc, ins, out):
    kn = Buffers()
    kn.nc, kn.ins, kn.out = nc, ins, out
    kn.tally = nc.alloc_semaphore("tally")
    kn.slot_regs = {n: [e.alloc_register(f"slot{j}") for j in range(G)]
                    for n, e in (("vector", nc.vector), ("tensor", nc.tensor), ("scalar", nc.scalar), ("sync", nc.sync))}
    with ExitStack() as ctx:
        setup(kn, ctx)
        constants(kn)
        with ExitStack() as keys_ctx:
            kn.keys_ctx = keys_ctx
            split_keys(kn)
            histogram(kn)
            offsets(kn)
            sort(kn)
        node_buffers(kn, ctx)
        slot_columns(kn)
        with ExitStack() as l0:
            kn.sij = l0.enter_context(nc.sbuf_tensor("sij", [P, NB * 2 * HEADS], F32))
            layernorm(kn, "ln0")
            l0_nodes(kn)
            l0_scores(kn)
            l0_segments(kn)
            l0_table(kn)
            l0_edges(kn)
        l0_close(kn)
        kn.products = dram(kn, "products", (EP, H))
        layernorm(kn, "ln1")
        turn_nodes(kn)
        l1_nodes_i(kn)
        l1_nodes_j(kn)
        l1_edges(kn)
        sum_by_src(kn, "l1r")
        l1_layers(kn)
        add_turned(kn, "l1c", kn.Hn)
        layernorm(kn, "ln2")
        kn.l2_rows = dram(kn, "l2_rows", (NP, H))
        tables(kn, "l2t", "msg_bottom", "msg_top", "msg_b", kn.l2_rows)
        l2_edges(kn)
        l2_update(kn)
        layernorm(kn, "ln2b", kn.TB, kn.MT, ACT.Identity)
        l2_close(kn)
        layernorm(kn, "ln3")
        tables(kn, "l3t", "lin1")
        l3_edges(kn)
        sum_by_src(kn, "l3r", clear=True)
        linear_ssp(kn, "l3o", kn.MT, kn.AC, "lin2", "lin2_b")
        add_turned(kn, "l3c", kn.MT, kn.Hn)
        store(kn)


_ORDER = ["x", "rec", "src_lin", "dst_lin", "src_tiles", "dst_tiles", "mats", "vecs", "rows"]


def kernel(**inputs):
    import numpy as _np
    import concourse.bacc as _bacc
    from concourse import mybir as _mybir
    from concourse.bass_utils import run_bass_kernel_spmd as _run

    nc = _bacc.Bacc("TRN2", target_bir_lowering=False, num_devices=1)
    arrays = layout(inputs)
    args = {n: nc.dram_tensor(n, arrays[n].shape, _mybir.dt.from_np(arrays[n].dtype), kind="ExternalInput").ap()
            for n in _ORDER}
    out = nc.dram_tensor("out", (N, H), F32, kind="ExternalOutput").ap()
    build_program(nc, args, out)
    r = _run(nc, [arrays], core_ids=[0])
    return r.results[0]["out"]
```
